# Optimizing a Trainium2 kernel written in Bass

```python
import numpy as np
import jax
import jax.numpy as jnp

def _softmax(x, axis=-1):
    return jax.nn.softmax(x, axis=axis)

def _gelu(x):
    return jax.nn.gelu(x, approximate=True)

def _silu(x):
    return jax.nn.silu(x)

def _sigmoid(x):
    return jax.nn.sigmoid(x)

def _layernorm(x, axis=-1, eps=1e-05):
    m = jnp.mean(x, axis=axis, keepdims=True)
    v = jnp.var(x, axis=axis, keepdims=True)
    return (x - m) / jnp.sqrt(v + eps)

def _scatter_add(tgt, idx, src, axis=0):
    return tgt.at[idx].add(src)

def _segment_sum(src, seg, n):
    return jax.ops.segment_sum(src, seg, n)
kernel_name = 'mk_gnn_ffn_d2_gnn_r64_708143'

def setup_inputs(seed: int=0):
    np.random.seed(seed)
    _w = jnp.asarray

    def _rec_inputs():
        import jax
        import jax.numpy as jnp
        _gk = jax.random.key(seed)
        x = -8.776e-05 + 1 * jax.random.normal(jax.random.fold_in(_gk, 1), (10000, 512), jnp.float32)
        _s = jax.random.randint(jax.random.fold_in(_gk, 2), (2500,), 0, 10000, jnp.int32)
        _d = jax.random.randint(jax.random.fold_in(_gk, 3), (2500,), 0, 10000, jnp.int32)
        _loop = jnp.arange(10000, dtype=jnp.int32)
        src = jnp.concatenate([_s, _d, _loop])
        dst = jnp.concatenate([_d, _s, _loop])
        _o = jnp.argsort(dst, stable=True)
        src = src[_o]
        dst = dst[_o]
        return (x, src, dst)
    x, src, dst = _rec_inputs()

    def _L0_gnn_setup():
        import jax, jax.numpy as jnp
        import numpy as np
        N, E, D, H = (10000, 2500, 512, 8)
        C = D // H
        key = jax.random.key(seed)
        ks = jax.random.split(key, 5)
        x = jax.random.normal(ks[0], (N, D), dtype=jnp.float32)
        edge_index = jax.random.randint(ks[1], (2, E), 0, N, dtype=jnp.int64 if jax.config.jax_enable_x64 else jnp.int32)
        scale = 1.0 / np.sqrt(D).astype(np.float32)
        W_l = jax.random.normal(ks[2], (D, D), dtype=jnp.float32) * scale
        W_r = jax.random.normal(ks[3], (D, D), dtype=jnp.float32) * scale
        att = jax.random.normal(ks[4], (H, C), dtype=jnp.float32) * np.float32(1.0 / np.sqrt(C))
        bias = jnp.zeros((D,), dtype=jnp.float32)
        return {'x': x, 'edge_index': edge_index, 'W_l': W_l, 'W_r': W_r, 'att': att, 'bias': bias}
    _L0_gnn_all = _L0_gnn_setup()
    _L0_gnn_in = {k: v for k, v in _L0_gnn_all.items() if k in ('W_l', 'W_r', 'att', 'bias')}
    del _L0_gnn_all

    def _L0_ffn_setup():
        import jax, jax.numpy as jnp
        import numpy as np
        B, S, D = (8, 64, 512)
        H = 32
        O = 512
        E = 8
        TOP_K = 1
        key = jax.random.key(seed)
        ks = jax.random.split(key, 8)
        sc = 0.02
        return {'x': jax.random.normal(ks[0], (B, S, D), dtype=jnp.float32), 'Wr': jax.random.normal(ks[1], (D, E), dtype=jnp.float32) * sc, 'br': jnp.zeros((E,), dtype=jnp.float32), 'W1': jax.random.normal(ks[2], (E, D, H), dtype=jnp.float32) * sc, 'b1': jnp.zeros((E, H), dtype=jnp.float32), 'W2': jax.random.normal(ks[3], (E, H, O), dtype=jnp.float32) * sc, 'b2': jnp.zeros((E, O), dtype=jnp.float32)}
    _L0_ffn_all = _L0_ffn_setup()
    _L0_ffn_in = {k: v for k, v in _L0_ffn_all.items() if k in ('Wr', 'br', 'W1', 'b1', 'W2', 'b2')}
    del _L0_ffn_all

    def _L1_gnn_setup():
        import jax, jax.numpy as jnp
        import numpy as np
        N_NODES = 50000
        N_EDGES = 6250
        IN_DIM = 512
        OUT_DIM = 512
        key = jax.random.key(seed)
        k1, k2, k3, k4 = jax.random.split(key, 4)
        x = jax.random.normal(k1, (N_NODES, IN_DIM), dtype=jnp.float32)
        edge_index = jax.random.randint(k2, (2, N_EDGES), 0, N_NODES, dtype=jnp.int64)
        W = jax.random.normal(k3, (OUT_DIM, IN_DIM), dtype=jnp.float32) / np.sqrt(IN_DIM)
        b = jax.random.normal(k4, (OUT_DIM,), dtype=jnp.float32) * 0.01
        return {'x': x, 'edge_index': edge_index, 'W': W, 'b': b}
    _L1_gnn_all = _L1_gnn_setup()
    _L1_gnn_in = {k: v for k, v in _L1_gnn_all.items() if k in ('W', 'b')}
    del _L1_gnn_all

    def _L1_ffn_setup():
        import jax, jax.numpy as jnp
        import numpy as np
        K_ACTIVE = 2
        CAP_FACTOR = 4

        def _route(x, hash_proj, k):
            logits = jnp.einsum('td,hde->hte', x, hash_proj)
            cand = jnp.argmax(logits, axis=-1)
            scores = jnp.take_along_axis(logits, cand[..., None], axis=-1)[..., 0]
            cand_t = cand.T
            scores_t = scores.T
            top_s, top_i = jax.lax.top_k(scores_t, k)
            sel = jnp.take_along_axis(cand_t, top_i, axis=1)
            return sel

        def _moe(x, sel, W1, W2):
            T, d = x.shape
            E = W1.shape[0]
            k = sel.shape[1]
            C = CAP_FACTOR * T * k // E
            se = sel.reshape(-1)
            oh = jax.nn.one_hot(se, E, dtype=jnp.int32)
            pos = jnp.take_along_axis(jnp.cumsum(oh, axis=0) - 1, se[:, None], axis=1)[:, 0]
            keep = pos < C
            posc = jnp.where(keep, pos, 0)
            xr = jnp.repeat(x, k, axis=0)
            xr = jnp.where(keep[:, None], xr, 0.0)
            buf = jnp.zeros((E, C, d), x.dtype).at[se, posc].add(xr)
            h = jax.nn.gelu(jnp.einsum('ecd,edf->ecf', buf, W1), approximate=False)
            y = jnp.einsum('ecf,efd->ecd', h, W2)
            out = y[se, posc] * keep[:, None].astype(x.dtype)
            return out.reshape(T, k, d)
        key = jax.random.key(seed)
        k1, k2, k3, k4 = jax.random.split(key, 4)
        B, S, D, F, E, H = (4, 32, 512, 32, 64, 4)
        hidden_states = jax.random.normal(k1, (B, S, D), dtype=jnp.float32)
        hash_proj = jax.random.normal(k2, (H, D, E), dtype=jnp.float32)
        W1 = jax.random.normal(k3, (E, D, F), dtype=jnp.float32) * (1.0 / np.sqrt(D))
        W2 = jax.random.normal(k4, (E, F, D), dtype=jnp.float32) * (1.0 / np.sqrt(F))
        return {'hidden_states': hidden_states, 'hash_proj': hash_proj, 'W1': W1, 'W2': W2}
    _L1_ffn_all = _L1_ffn_setup()
    _L1_ffn_in = {k: v for k, v in _L1_ffn_all.items() if k in ('hash_proj', 'W1', 'W2')}
    del _L1_ffn_all
    return {'x': x, 'src': src, 'dst': dst, 'L0_gnn_W_l': _L0_gnn_in['W_l'], 'L0_gnn_W_r': _L0_gnn_in['W_r'], 'L0_gnn_att': _L0_gnn_in['att'], 'L0_gnn_bias': _L0_gnn_in['bias'], 'L0_ffn_Wr': _L0_ffn_in['Wr'], 'L0_ffn_br': _L0_ffn_in['br'], 'L0_ffn_W1': _L0_ffn_in['W1'], 'L0_ffn_b1': _L0_ffn_in['b1'], 'L0_ffn_W2': _L0_ffn_in['W2'], 'L0_ffn_b2': _L0_ffn_in['b2'], 'L1_gnn_W': _L1_gnn_in['W'], 'L1_gnn_b': _L1_gnn_in['b'], 'L1_ffn_hash_proj': _L1_ffn_in['hash_proj'], 'L1_ffn_W1': _L1_ffn_in['W1'], 'L1_ffn_W2': _L1_ffn_in['W2']}

def reference(x, src, dst, L0_gnn_W_l, L0_gnn_W_r, L0_gnn_att, L0_gnn_bias, L0_ffn_Wr, L0_ffn_br, L0_ffn_W1, L0_ffn_b1, L0_ffn_W2, L0_ffn_b2, L1_gnn_W, L1_gnn_b, L1_ffn_hash_proj, L1_ffn_W1, L1_ffn_W2):
    import jax
    import jax.numpy as jnp

    def _L0_gnn_ref(x, edge_index, W_l, W_r, att, bias):
        import jax, jax.numpy as jnp
        import numpy as np
        N, E, D, H = (10000, 2500, 512, 8)
        C = D // H
        n = x.shape[0]
        self_idx = jnp.arange(n, dtype=edge_index.dtype)
        src = jnp.concatenate([edge_index[0], self_idx])
        dst = jnp.concatenate([edge_index[1], self_idx])
        x_l = (x @ W_l).reshape(n, H, C)
        x_r = (x @ W_r).reshape(n, H, C)
        m = jax.nn.leaky_relu(x_l[src] + x_r[dst], negative_slope=0.2)
        alpha = jnp.einsum('ehc,hc->eh', m, att)
        amax = jax.lax.stop_gradient(jax.ops.segment_max(alpha, dst, num_segments=n))
        ea = jnp.exp(alpha - amax[dst])
        denom = jax.ops.segment_sum(ea, dst, num_segments=n)
        w = ea / jnp.maximum(denom[dst], 1e-16)
        out = jax.ops.segment_sum(w[:, :, None] * x_l[src], dst, num_segments=n)
        out = out.reshape(n, H * C) + bias
        return jax.nn.elu(out) + x

    def _L0_ffn_ref(x, Wr, br, W1, b1, W2, b2):
        import jax, jax.numpy as jnp
        import numpy as np
        B, S, D = (8, 64, 512)
        H = 32
        O = 512
        E = 8
        TOP_K = 1
        b, s, d = x.shape
        xf = x.reshape(-1, d)
        router_logits = xf @ Wr + br
        topk_logits, topk_idx = jax.lax.top_k(router_logits, TOP_K)
        topk_gates = jax.nn.softmax(topk_logits, axis=1)
        out = jnp.zeros((xf.shape[0], O), dtype=x.dtype)
        for k in range(TOP_K):
            idx_k = topk_idx[:, k]
            gate_k = topk_gates[:, k:k + 1]
            for e in range(E):
                h = jax.nn.relu(xf @ W1[e] + b1[e])
                oe = h @ W2[e] + b2[e]
                mask = (idx_k == e)[:, None]
                out = out + jnp.where(mask, gate_k * oe, 0.0)
        return out.reshape(b, s, O)

    def _L1_gnn_ref(x, edge_index, W, b):
        import jax, jax.numpy as jnp
        import numpy as np
        N_NODES = 50000
        N_EDGES = 6250
        IN_DIM = 512
        OUT_DIM = 512
        n = x.shape[0]
        loops = jnp.arange(n, dtype=edge_index.dtype)
        row = jnp.concatenate([edge_index[0], loops])
        col = jnp.concatenate([edge_index[1], loops])
        deg = jax.ops.segment_sum(jnp.ones(row.shape[0], dtype=x.dtype), row, num_segments=n)
        dis = jax.lax.rsqrt(deg)
        norm = dis[row] * dis[col]
        h = x @ W.T + b
        out = jax.ops.segment_sum(norm[:, None] * h[row], col, num_segments=n)
        return jax.nn.relu(out)

    def _L1_ffn_ref(hidden_states, hash_proj, W1, W2):
        import jax, jax.numpy as jnp
        import numpy as np
        K_ACTIVE = 2
        CAP_FACTOR = 4

        def _route(x, hash_proj, k):
            logits = jnp.einsum('td,hde->hte', x, hash_proj)
            cand = jnp.argmax(logits, axis=-1)
            scores = jnp.take_along_axis(logits, cand[..., None], axis=-1)[..., 0]
            cand_t = cand.T
            scores_t = scores.T
            top_s, top_i = jax.lax.top_k(scores_t, k)
            sel = jnp.take_along_axis(cand_t, top_i, axis=1)
            return sel

        def _moe(x, sel, W1, W2):
            T, d = x.shape
            E = W1.shape[0]
            k = sel.shape[1]
            C = CAP_FACTOR * T * k // E
            se = sel.reshape(-1)
            oh = jax.nn.one_hot(se, E, dtype=jnp.int32)
            pos = jnp.take_along_axis(jnp.cumsum(oh, axis=0) - 1, se[:, None], axis=1)[:, 0]
            keep = pos < C
            posc = jnp.where(keep, pos, 0)
            xr = jnp.repeat(x, k, axis=0)
            xr = jnp.where(keep[:, None], xr, 0.0)
            buf = jnp.zeros((E, C, d), x.dtype).at[se, posc].add(xr)
            h = jax.nn.gelu(jnp.einsum('ecd,edf->ecf', buf, W1), approximate=False)
            y = jnp.einsum('ecf,efd->ecd', h, W2)
            out = y[se, posc] * keep[:, None].astype(x.dtype)
            return out.reshape(T, k, d)
        B, S, D = hidden_states.shape
        x = hidden_states.reshape(B * S, D)
        sel = _route(x, hash_proj, K_ACTIVE)
        expert_outputs = _moe(x, sel, W1, W2)
        out = expert_outputs.mean(axis=1)
        return out.reshape(B, S, D)
    edge_index = jnp.stack([src, dst])
    x = x + _L0_gnn_ref(_layernorm(x, axis=-1), edge_index, L0_gnn_W_l, L0_gnn_W_r, L0_gnn_att, L0_gnn_bias)
    x = x + _L0_ffn_ref(_layernorm(x, axis=-1)[None], L0_ffn_Wr, L0_ffn_br, L0_ffn_W1, L0_ffn_b1, L0_ffn_W2, L0_ffn_b2)[0]
    x = x + _L1_gnn_ref(_layernorm(x, axis=-1), edge_index, L1_gnn_W, L1_gnn_b)
    x = x + _L1_ffn_ref(_layernorm(x, axis=-1)[None], L1_ffn_hash_proj, L1_ffn_W1, L1_ffn_W2)[0]
    return x

_drawn_inputs = setup_inputs


def setup_inputs(seed=0):
    import zlib

    import numpy as np

    out = dict(_drawn_inputs(seed))
    spreads = {'L0_gnn_bias': (0.0, 0.1),
     'L0_ffn_br': (0.0, 0.1),
     'L0_ffn_b1': (0.0, 0.382),
     'L0_ffn_b2': (0.0, 0.1)}
    factors = {'L1_gnn_b': 3.787}
    for name, (base, spread) in spreads.items():
        noise = np.random.default_rng([zlib.crc32(name.encode()), seed]).standard_normal(out[name].shape)
        drawn = base * np.exp(spread * noise) if base else spread * noise
        out[name] = jnp.asarray(drawn.astype(out[name].dtype))
    for name, factor in factors.items():
        out[name] = (out[name] * factor).astype(out[name].dtype)
    return out
```

```python
import numpy as np
from contextlib import ExitStack

import concourse.bass as bass
from concourse import mybir
from concourse.alu_op_type import AluOpType as ALU

ACT = mybir.ActivationFunctionType
F32 = mybir.dt.float32
BF16 = mybir.dt.bfloat16
I32 = mybir.dt.int32
U32 = mybir.dt.uint32
AX = mybir.AxisListType

P = 128
N, D = 10000, 512
E = 15000
H, C = 8, 64
DK = D // P
NT = -(-N // P)
NP = NT * P
TAIL = N - (NT - 1) * P
CE = C + 1
XE = H * CE
AW = XE + H
W = P - 1
ET = -(-E // W)
EP, EC = 120, E // 120
FL = EP * P
NE, FH = 8, 32
FC = NE * FH
ME, MH, MF = 64, 4, 32
MC = ME * MF
CAP = 4 * N * 2 // ME
SKIP = 20000.0
BIG = 1.0e30
EPS = 1e-5
SLOPE = 0.2


def stream(eng, n, ring, body, peel=1):
    for g in range(peel):
        for s in range(ring):
            body(g, s)
    with eng.Fori(peel, n // ring) as g:
        for s in range(ring):
            body(g, s)
    for s in range(n % ring):
        body(n // ring, s)


def warm(g, s, lag, ring):
    return not isinstance(g, int) or g * ring + s >= lag


def gnn_ffn(nc, x, src, dst, Wl, Wr, att, gbias, Wc0, b1c, W2e, b2e, WT, bG, hashp, M1, M2, out):
    ctx = ExitStack()
    with ctx:
        def sb(name, shape, dt=F32, on=None):
            return (on or ctx).enter_context(nc.sbuf_tensor(name, shape, dt))

        phase = []

        def sem(name):
            phase.append(nc.alloc_semaphore(name=name))
            return phase[-1]

        def end_phase(buffers):
            buffers.close()
            nc.clear_and_free_semaphores(phase)
            phase.clear()
            nc.all_engine_barrier()

        def sems(name, n):
            return [sem(f"{name}{i}") for i in range(n)]

        psum = ctx.enter_context(nc.psum_tensor("psum", [P, 8, 512], F32))
        bank = [psum[:, i, :] for i in range(8)]
        pair = [psum[:, 4 + 2 * i:6 + 2 * i, 0:XE // 2] for i in range(2)]

        XLE = nc.dram_tensor("xl_ext", [NP, XE], F32).ap()
        XR = nc.dram_tensor("xr_rows", [NP, D], F32).ap()
        AGG = nc.dram_tensor("edge_sums0", [NP, AW], F32).ap()
        X2 = nc.dram_tensor("x2_rows", [NP, D], F32).ap()
        GR = nc.dram_tensor("gcn_rows", [NP, D], F32).ap()
        AG2 = nc.dram_tensor("edge_sums1", [NP, D], F32).ap()
        FD = nc.dram_tensor("flat_dst", [FL], F32).ap()
        FS = nc.dram_tensor("flat_src", [FL], F32).ap()
        MDR = nc.dram_tensor("window_dst", [ET, P], F32).ap()
        RRR = nc.dram_tensor("window_resets", [ET, 2 * P], F32).ap()

        ident = sb("ident", [P, P])
        identb = sb("identb", [P, P], BF16)
        tri = sb("tri", [P, P], BF16)
        onesb = sb("onesb", [P, P], BF16)
        iota = sb("iota", [P, P])
        mhalf = sb("mhalf", [P, NT])
        epst = sb("epst", [P, 1])
        minus1 = sb("minus1", [P, 1])
        one = sb("one", [P, 1])
        att_b = sb("att_b", [P, D])
        gb_b = sb("gb_b", [P, D])
        wl = sb("wl", [P, DK, D])
        wr = sb("wr", [P, DK, D])
        wc = sb("wc", [P, DK, FC + NE])
        w2 = sb("w2", [P, FC // P, D])
        b1b = sb("b1b", [P, FC + NE])
        b2 = sb("b2", [NE, D])
        wg = sb("wg", [P, DK, D])
        bgb = sb("bgb", [P, D])
        hp = sb("hp", [P, DK, MH * ME])
        selfa = sb("selfa", [P, NT, H])
        xsc = sb("xsc", [P, NT, 2])
        dis = sb("dis", [P, NT])
        kd = sb("kd", [P, ET])
        idx = sb("idx", [P, 3, ET], I32)

        slot = sb("slot", [P, 4, 3], I32)
        held = sb("held", [P, 2, 4])

        def hold(pool, site, s, done, t):
            if not isinstance(t, int) or t >= 4:
                pool.wait_ge(done, t - 3)
            pool.tensor_tensor(held[:, site, s:s + 1], mhalf[:, 0:1], mhalf[:, 1:2], ALU.add).then_inc(done, 1)

        consts = sem("consts")
        loaded = sem("loaded")
        c_flat, c_int, c_f32, c_win, c_cmp, c_rows, c_tr, c_idx = (
            sem(n) for n in ("c_flat", "c_int", "c_f32", "c_win", "c_cmp", "c_rows", "c_tr", "c_idx"))
        h_oh, h_mm, h_deg, h_dis, h_init = (sem(n) for n in ("h_oh", "h_mm", "h_deg", "h_dis", "h_init"))

        prep = ExitStack()
        ei = sb("ei", [EP, 2, EC], I32, prep)
        ef = sb("ef", [EP, 2, EC], F32, prep)
        eh = sb("eh", [EP, 2, EC], I32, prep)
        ehf = sb("ehf", [EP, 2, EC], F32, prep)
        ohl = sb("ohl", [EP, 2, P], BF16, prep)
        ohh = sb("ohh", [EP, 2, NT], BF16, prep)
        padt = sb("padt", [EP, P], F32, prep)
        win = sb("win", [ET, 2, P + 2], F32, prep)
        ne = sb("ne", [ET, P], F32, prep)
        rr = sb("rr", [ET, 2, P], F32, prep)
        mdw = sb("mdw", [ET, P], F32, prep)
        wcol = sb("wcol", [ET, 3, P], F32, prep)
        deg1 = sb("deg1", [P, NT], F32, prep)
        zin = sb("zin", [P, AW], F32, prep)

        with nc.Block() as block:
            @block.sync
            def _(sp):
                sp.dma_start(ei[:, 0, :], dst.rearrange("(p c) -> p c", c=EC)).then_inc(c_int, 16)
                sp.dma_start(ei[:, 1, :], src.rearrange("(p c) -> p c", c=EC)).then_inc(c_int, 16)
                sp.wait_ge(consts, 6)
                sp.dma_start(FD.rearrange("(p c) -> p c", c=P), padt[:]).then_inc(c_flat, 16)
                sp.dma_start(FS.rearrange("(p c) -> p c", c=P), padt[:]).then_inc(c_flat, 16)
                sp.wait_ge(c_flat, 32)
                sp.wait_ge(c_f32, 1)
                sp.dma_start(FD[1:1 + E].rearrange("(p c) -> p c", c=EC), ef[:, 0, :]).then_inc(c_flat, 16)
                sp.dma_start(FS[1:1 + E].rearrange("(p c) -> p c", c=EC), ef[:, 1, :]).then_inc(c_flat, 16)
                sp.wait_ge(c_flat, 64)
                for k, f in enumerate((FD, FS)):
                    v = bass.AP(f.tensor, 0, [[W, ET], [1, P + 1]])
                    sp.dma_start(win[:, k, 0:P + 1], v).then_inc(c_win, 16)
                for t, s in ((wl, Wl), (wr, Wr), (wc, Wc0), (wg, WT), (hp, hashp), (w2, W2e)):
                    sp.dma_start(t[:], s.rearrange("(k p) n -> p k n", p=P)).then_inc(loaded, 16)
                for t, s in ((att_b, att), (gb_b, gbias), (b1b, b1c), (bgb, bG)):
                    sp.dma_start(t[:], s.partition_broadcast(P)).then_inc(loaded, 16)
                sp.dma_start(b2[:], b2e).then_inc(loaded, 16)
                sp.dma_start(AGG.rearrange("(t p) c -> p t c", p=P),
                             zin[:].unsqueeze(1).to_broadcast([P, NT, AW])).then_inc(h_init, 16)
                sp.dma_start(AG2.rearrange("(t p) c -> p t c", p=P),
                             zin[:, 0:D].unsqueeze(1).to_broadcast([P, NT, D])).then_inc(h_init, 16)
                sp.wait_ge(c_rows, 1)
                sp.dma_start(MDR, mdw[:]).then_inc(h_init, 16)
                sp.dma_start(RRR, rr[:].rearrange("t a p -> t (a p)")).then_inc(h_init, 16)
                sp.wait_ge(loaded, 11 * 16)
                sp.wait_ge(h_init, 4 * 16)

            @block.gpsimd
            def _(pool):
                pool.memset(padt[:], SKIP).then_inc(consts, 1)
                pool.memset(zin[:, 0:XE], 0.0).then_inc(consts, 1)
                pool.memset(zin[:, XE:AW], -BIG).then_inc(consts, 1)
                pool.memset(mhalf[:], -0.5)
                pool.memset(epst[:], EPS)
                pool.memset(one[:], 1.0)
                pool.memset(minus1[:], -1.0).then_inc(consts, 1)
                pool.memset(onesb[:], 1.0).then_inc(consts, 1)
                pool.iota(iota[:], [[1, P]], base=0, channel_multiplier=0,
                          allow_small_or_imprecise_dtypes=True).then_inc(consts, 1)
                pool.memset(ident[:], 0.0).then_inc(consts, 1)
                pool.memset(identb[:], 0.0).then_inc(consts, 1)
                pool.memset(tri[:], 1.0).then_inc(consts, 1)
                pool.wait_ge(consts, 9)
                for m in (ident, identb):
                    pool.affine_select(out=m[:], in_=m[:], compare_op=ALU.not_equal, fill=1.0, base=0,
                                       pattern=[[-1, P]], channel_multiplier=1).then_inc(consts, 1)
                pool.affine_select(out=tri[:], in_=tri[:], compare_op=ALU.is_gt, fill=0.0, base=0,
                                   pattern=[[1, P]], channel_multiplier=-1).then_inc(consts, 1)
                pool.wait_ge(h_deg, 1)
                pool.wait_ge(consts, 12)
                pool.tensor_tensor(dis[:], deg1[:], mhalf[:], ALU.pow).then_inc(h_dis, 1)
                pool.wait_ge(h_dis, 1)

            @block.vector
            def _(dve):
                dve.wait_ge(c_int, 32)
                nc.vector.tensor_copy(ef[:], ei[:]).then_inc(c_f32, 1)
                nc.vector.tensor_scalar(eh[:, 0, :], ei[:, 1, :], P - 1, None, ALU.bitwise_and).then_inc(c_f32, 1)
                nc.vector.tensor_scalar(eh[:, 1, :], ei[:, 1, :], 7, None,
                                        ALU.logical_shift_right).then_inc(c_f32, 1)
                dve.wait_ge(c_f32, 3)
                nc.vector.tensor_copy(ehf[:], eh[:]).then_inc(c_f32, 1)
                dve.wait_ge(c_f32, 4)
                dve.wait_ge(consts, 12)

                def onehots(g, s):
                    t = g * 2 + s
                    if warm(g, s, 2, 2):
                        dve.wait_ge(h_mm, t - 1)
                    nc.vector.tensor_scalar(ohl[:, s, :], iota[0:EP, :], ehf[:, 0, bass.ds(t, 1)], None,
                                            ALU.is_equal)
                    nc.vector.tensor_scalar(ohh[:, s, :], iota[0:EP, 0:NT], ehf[:, 1, bass.ds(t, 1)], None,
                                            ALU.is_equal).then_inc(h_oh, 1)

                stream(dve, EC, 2, onehots)
                dve.wait_ge(h_mm, EC)
                nc.vector.tensor_scalar_add(deg1[:], bank[0][:, 0:NT], 1.0).then_inc(h_deg, 1)

                dve.wait_ge(c_win, 32)
                nc.vector.memset(win[0:1, 0, 0:1], -1.0).then_inc(c_cmp, 1)
                nc.vector.memset(rr[:], -BIG).then_inc(c_cmp, 1)
                nc.vector.memset(wcol[:], SKIP).then_inc(c_cmp, 1)
                dve.wait_ge(c_cmp, 3)
                nc.vector.tensor_tensor(ne[:], win[:, 0, 1:P + 1], win[:, 0, 0:P], ALU.not_equal).then_inc(c_cmp, 1)
                dve.wait_ge(c_cmp, 4)
                nc.vector.tensor_scalar_mul(rr[:, 0, 1:P], ne[:, 0:P - 1], -BIG).then_inc(c_cmp, 1)
                nc.vector.tensor_scalar_mul(rr[:, 1, 0:P - 1], ne[:, 0:P - 1], -BIG).then_inc(c_cmp, 1)
                nc.vector.tensor_copy(mdw[:, 0:1], win[:, 0, W:P]).then_inc(c_cmp, 1)
                nc.vector.tensor_copy(mdw[:, 1:P], win[:, 0, 1:P]).then_inc(c_cmp, 1)
                nc.vector.tensor_copy(wcol[:, 0, 1:P], win[:, 1, 1:P]).then_inc(c_cmp, 1)
                nc.vector.tensor_copy(wcol[:, 1, 1:P], win[:, 0, 1:P]).then_inc(c_cmp, 1)
                nc.vector.scalar_tensor_tensor(wcol[:, 2, 1:P], win[:, 0, 1:P], -SKIP, ne[:, 1:P],
                                               ALU.add, ALU.mult).then_inc(c_cmp, 1)
                dve.wait_ge(c_cmp, 11)
                nc.vector.tensor_scalar_add(wcol[:, 2, 1:P], wcol[:, 2, 1:P], SKIP).then_inc(c_rows, 1)
                dve.wait_ge(c_tr, 1)
                nc.vector.tensor_copy(kd[:], bank[1][:, 0:ET]).then_inc(c_idx, 1)
                nc.vector.tensor_copy(idx[:], bank[2][:, 0:3 * ET].rearrange("p (a t) -> p a t", a=3))\
                    .then_inc(c_idx, 1)
                dve.wait_ge(c_idx, 2)

            @block.tensor
            def _(pe):
                def count(g, s):
                    t = g * 2 + s
                    pe.wait_ge(h_oh, t + 1)
                    first = isinstance(g, int) and t == 0
                    last = isinstance(g, int) and t == EC - 1
                    nc.tensor.matmul(bank[0][:, 0:NT], ohl[:, s, :], ohh[:, s, :], start=first, stop=last,
                                     skip_group_check=True).then_inc(h_mm, 1)

                stream(pe, EC, 2, count)
                pe.wait_ge(c_rows, 1)
                nc.tensor.transpose(bank[1][:, 0:ET], win[:, 0, 0:P], ident[0:ET, 0:ET])
                for a in range(3):
                    last = nc.tensor.transpose(bank[2][:, a * ET:(a + 1) * ET], wcol[:, a, :], ident[0:ET, 0:ET])
                last.then_inc(c_tr, 1)
        end_phase(prep)

        def mm4(ps, lhs, rhs):
            for k in range(DK):
                last = nc.tensor.matmul(ps, lhs[:, k, :], rhs[:, k, :], start=(k == 0), stop=(k == DK - 1))
            return last

        def tr4(ps, rows, n=DK):
            for k in range(n):
                last = nc.tensor.transpose(ps[:, k * P:(k + 1) * P], rows[:, k * P:(k + 1) * P], ident[:])
            return last

        pa = ExitStack()
        xa = sb("xa", [P, 2, D], F32, pa)
        st6 = sb("st6", [P, 2, 6], F32, pa)
        mv = sb("mv", [P, 2, 2], F32, pa)
        ve = sb("ve", [P, 2, 1], F32, pa)
        rs = sb("rs", [P, 2, 1], F32, pa)
        nm = sb("nm", [P, 2, 1], F32, pa)
        xn = sb("xn", [P, 2, D], F32, pa)
        xT = sb("xT", [P, 2, DK, P], F32, pa)
        xle = sb("xle", [P, 2, XE], F32, pa)
        xr = sb("xr", [P, 2, D], F32, pa)
        mm = sb("mm", [P, 2, D], F32, pa)
        la = sb("la", [P, 2, D], F32, pa)
        a_ld, a_st, a_sr = sems("a_ld", 2), sems("a_st", 2), sems("a_sr", 2)
        (a_bn, a_mv, a_ve, a_rs, a_nm, a_sc, a_norm, a_tr, a_xT, a_mm, a_xl, a_xr, a_m, a_lr, a_la, a_al, a_one) = (
            sem("a_" + n) for n in ("bn", "mv", "ve", "rs", "nm", "sc", "norm", "tr", "xT", "mm", "xl", "xr", "m",
                                    "lr", "la", "al", "one"))

        def heads(a, w=C):
            return a.rearrange("p (h c) -> p h c", h=H)[:, :, 0:w]

        def row(a, t, n=P):
            return a[bass.ds(t * P, n), :]

        with nc.Block() as block:
            @block.sync
            def _(sp):
                def body(g, s):
                    t = g * 2 + s
                    if warm(g, s, 2, 2):
                        sp.wait_ge(a_norm, t - 1)
                    n = TAIL if isinstance(g, int) and t == NT - 1 else P
                    sp.dma_start(xa[0:n, s, :], row(x, t, n)).then_inc(a_ld[s], 16)

                stream(sp, NT, 2, body)

            @block.gpsimd
            def _(pool):
                def body(g, s):
                    t = g * 2 + s
                    pool.wait_ge(a_mv, t + 1)
                    if warm(g, s, 2, 2):
                        pool.wait_ge(a_norm, t - 1)
                    pool.tensor_tensor(ve[:, s, :], mv[:, s, 1:2], epst[:], ALU.add).then_inc(a_ve, 1)
                    pool.wait_ge(a_ve, t + 1)
                    pool.tensor_tensor(rs[:, s, :], ve[:, s, :], mhalf[:, 0:1], ALU.pow).then_inc(a_rs, 1)
                    pool.wait_ge(a_rs, t + 1)
                    pool.tensor_tensor(nm[:, s, :], mv[:, s, 0:1], rs[:, s, :], ALU.mult).then_inc(a_nm, 1)
                    pool.wait_ge(a_nm, t + 1)
                    pool.tensor_tensor(nm[:, s, :], nm[:, s, :], minus1[:], ALU.mult).then_inc(a_sc, 1)
                    pool.wait_ge(a_sc, 2 * t + 1)
                    pool.tensor_copy(xsc[:, bass.ds(t, 1), 0], nm[:, s, :])
                    pool.tensor_tensor(xsc[:, bass.ds(t, 1), 1], rs[:, s, :], one[:], ALU.add).then_inc(a_sc, 1)
                    if warm(g, s, 1, 2):
                        att_mul(t - 1, 1 - s)

                def att_mul(t, s):
                    pool.wait_ge(a_lr, t + 1)
                    if not isinstance(t, int) or t >= 2:
                        pool.wait_ge(a_al, t - 1)
                    pool.tensor_tensor(la[:, s, :], mm[:, s, :], att_b[:], ALU.mult).then_inc(a_la, 1)

                stream(pool, NT, 2, body)
                att_mul(NT - 1, (NT - 1) % 2)
                pool.wait_ge(a_sc, 2 * NT)

            @block.vector
            def _(dve):
                def stats(g, s):
                    t = g * 2 + s
                    dve.wait_ge(a_ld[s], 16 * (g + 1))
                    nc.vector.bn_stats(st6[:, s, :], xa[:, s, :]).then_inc(a_bn, 1)
                    if warm(g, s, 2, 2):
                        dve.wait_ge(a_nm, t - 1)
                    if warm(g, s, 1, 2):
                        norm(t - 1, 1 - s, t)
                    else:
                        dve.wait_ge(a_bn, t + 1)
                    nc.vector.bn_aggr(mv[:, s, :], st6[:, s, :]).then_inc(a_mv, 1)

                def norm(t, s, stats_of=None):
                    dve.wait_ge(a_rs, t + 1)
                    if stats_of is not None:
                        dve.wait_ge(a_bn, stats_of + 1)
                    if not isinstance(t, int) or t >= 2:
                        dve.wait_ge(a_tr, t - 1)
                    nc.vector.tensor_scalar(xn[:, s, :], xa[:, s, :], mv[:, s, 0:1], rs[:, s, :],
                                            ALU.subtract, ALU.mult).then_inc(a_norm, 1)

                def add(t, s):
                    dve.wait_ge(a_mm, t + 1)
                    if not isinstance(t, int) or t >= 2:
                        dve.wait_ge(a_sr[s], 16 * ((t - s) // 2))
                        dve.wait_ge(a_la, t - 1)
                    nc.vector.tensor_copy(xr[:, s, :], bank[4 + s][:]).then_inc(a_xr, 1)
                    dve.wait_ge(a_xl, t + 1)
                    dve.wait_ge(a_xr, t + 1)
                    nc.vector.tensor_tensor(heads(mm[:, s, :]), heads(xle[:, s, :]), heads(xr[:, s, :]), ALU.add)\
                        .then_inc(a_m, 1)
                    dve.wait_ge(a_m, t + 1)
                    nc.vector.scalar_tensor_tensor(mm[:, s, :], mm[:, s, :], SLOPE, mm[:, s, :],
                                                   ALU.mult, ALU.max).then_inc(a_lr, 1)

                def logit(t, s):
                    dve.wait_ge(a_la, t + 1)
                    nc.vector.tensor_reduce(selfa[:, bass.ds(t, 1), :].rearrange("p t h -> p (t h)"),
                                            heads(la[:, s, :]), AX.X, ALU.add).then_inc(a_al, 1)

                def body(g, s):
                    t = g * 2 + s
                    stats(g, s)
                    if warm(g, s, 2, 2):
                        add(t - 2, s)
                    if isinstance(g, int) and t < 3:
                        return
                    logit(t - 3, 1 - s)

                for s in range(2):
                    body(0, s)
                for s in range(2):
                    body(1, s)
                with dve.Fori(2, NT // 2) as g:
                    for s in range(2):
                        body(g, s)
                body(NT // 2, 0)
                norm(NT - 1, 0)
                add(NT - 2, 1)
                logit(NT - 3, 0)
                add(NT - 1, 0)
                logit(NT - 2, 1)
                logit(NT - 1, 0)
                dve.wait_ge(a_al, NT)

            @block.tensor
            def _(pe):
                def project(t, s):
                    pe.wait_ge(a_xT, t + 1)
                    if not isinstance(t, int) or t >= 2:
                        pe.wait_ge(a_xl, t - 1)
                        pe.wait_ge(a_xr, t - 1)
                    mm4(bank[2 + s][:], xT[:, s, :, :], wl)
                    mm4(bank[4 + s][:], xT[:, s, :, :], wr).then_inc(a_mm, 1)

                def body(g, s):
                    t = g * 2 + s
                    pe.wait_ge(a_norm, t + 1)
                    if warm(g, s, 2, 2):
                        pe.wait_ge(a_xT, t - 1)
                    tr4(bank[s], xn[:, s, :]).then_inc(a_tr, 1)
                    if warm(g, s, 1, 2):
                        project(t - 1, 1 - s)

                stream(pe, NT, 2, body)
                project(NT - 1, (NT - 1) % 2)

            @block.scalar
            def _(act):
                act.activation(heads(xle[:, 0, :], CE)[:, :, C:CE], ident[:, 0:H].unsqueeze(2), ACT.Copy,
                               scale=0.0, bias=1.0).then_inc(a_one, 1)
                act.activation(heads(xle[:, 1, :], CE)[:, :, C:CE], ident[:, 0:H].unsqueeze(2), ACT.Copy,
                               scale=0.0, bias=1.0).then_inc(a_one, 1)

                def evac(t, s):
                    act.wait_ge(a_mm, t + 1)
                    if not isinstance(t, int) or t >= 2:
                        act.wait_ge(a_st[s], 16 * ((t - s) // 2))
                        act.wait_ge(a_m, t - 1)
                    act.activation(heads(xle[:, s, :]), heads(bank[2 + s][:]), ACT.Copy).then_inc(a_xl, 1)
                    act.wait_ge(a_xl, t + 1)
                    act.wait_ge(a_one, 2)
                    act.dma_start(row(XLE, t), xle[:, s, :]).then_inc(a_st[s], 16)
                    act.wait_ge(a_xr, t + 1)
                    act.dma_start(row(XR, t), xr[:, s, :]).then_inc(a_sr[s], 16)

                def body(g, s):
                    t = g * 2 + s
                    act.wait_ge(a_tr, t + 1)
                    if warm(g, s, 2, 2):
                        act.wait_ge(a_mm, t - 1)
                    act.activation(xT[:, s, :, :].rearrange("p k n -> p (k n)"), bank[s][:], ACT.Copy)\
                        .then_inc(a_xT, 1)
                    if warm(g, s, 1, 2):
                        evac(t - 1, 1 - s)

                stream(act, NT, 2, body)
                evac(NT - 1, (NT - 1) % 2)
                for s in range(2):
                    act.wait_ge(a_st[s], 16 * ((NT + 1 - s) // 2))
                    act.wait_ge(a_sr[s], 16 * ((NT + 1 - s) // 2))
        end_phase(pa)

        pb = ExitStack()
        gl = sb("gl", [P, 4, XE], F32, pb)
        gr = sb("gr", [P, 4, D], F32, pb)
        md = sb("md", [P, 4, P], F32, pb)
        rst = sb("rst", [H, 4, 2 * P], F32, pb)
        me = sb("me", [P, 2, D], F32, pb)
        al = sb("al", [P, 2, H], F32, pb)
        aT = sb("aT", [H, 2, P], F32, pb)
        pf = sb("pf", [H, 2, P], F32, pb)
        mx = sb("mx", [P, 2, P], F32, pb)
        dd = sb("dd", [H, 2, P], F32, pb)
        ea = sb("ea", [P, 2, P], F32, pb)
        sm = sb("sm", [P, 2, P], F32, pb)
        vv = sb("vv", [P, 2, XE], F32, pb)
        eo = sb("eo", [P, 4, AW], F32, pb)
        b_gl, b_gr, b_md, b_sc = sems("b_gl", 4), sems("b_gr", 4), sems("b_md", 4), sems("b_sc", 4)
        b_h0, b_h1 = sem("b_h0"), sem("b_h1")
        (b_0, b_ix, b_m, b_lr, b_la, b_al, b_at, b_ac, b_pf, b_mx, b_d, b_e, b_et, b_S, b_v, b_s, b_car, b_out) = (
            sem("b_" + n) for n in ("0", "ix", "m", "lr", "la", "al", "at", "ac", "pf", "mx", "d", "e", "et", "S",
                                    "v", "s", "car", "out"))

        def ago(g, s, lag):
            return g + (s - lag) // 4, (s - lag) % 4, g * 4 + s - lag

        with nc.Block() as block:
            @block.sync
            def _(sp):
                def body(g, s):
                    t = g * 4 + s
                    if warm(g, s, 4, 4):
                        sp.wait_ge(b_v, t - 3)
                    sp.dma_start(md[:, s, :], MDR[bass.ds(t, 1), :].to_broadcast([P, P])).then_inc(b_md[s], 16)
                    sp.dma_start(rst[:, s, :], RRR[bass.ds(t, 1), :].to_broadcast([H, 2 * P]))\
                        .then_inc(b_md[s], 16)

                stream(sp, ET, 4, body, 2)

            @block.gpsimd
            def _(pool):
                def scatter(g, s, t):
                    pool.wait_ge(b_out, t + 1)
                    hold(pool, 1, s, b_h1, t)
                    pool.indirect_dma_start(AGG, bass.IndirectOffsetOnAxis(slot[:, s, 2:3], 0), eo[:, s, :], None,
                                            bounds_check=NP - 1, oob_is_err=False).then_inc(b_sc[s], 16)

                def body(g, s):
                    t = g * 4 + s
                    if warm(g, s, 4, 4):
                        pool.wait_ge(b_sc[s], 16 * g)
                        pool.wait_ge(b_v, t - 3)
                    pool.tensor_copy(slot[:, s, :], idx[:, :, bass.ds(t, 1)].rearrange("p a t -> p (a t)"))\
                        .then_inc(b_ix, 1)
                    pool.wait_ge(b_ix, t + 1)
                    pool.wait_ge(b_0, 2)
                    hold(pool, 0, s, b_h0, t)
                    pool.indirect_dma_start(gl[:, s, :], None, XLE, bass.IndirectOffsetOnAxis(slot[:, s, 0:1], 0),
                                            bounds_check=NP - 1, oob_is_err=False).then_inc(b_gl[s], 16)
                    pool.indirect_dma_start(gr[:, s, :], None, XR, bass.IndirectOffsetOnAxis(slot[:, s, 1:2], 0),
                                            bounds_check=NP - 1, oob_is_err=False).then_inc(b_gr[s], 16)
                    if warm(g, s, 3, 4):
                        scatter(*ago(g, s, 3))

                stream(pool, ET, 4, body, 2)
                for t in range(ET - 3, ET):
                    scatter(*ago(0, t, 0))
                for s in range(4):
                    pool.wait_ge(b_sc[s], 16 * ((ET + 3 - s) // 4))

            @block.vector
            def _(dve):
                nc.vector.memset(gl[:], 0.0).then_inc(b_0, 1)
                nc.vector.memset(gr[:], 0.0).then_inc(b_0, 1)
                nc.vector.memset(mx[:], 0.0).then_inc(b_0, 1)
                nc.vector.memset(ea[:], 0.0).then_inc(b_0, 1)
                dve.wait_ge(b_0, 4)

                def logits(g, s, t):
                    h = s % 2
                    dve.wait_ge(b_gl[s], 16 * (g + 1))
                    dve.wait_ge(b_gr[s], 16 * (g + 1))
                    nc.vector.tensor_tensor(heads(me[:, h, :]), heads(gl[:, s, :]), heads(gr[:, s, :]), ALU.add)\
                        .then_inc(b_m, 1)
                    dve.wait_ge(b_m, t + 1)
                    nc.vector.scalar_tensor_tensor(me[:, h, :], me[:, h, :], SLOPE, me[:, h, :],
                                                   ALU.mult, ALU.max).then_inc(b_lr, 1)
                    dve.wait_ge(b_lr, t + 1)
                    nc.vector.tensor_tensor(me[:, h, :], me[:, h, :], att_b[:], ALU.mult).then_inc(b_la, 1)
                    dve.wait_ge(b_la, t + 1)
                    if not isinstance(t, int) or t >= 2:
                        dve.wait_ge(b_at, t - 1)
                    nc.vector.tensor_reduce(al[:, h, :], heads(me[:, h, :]), AX.X, ALU.add).then_inc(b_al, 1)

                def maxima(g, s, t):
                    h = s % 2
                    dve.wait_ge(b_at, t + 1)
                    if isinstance(t, int) and t == 0:
                        nc.vector.memset(aT[:, h, 0:1], 0.0)
                    else:
                        dve.wait_ge(b_mx, t)
                        nc.vector.tensor_copy(aT[:, h, 0:1], mx[0:H, 1 - h, P - 1:P])
                    nc.vector.tensor_copy(aT[:, h, 1:P], bank[h][0:H, 1:P]).then_inc(b_ac, 1)
                    dve.wait_ge(b_md[s], 32 * (g + 1))
                    dve.wait_ge(b_ac, t + 1)
                    nc.vector.tensor_tensor_scan(pf[:, h, :], rst[:, s, 0:P], aT[:, h, :], 0.0,
                                                 ALU.add, ALU.max).then_inc(b_pf, 1)
                    dve.wait_ge(b_pf, t + 1)
                    if not isinstance(t, int) or t >= 2:
                        dve.wait_ge(b_et, t - 1)
                    nc.vector.tensor_tensor_scan(mx[0:H, h, ::-1], rst[:, s, 2 * P - 1:P - 1:-1], pf[:, h, ::-1], 0.0,
                                                 ALU.add, ALU.max).then_inc(b_mx, 1)
                    dve.wait_ge(b_mx, t + 1)
                    if not isinstance(t, int) or t >= 2:
                        dve.wait_ge(b_e, t - 1)
                    nc.vector.tensor_tensor(dd[:, h, :], aT[:, h, :], mx[0:H, h, :], ALU.subtract).then_inc(b_d, 1)

                def weigh(g, s, t):
                    h = s % 2
                    if not isinstance(t, int) or t >= 2:
                        dve.wait_ge(b_s, t - 1)
                    nc.vector.tensor_scalar(sm[:, h, :], md[:, s, :], kd[:, bass.ds(t, 1)], None,
                                            ALU.is_equal).then_inc(b_S, 1)
                    dve.wait_ge(b_et, t + 1)
                    if not isinstance(t, int) or t >= 1:
                        dve.wait_ge(b_car, t)
                    nc.vector.tensor_tensor(heads(vv[:, h, :], CE), heads(gl[:, s, :], CE),
                                            bank[2 + h][:, 0:H].unsqueeze(2).to_broadcast([P, H, CE]),
                                            ALU.mult).then_inc(b_v, 1)

                def body(g, s):
                    logits(*ago(g, s, 0))
                    if warm(g, s, 1, 4):
                        maxima(*ago(g, s, 1))
                    if warm(g, s, 2, 4):
                        weigh(*ago(g, s, 2))

                stream(dve, ET, 4, body, 2)
                maxima(*ago(0, ET, 1))
                weigh(*ago(0, ET, 2))
                weigh(*ago(0, ET, 1))

            @block.tensor
            def _(pe):
                def alphas(g, s, t):
                    h = s % 2
                    pe.wait_ge(b_al, t + 1)
                    if not isinstance(t, int) or t >= 2:
                        pe.wait_ge(b_ac, t - 1)
                    nc.tensor.transpose(bank[h][0:H, 0:P], al[:, h, :], ident[:]).then_inc(b_at, 1)

                def weights(g, s, t):
                    h = s % 2
                    pe.wait_ge(b_e, t + 1)
                    if not isinstance(t, int) or t >= 2:
                        pe.wait_ge(b_out, t - 1)
                    nc.tensor.transpose(bank[2 + h][:, 0:P], ea[:, h, :], ident[:])
                    nc.tensor.transpose(bank[2 + h][:, P:2 * P], mx[:, h, :], ident[:]).then_inc(b_et, 1)

                def sums(g, s, t):
                    h = s % 2
                    pe.wait_ge(b_S, t + 1)
                    pe.wait_ge(b_v, t + 1)
                    for a in range(2):
                        last = nc.tensor.matmul(pair[h][:, a, :], sm[:, h, :], vv[:, h, a * XE // 2:(a + 1) * XE // 2],
                                                start=True, stop=True)
                    last.then_inc(b_s, 1)

                def body(g, s):
                    alphas(*ago(g, s, 0))
                    if warm(g, s, 1, 4):
                        weights(*ago(g, s, 1))
                    if warm(g, s, 2, 4):
                        sums(*ago(g, s, 2))

                stream(pe, ET, 4, body, 2)
                weights(*ago(0, ET, 1))
                sums(*ago(0, ET, 2))
                sums(*ago(0, ET, 1))

            @block.scalar
            def _(act):
                act.wait_ge(b_0, 4)

                def expo(g, s, t):
                    h = s % 2
                    act.wait_ge(b_d, t + 1)
                    if not isinstance(t, int) or t >= 2:
                        act.wait_ge(b_et, t - 1)
                    act.activation(ea[0:H, h, :], dd[:, h, :], ACT.Exp).then_inc(b_e, 1)

                def results(g, s, t, last=False):
                    h = s % 2
                    act.wait_ge(b_s, t + 1)
                    if not last:
                        act.wait_ge(b_m, t + 2)
                        act.activation(gl[0:1, (s + 1) % 4, :].rearrange("p (a c) -> p a c", a=2),
                                       pair[h][0:1, :, :], ACT.Copy).then_inc(b_car, 1)
                    if not isinstance(t, int) or t >= 4:
                        act.wait_ge(b_sc[s], 16 * g)
                    act.activation(eo[:, s, 0:XE].rearrange("p (a c) -> p a c", a=2), pair[h], ACT.Copy)
                    act.activation(eo[:, s, XE:AW], bank[2 + h][:, P:P + H], ACT.Copy).then_inc(b_out, 1)

                def body(g, s):
                    if warm(g, s, 1, 4):
                        expo(*ago(g, s, 1))
                    if warm(g, s, 2, 4):
                        results(*ago(g, s, 2))

                stream(act, ET, 4, body, 2)
                expo(*ago(0, ET, 1))
                results(*ago(0, ET, 2))
                results(*ago(0, ET, 1), last=True)
        end_phase(pb)

        pc = ExitStack()
        xi = sb("xi", [P, 4, D], F32, pc)
        ai = sb("ai", [P, 4, AW], F32, pc)
        li = sb("li", [P, 4, XE], F32, pc)
        mxn = sb("mxn", [P, 2, H], F32, pc)
        df = sb("df", [P, 2, 2, H], F32, pc)
        fe = sb("fe", [P, 2, 2, H], F32, pc)
        rd = sb("rd", [P, 2, H], F32, pc)
        oc = sb("oc", [P, 2, D], F32, pc)
        mi = sb("mi", [P, 2, D], F32, pc)
        xx = sb("xx", [P, 4, D], F32, pc)
        x1 = sb("x1", [P, 4, D], F32, pc)
        cst = sb("cst", [P, 2, 6], F32, pc)
        cmv = sb("cmv", [P, 2, 2], F32, pc)
        cve = sb("cve", [P, 2, 1], F32, pc)
        crs = sb("crs", [P, 2, 1], F32, pc)
        n1 = sb("n1", [P, 2, D], F32, pc)
        n1T = sb("n1T", [P, 2, DK, P], F32, pc)
        hb = sb("hb", [P, 2, FC + NE], F32, pc)
        m8 = sb("m8", [P, 2, 8], F32, pc)
        i8 = sb("i8", [P, 2, 8], U32, pc)
        ix = sb("ix", [P, 2, 1], F32, pc)
        hm = sb("hm", [P, 2, FC + NE], F32, pc)
        hT = sb("hT", [P, 2, 3, P], F32, pc)
        x2 = sb("x2", [P, 4, D], F32, pc)
        st2 = sb("st2", [P, 2, 6], F32, pc)
        mv2 = sb("mv2", [P, 2, 2], F32, pc)
        ve2 = sb("ve2", [P, 2, 1], F32, pc)
        rs2 = sb("rs2", [P, 2, 1], F32, pc)
        n2 = sb("n2", [P, 2, D], F32, pc)
        n2T = sb("n2T", [P, 2, DK, P], F32, pc)
        gb = sb("gb", [P, 2, D], F32, pc)
        gs = sb("gs", [P, 4, D], F32, pc)
        c_hold = sb("c_hold", [P, 4, 2], F32, pc)
        c_ld, c_sx, c_sg = sems("c_ld", 4), sems("c_sx", 4), sems("c_sg", 4)
        (c_mn, c_df, c_f, c_t1, c_t2, c_s, c_den, c_rd, c_o, c_ob, c_mi, c_ex, c_xx, c_r, c_x1, c_bn, c_mv, c_ve, c_rs,
         c_n1, c_tr1, c_n1T, c_up, c_hb, c_m8, c_i8, c_ix, c_oh, c_hm, c_trh, c_hT, c_dn, c_x2, c_bn2, c_mv2, c_ve2,
         c_rs2, c_n2, c_tr2, c_n2T, c_g, c_gb, c_gs, c_hd1, c_hd2) = (
            sem("c_" + n) for n in ("mn df f t1 t2 s den rd o ob mi ex xx r x1 bn mv ve rs n1 tr1 n1T up hb m8 i8 ix "
                                    "oh hm trh hT dn x2 bn2 mv2 ve2 rs2 n2 tr2 n2T g gb gs hd1 hd2").split())

        def since(eng, done, t, lag):
            if not isinstance(t, int) or t >= lag:
                eng.wait_ge(done, t - lag + 1)

        with nc.Block() as block:
            @block.sync
            def _(sp):
                def store_x2(g, s, t):
                    sp.wait_ge(c_x2, t + 1)
                    sp.dma_start(row(X2, t), x2[:, s, :]).then_inc(c_sx[s], 16)

                def store_g(g, s, t):
                    sp.wait_ge(c_gs, t + 1)
                    sp.dma_start(row(GR, t), gs[:, s, :]).then_inc(c_sg[s], 16)

                def body(g, s):
                    t = g * 4 + s
                    since(sp, c_xx, t, 4)
                    since(sp, c_o, t, 4)
                    n = TAIL if isinstance(g, int) and t == NT - 1 else P
                    sp.dma_start(xi[0:n, s, :], row(x, t, n)).then_inc(c_ld[s], 16)
                    sp.dma_start(ai[:, s, :], row(AGG, t)).then_inc(c_ld[s], 16)
                    sp.dma_start(li[:, s, :], row(XLE, t)).then_inc(c_ld[s], 16)
                    if warm(g, s, 7, 4):
                        store_x2(*ago(g, s, 7))
                    if warm(g, s, 9, 4):
                        store_g(*ago(g, s, 9))

                stream(sp, NT, 4, body, 3)
                for t in range(NT, NT + 9):
                    if t - 7 < NT:
                        store_x2(*ago(0, t, 7))
                    store_g(*ago(0, t, 9))
                for s in range(4):
                    sp.wait_ge(c_sx[s], 16 * ((NT + 3 - s) // 4))
                    sp.wait_ge(c_sg[s], 16 * ((NT + 3 - s) // 4))

            @block.gpsimd
            def _(pool):
                def self_part(g, s, t):
                    h = s % 2
                    pool.wait_ge(c_ld[s], 48 * (g + 1))
                    pool.wait_ge(c_f, t + 1)
                    pool.tensor_tensor(heads(li[:, s, :], CE), heads(li[:, s, :], CE),
                                       fe[:, h, 1, :].unsqueeze(2).to_broadcast([P, H, CE]), ALU.mult)\
                        .then_inc(c_t2, 1)

                def root(t, h, mv_, ve_, rs_, d_mv, d_ve, d_rs, d_n):
                    pool.wait_ge(d_mv, t + 1)
                    pool.tensor_tensor(ve_[:, h, :], mv_[:, h, 1:2], epst[:], ALU.add).then_inc(d_ve, 1)
                    since(pool, d_n, t, 2)
                    pool.wait_ge(d_ve, t + 1)
                    pool.tensor_tensor(rs_[:, h, :], ve_[:, h, :], mhalf[:, 0:1], ALU.pow).then_inc(d_rs, 1)

                def body(g, s):
                    self_part(*ago(g, s, 0))
                    if warm(g, s, 5, 4):
                        root(g * 4 + s - 5, (s + 1) % 2, mv2, ve2, rs2, c_mv2, c_ve2, c_rs2, c_n2)
                    if warm(g, s, 2, 4):
                        root(g * 4 + s - 2, s % 2, cmv, cve, crs, c_mv, c_ve, c_rs, c_n1)

                stream(pool, NT, 4, body, 2)
                for t in range(NT, NT + 5):
                    root(t - 5, (t - 5) % 2, mv2, ve2, rs2, c_mv2, c_ve2, c_rs2, c_n2)
                    if t - 2 < NT:
                        root(t - 2, t % 2, cmv, cve, crs, c_mv, c_ve, c_rs, c_n1)

            @block.vector
            def _(dve):
                def shifts(g, s, t):
                    h = s % 2
                    dve.wait_ge(c_ld[s], 48 * (g + 1))
                    own = selfa[:, bass.ds(t, 1), :].rearrange("p t h -> p (t h)")
                    nc.vector.tensor_tensor(mxn[:, h, :], ai[:, s, XE:AW], own, ALU.max).then_inc(c_mn, 1)
                    since(dve, c_f, t, 2)
                    dve.wait_ge(c_mn, t + 1)
                    nc.vector.tensor_tensor(df[:, h, 0, :], ai[:, s, XE:AW], mxn[:, h, :], ALU.subtract)
                    nc.vector.tensor_tensor(df[:, h, 1, :], own, mxn[:, h, :], ALU.subtract).then_inc(c_df, 1)

                def average(g, s, t):
                    h = s % 2
                    dve.wait_ge(c_f, t + 1)
                    nc.vector.tensor_tensor(heads(ai[:, s, 0:XE], CE), heads(ai[:, s, 0:XE], CE),
                                            fe[:, h, 0, :].unsqueeze(2).to_broadcast([P, H, CE]), ALU.mult)\
                        .then_inc(c_t1, 1)
                    dve.wait_ge(c_t1, t + 1)
                    dve.wait_ge(c_t2, t + 1)
                    nc.vector.tensor_tensor(ai[:, s, 0:XE], ai[:, s, 0:XE], li[:, s, :], ALU.add).then_inc(c_s, 1)
                    dve.wait_ge(c_s, t + 1)
                    nc.vector.tensor_scalar_max(rd[:, h, :], heads(ai[:, s, 0:XE], CE)[:, :, C:CE].rearrange(
                        "p h c -> p (h c)"), 1e-16).then_inc(c_den, 1)
                    dve.wait_ge(c_den, t + 1)
                    nc.vector.reciprocal(rd[:, h, :], rd[:, h, :]).then_inc(c_rd, 1)
                    dve.wait_ge(c_rd, t + 1)
                    nc.vector.tensor_tensor(heads(oc[:, h, :]), heads(ai[:, s, 0:XE], CE)[:, :, 0:C],
                                            rd[:, h, :].unsqueeze(2).to_broadcast([P, H, C]), ALU.mult)\
                        .then_inc(c_o, 1)
                    dve.wait_ge(c_o, t + 1)
                    nc.vector.tensor_tensor(oc[:, h, :], oc[:, h, :], gb_b[:], ALU.add).then_inc(c_ob, 1)
                    dve.wait_ge(c_ob, t + 1)
                    nc.vector.tensor_scalar_min(mi[:, h, :], oc[:, h, :], 0.0).then_inc(c_mi, 1)

                def elu(g, s, t):
                    h = s % 2
                    dve.wait_ge(c_ex, t + 1)
                    nc.vector.scalar_tensor_tensor(mi[:, h, :], oc[:, h, :], 0.0, mi[:, h, :],
                                                   ALU.max, ALU.add).then_inc(c_r, 1)
                    dve.wait_ge(c_xx, t + 1)
                    dve.wait_ge(c_r, t + 1)
                    nc.vector.scalar_tensor_tensor(x1[:, s, :], mi[:, h, :], -1.0, xx[:, s, :],
                                                   ALU.add, ALU.add).then_inc(c_x1, 1)
                    dve.wait_ge(c_x1, t + 1)
                    nc.vector.bn_stats(cst[:, h, :], x1[:, s, :]).then_inc(c_bn, 1)
                    dve.wait_ge(c_bn, t + 1)
                    nc.vector.memset(c_hold[:, s, 0:1], 0.0)
                    nc.vector.bn_aggr(cmv[:, h, :], cst[:, h, :]).then_inc(c_mv, 1)

                def norm1(g, s, t):
                    h = s % 2
                    dve.wait_ge(c_rs, t + 1)
                    since(dve, c_tr1, t, 2)
                    nc.vector.tensor_scalar(n1[:, h, :], x1[:, s, :], cmv[:, h, 0:1], crs[:, h, :],
                                            ALU.subtract, ALU.mult).then_inc(c_n1, 1)

                def route(g, s, t):
                    h = s % 2
                    dve.wait_ge(c_up, t + 1)
                    nc.vector.tensor_tensor(hb[:, h, :], bank[1][:, 0:FC + NE], b1b[:], ALU.add).then_inc(c_hb, 1)
                    dve.wait_ge(c_hb, t + 1)
                    nc.vector.memset(c_hold[:, s, 1:2], 0.0)
                    nc.vector.max(m8[:, h, :], hb[:, h, FC:FC + NE]).then_inc(c_m8, 1)
                    dve.wait_ge(c_m8, t + 1)
                    nc.vector.memset(c_hold[:, s, 1:2], 0.0)
                    nc.vector.max_index(i8[:, h, :], m8[:, h, :], hb[:, h, FC:FC + NE]).then_inc(c_i8, 1)
                    dve.wait_ge(c_i8, t + 1)
                    nc.vector.tensor_copy(ix[:, h, :], i8[:, h, 0:1]).then_inc(c_ix, 1)
                    since(dve, c_trh, t, 2)
                    dve.wait_ge(c_ix, t + 1)
                    nc.vector.tensor_scalar(hm[:, h, FC:FC + NE], iota[:, 0:NE], ix[:, h, :], None,
                                            ALU.is_equal).then_inc(c_oh, 1)
                    dve.wait_ge(c_oh, t + 1)
                    nc.vector.scalar_tensor_tensor(
                        hm[:, h, 0:FC].rearrange("p (e f) -> p e f", e=NE),
                        hb[:, h, 0:FC].rearrange("p (e f) -> p e f", e=NE), 0.0,
                        hm[:, h, FC:FC + NE].unsqueeze(2).to_broadcast([P, NE, FH]), ALU.max, ALU.mult)\
                        .then_inc(c_hm, 1)

                def add_experts(g, s, t):
                    h = s % 2
                    if not isinstance(t, int) or t >= 4:
                        dve.wait_ge(c_sx[s], 16 * g)
                    dve.wait_ge(c_dn, t + 1)
                    nc.vector.tensor_tensor(x2[:, s, :], bank[3], x1[:, s, :], ALU.add).then_inc(c_x2, 1)
                    dve.wait_ge(c_x2, t + 1)
                    nc.vector.bn_stats(st2[:, h, :], x2[:, s, :]).then_inc(c_bn2, 1)
                    dve.wait_ge(c_bn2, t + 1)
                    nc.vector.memset(c_hold[:, s, 0:1], 0.0)
                    nc.vector.bn_aggr(mv2[:, h, :], st2[:, h, :]).then_inc(c_mv2, 1)

                def norm2(g, s, t):
                    h = s % 2
                    dve.wait_ge(c_rs2, t + 1)
                    since(dve, c_tr2, t, 2)
                    nc.vector.tensor_scalar(n2[:, h, :], x2[:, s, :], mv2[:, h, 0:1], rs2[:, h, :],
                                            ALU.subtract, ALU.mult).then_inc(c_n2, 1)

                def gcn_bias(g, s, t):
                    h = s % 2
                    dve.wait_ge(c_g, t + 1)
                    since(dve, c_gs, t, 2)
                    nc.vector.tensor_tensor(gb[:, h, :], bank[5], bgb[:], ALU.add).then_inc(c_gb, 1)

                steps = ((7, gcn_bias), (6, norm2), (5, add_experts), (4, route), (3, norm1), (2, elu), (1, average))

                def body(g, s):
                    for lag, step in steps:
                        if warm(g, s, lag, 4):
                            step(*ago(g, s, lag))
                    shifts(*ago(g, s, 0))

                stream(dve, NT, 4, body, 2)
                for t in range(NT, NT + 7):
                    for lag, step in steps:
                        if t - lag < NT:
                            step(*ago(0, t, lag))

            @block.tensor
            def _(pe):
                def up(g, s, t):
                    pe.wait_ge(c_n1T, t + 1)
                    since(pe, c_hb, t, 1)
                    mm4(bank[1][:, 0:FC + NE], n1T[:, s % 2, :, :], wc).then_inc(c_up, 1)

                def down(g, s, t):
                    h = s % 2
                    pe.wait_ge(c_hT, t + 1)
                    since(pe, c_x2, t, 1)
                    for k in range(FC // P):
                        nc.tensor.matmul(bank[3], hT[:, h, k, :], w2[:, k, :], start=(k == 0), stop=False)
                    nc.tensor.matmul(bank[3], hT[0:NE, h, 2, :], b2[:], start=False, stop=True).then_inc(c_dn, 1)

                def gcn(g, s, t):
                    pe.wait_ge(c_n2T, t + 1)
                    since(pe, c_gb, t, 1)
                    mm4(bank[5], n2T[:, s % 2, :, :], wg).then_inc(c_g, 1)

                def turn2(g, s, t):
                    pe.wait_ge(c_n2, t + 1)
                    since(pe, c_n2T, t, 1)
                    tr4(bank[4], n2[:, s % 2, :]).then_inc(c_tr2, 1)

                def turn_h(g, s, t):
                    h = s % 2
                    pe.wait_ge(c_hm, t + 1)
                    since(pe, c_hT, t, 1)
                    tr4(bank[2], hm[:, h, :], FC // P)
                    nc.tensor.transpose(bank[2][0:NE, FC:FC + P], hm[:, h, FC:FC + NE], ident[:]).then_inc(c_trh, 1)

                def turn1(g, s, t):
                    pe.wait_ge(c_n1, t + 1)
                    since(pe, c_n1T, t, 1)
                    tr4(bank[0], n1[:, s % 2, :]).then_inc(c_tr1, 1)

                steps = ((7, gcn), (5, down), (4, up), (6, turn2), (4, turn_h), (3, turn1))

                def body(g, s):
                    for lag, step in steps:
                        if warm(g, s, lag, 4):
                            step(*ago(g, s, lag))

                stream(pe, NT, 4, body, 2)
                for t in range(NT, NT + 7):
                    for lag, step in steps:
                        if t - lag < NT:
                            step(*ago(0, t, lag))

            @block.scalar
            def _(act):
                def scaled(g, s, t):
                    act.wait_ge(c_gb, t + 1)
                    if not isinstance(t, int) or t >= 4:
                        act.wait_ge(c_sg[s], 16 * g)
                    act.activation(gs[:, s, :], gb[:, s % 2, :], ACT.Copy, scale=dis[:, bass.ds(t, 1)])\
                        .then_inc(c_gs, 1)

                def copy2(g, s, t):
                    act.wait_ge(c_tr2, t + 1)
                    since(act, c_g, t, 2)
                    act.activation(n2T[:, s % 2, :, :].rearrange("p k n -> p (k n)"), bank[4], ACT.Copy)\
                        .then_inc(c_n2T, 1)

                def copy_h(g, s, t):
                    h = s % 2
                    act.wait_ge(c_trh, t + 1)
                    since(act, c_dn, t, 2)
                    act.activation(hT[:, h, 0:2, :].rearrange("p k n -> p (k n)"), bank[2][:, 0:FC], ACT.Copy)
                    act.activation(hT[0:NE, h, 2, :], bank[2][0:NE, FC:FC + P], ACT.Copy).then_inc(c_hT, 1)

                def copy1(g, s, t):
                    act.wait_ge(c_tr1, t + 1)
                    since(act, c_up, t, 2)
                    act.activation(n1T[:, s % 2, :, :].rearrange("p k n -> p (k n)"), bank[0], ACT.Copy)\
                        .then_inc(c_n1T, 1)

                def exp_min(g, s, t):
                    act.wait_ge(c_mi, t + 1)
                    act.activation(mi[:, s % 2, :], mi[:, s % 2, :], ACT.Exp).then_inc(c_ex, 1)

                def exp_shift(g, s, t):
                    h = s % 2
                    act.wait_ge(c_ld[s], 48 * (g + 1))
                    since(act, c_x1, t, 4)
                    act.activation(xx[:, s, :], xi[:, s, :], ACT.Identity, scale=xsc[:, bass.ds(t, 1), 1],
                                   bias=xsc[:, bass.ds(t, 1), 0]).then_inc(c_xx, 1)
                    act.wait_ge(c_df, t + 1)
                    since(act, c_t1, t, 2)
                    since(act, c_t2, t, 2)
                    act.activation(fe[:, h, :, :], df[:, h, :, :], ACT.Exp).then_inc(c_f, 1)

                steps = ((7, scaled), (6, copy2), (4, copy_h), (3, copy1), (1, exp_min))

                def body(g, s):
                    for lag, step in steps:
                        if warm(g, s, lag, 4):
                            step(*ago(g, s, lag))
                    exp_shift(*ago(g, s, 0))

                stream(act, NT, 4, body, 2)
                for t in range(NT, NT + 7):
                    for lag, step in steps:
                        if t - lag < NT:
                            step(*ago(0, t, lag))
        end_phase(pc)

        m1 = sb("m1", [P, DK, MC])
        m2 = sb("m2", [P, MC // P, D])
        m_ld = sem("m_ld")
        pd = ExitStack()
        gg = sb("gg", [P, 4, D], F32, pd)
        md2 = sb("md2", [P, 4, P], F32, pd)
        sm2 = sb("sm2", [P, 2, P], F32, pd)
        go = sb("go", [P, 4, D], F32, pd)
        d_ld, d_md, d_sc = sems("d_ld", 4), sems("d_md", 4), sems("d_sc", 4)
        d_0, d_ix, d_S, d_s, d_car, d_out, d_h0, d_h1 = (
            sem("d_" + n) for n in ("0", "ix", "S", "s", "car", "out", "h0", "h1"))

        with nc.Block() as block:
            @block.sync
            def _(sp):
                def body(g, s):
                    t = g * 4 + s
                    since(sp, d_S, t, 4)
                    sp.dma_start(md2[:, s, :], MDR[bass.ds(t, 1), :].to_broadcast([P, P])).then_inc(d_md[s], 16)

                stream(sp, ET, 4, body)
                for t, s in ((m1, M1), (m2, M2)):
                    sp.dma_start(t[:], s.rearrange("(k p) n -> p k n", p=P)).then_inc(m_ld, 16)
                sp.wait_ge(m_ld, 32)

            @block.gpsimd
            def _(pool):
                def scatter(g, s, t):
                    pool.wait_ge(d_out, t + 1)
                    hold(pool, 1, s, d_h1, t)
                    pool.indirect_dma_start(AG2, bass.IndirectOffsetOnAxis(slot[:, s, 2:3], 0), go[:, s, :], None,
                                            bounds_check=NP - 1, oob_is_err=False).then_inc(d_sc[s], 16)

                def body(g, s):
                    t = g * 4 + s
                    if warm(g, s, 4, 4):
                        pool.wait_ge(d_sc[s], 16 * g)
                        pool.wait_ge(d_s, t - 3)
                    pool.tensor_copy(slot[:, s, :], idx[:, :, bass.ds(t, 1)].rearrange("p a t -> p (a t)"))\
                        .then_inc(d_ix, 1)
                    pool.wait_ge(d_ix, t + 1)
                    pool.wait_ge(d_0, 1)
                    hold(pool, 0, s, d_h0, t)
                    pool.indirect_dma_start(gg[:, s, :], None, GR, bass.IndirectOffsetOnAxis(slot[:, s, 0:1], 0),
                                            bounds_check=NP - 1, oob_is_err=False).then_inc(d_ld[s], 16)
                    if warm(g, s, 3, 4):
                        scatter(*ago(g, s, 3))

                stream(pool, ET, 4, body, 2)
                for t in range(ET - 3, ET):
                    scatter(*ago(0, t, 0))
                for s in range(4):
                    pool.wait_ge(d_sc[s], 16 * ((ET + 3 - s) // 4))

            @block.vector
            def _(dve):
                nc.vector.memset(gg[:], 0.0).then_inc(d_0, 1)

                def results(g, s, t):
                    dve.wait_ge(d_s, t + 1)
                    if not isinstance(t, int) or t < ET - 1:
                        dve.wait_ge(d_car, t + 1)
                    if not isinstance(t, int) or t >= 4:
                        dve.wait_ge(d_sc[s], 16 * g)
                    nc.vector.tensor_copy(go[:, s, :], bank[s % 2]).then_inc(d_out, 1)

                def body(g, s):
                    t = g * 4 + s
                    dve.wait_ge(d_md[s], 16 * (g + 1))
                    since(dve, d_s, t, 2)
                    nc.vector.tensor_scalar(sm2[:, s % 2, :], md2[:, s, :], kd[:, bass.ds(t, 1)], None,
                                            ALU.is_equal).then_inc(d_S, 1)
                    if warm(g, s, 1, 4):
                        results(*ago(g, s, 1))

                stream(dve, ET, 4, body, 2)
                results(*ago(0, ET, 1))

            @block.tensor
            def _(pe):
                def body(g, s):
                    t = g * 4 + s
                    pe.wait_ge(d_S, t + 1)
                    pe.wait_ge(d_ld[s], 16 * (g + 1))
                    since(pe, d_car, t, 1)
                    since(pe, d_out, t, 2)
                    nc.tensor.matmul(bank[s % 2], sm2[:, s % 2, :], gg[:, s, :], start=True, stop=True)\
                        .then_inc(d_s, 1)

                stream(pe, ET, 4, body)

            @block.scalar
            def _(act):
                def body(g, s):
                    t = g * 4 + s
                    if isinstance(g, int) and t == ET - 1:
                        return
                    act.wait_ge(d_s, t + 1)
                    n = s + 1
                    act.wait_ge(d_ld[n % 4], 16 * (g + 1 + n // 4))
                    act.activation(gg[0:1, n % 4, :], bank[s % 2][0:1, :], ACT.Copy).then_inc(d_car, 1)

                stream(act, ET, 4, body)
        end_phase(pd)

        X3 = nc.dram_tensor("x3_rows", [NP, D], F32).ap()
        XN3 = nc.dram_tensor("n3_rows", [NP, D], F32).ap()
        wts = sb("wts", [P, NT, ME])
        pe_ = ExitStack()
        ex2 = sb("ex2", [P, 4, D], F32, pe_)
        eg = sb("eg", [P, 4, D], F32, pe_)
        ea2 = sb("ea2", [P, 4, D], F32, pe_)
        er = sb("er", [P, 2, D], F32, pe_)
        x3 = sb("x3", [P, 4, D], F32, pe_)
        est = sb("est", [P, 2, 6], F32, pe_)
        emv = sb("emv", [P, 2, 2], F32, pe_)
        eve = sb("eve", [P, 2, 1], F32, pe_)
        ers = sb("ers", [P, 2, 1], F32, pe_)
        n3 = sb("n3", [P, 4, D], F32, pe_)
        n3T = sb("n3T", [P, 2, DK, P], F32, pe_)
        lg = sb("lg", [P, 2, MH * ME], F32, pe_)
        hm8 = sb("hm8", [P, 2, MH, 8], F32, pe_)
        hi8 = sb("hi8", [P, 2, MH, 8], U32, pe_)
        sc8 = sb("sc8", [P, 2, 8], F32, pe_)
        cand = sb("cand", [P, 2, MH], F32, pe_)
        tm8 = sb("tm8", [P, 2, 8], F32, pe_)
        ti8 = sb("ti8", [P, 2, 8], U32, pe_)
        tf = sb("tf", [P, 2, 2], F32, pe_)
        pick = sb("pick", [P, 2, 2, MH], F32, pe_)
        sel = sb("sel", [P, 2, 2], F32, pe_)
        oh = sb("oh", [P, 2, 2, ME], BF16, pe_)
        ohs = sb("ohs", [P, 2, ME], BF16, pe_)
        cum = sb("cum", [P, 2, ME], BF16, pe_)
        pos1 = sb("pos1", [P, 2, ME], F32, pe_)
        keep = sb("keep", [P, 2, 2, ME], F32, pe_)
        ehold = sb("ehold", [P, 4, 8], F32, pe_)
        e_ld, e_s3, e_sn = sems("e_ld", 4), sems("e_s3", 4), sems("e_sn", 4)
        (e_0, e_y, e_r, e_x3, e_bn, e_mv, e_ve, e_rs, e_n3, e_tr, e_nT, e_lg, e_lc, e_m8, e_i8, e_sc, e_tm, e_ti, e_tf,
         e_pk, e_oh, e_os, e_cu, e_pre, e_p1, e_k0, e_k1, e_ks, e_w) = (
            sem("e_" + n) for n in ("0 y r x3 bn mv ve rs n3 tr nT lg lc m8 i8 sc tm ti tf pk oh os cu pre p1 k0 k1 ks "
                                    "w").split())

        with nc.Block() as block:
            @block.sync
            def _(sp):
                def store(g, s, t):
                    sp.wait_ge(e_x3, t + 1)
                    sp.dma_start(row(X3, t), x3[:, s, :]).then_inc(e_s3[s], 16)
                    sp.wait_ge(e_n3, t + 1)
                    sp.dma_start(row(XN3, t), n3[:, s, :]).then_inc(e_sn[s], 16)

                def body(g, s):
                    t = g * 4 + s
                    since(sp, e_x3, t, 4)
                    sp.dma_start(ex2[:, s, :], row(X2, t)).then_inc(e_ld[s], 16)
                    sp.dma_start(eg[:, s, :], row(GR, t)).then_inc(e_ld[s], 16)
                    sp.dma_start(ea2[:, s, :], row(AG2, t)).then_inc(e_ld[s], 16)
                    if warm(g, s, 4, 4):
                        store(*ago(g, s, 4))

                stream(sp, NT, 4, body, 2)
                for t in range(NT, NT + 4):
                    store(*ago(0, t, 4))
                for s in range(4):
                    sp.wait_ge(e_s3[s], 16 * ((NT + 3 - s) // 4))
                    sp.wait_ge(e_sn[s], 16 * ((NT + 3 - s) // 4))

            @block.gpsimd
            def _(pool):
                def body(g, s):
                    t, h = g * 4 + s, s % 2
                    pool.wait_ge(e_mv, t + 1)
                    pool.tensor_tensor(eve[:, h, :], emv[:, h, 1:2], epst[:], ALU.add).then_inc(e_ve, 1)
                    since(pool, e_n3, t, 2)
                    pool.wait_ge(e_ve, t + 1)
                    pool.tensor_tensor(ers[:, h, :], eve[:, h, :], mhalf[:, 0:1], ALU.pow).then_inc(e_rs, 1)

                stream(pool, NT, 4, body)

            @block.vector
            def _(dve):
                nc.vector.memset(cum[:], 0.0).then_inc(e_0, 1)
                nc.vector.memset(sc8[:], -BIG).then_inc(e_0, 1)
                dve.wait_ge(e_0, 2)

                def hold_dve(s, k):
                    nc.vector.memset(ehold[:, s, k:k + 1], 0.0)

                def both(g, s, t):
                    dve.wait_ge(e_ld[s], 48 * (g + 1))
                    nc.vector.tensor_tensor(ea2[:, s, :], ea2[:, s, :], eg[:, s, :], ALU.add).then_inc(e_y, 1)

                def residual(g, s, t):
                    h = s % 2
                    dve.wait_ge(e_r, t + 1)
                    if not isinstance(t, int) or t >= 4:
                        dve.wait_ge(e_s3[s], 16 * g)
                    nc.vector.tensor_tensor(x3[:, s, :], er[:, h, :], ex2[:, s, :], ALU.add).then_inc(e_x3, 1)
                    dve.wait_ge(e_x3, t + 1)
                    nc.vector.bn_stats(est[:, h, :], x3[:, s, :]).then_inc(e_bn, 1)
                    dve.wait_ge(e_bn, t + 1)
                    hold_dve(s, 0)
                    nc.vector.bn_aggr(emv[:, h, :], est[:, h, :]).then_inc(e_mv, 1)

                def norm(g, s, t):
                    h = s % 2
                    dve.wait_ge(e_rs, t + 1)
                    since(dve, e_tr, t, 4)
                    if not isinstance(t, int) or t >= 4:
                        dve.wait_ge(e_sn[s], 16 * g)
                    nc.vector.tensor_scalar(n3[:, s, :], x3[:, s, :], emv[:, h, 0:1], ers[:, h, :],
                                            ALU.subtract, ALU.mult).then_inc(e_n3, 1)

                def select(g, s, t):
                    h = s % 2
                    dve.wait_ge(e_lc, t + 1)
                    hold_dve(s, 1)
                    for k in range(MH):
                        last = nc.vector.max(hm8[:, h, k, :], lg[:, h, k * ME:(k + 1) * ME])
                    last.then_inc(e_m8, 1)
                    dve.wait_ge(e_m8, t + 1)
                    hold_dve(s, 2)
                    for k in range(MH):
                        last = nc.vector.max_index(hi8[:, h, k, :], hm8[:, h, k, :], lg[:, h, k * ME:(k + 1) * ME])
                    last.then_inc(e_i8, 1)
                    nc.vector.tensor_copy(sc8[:, h, 0:MH], hm8[:, h, :, 0]).then_inc(e_sc, 1)
                    dve.wait_ge(e_i8, t + 1)
                    nc.vector.tensor_copy(cand[:, h, :], hi8[:, h, :, 0]).then_inc(e_sc, 1)
                    dve.wait_ge(e_sc, 2 * t + 2)
                    hold_dve(s, 3)
                    nc.vector.max(tm8[:, h, :], sc8[:, h, :]).then_inc(e_tm, 1)
                    dve.wait_ge(e_tm, t + 1)
                    hold_dve(s, 4)
                    nc.vector.max_index(ti8[:, h, :], tm8[:, h, :], sc8[:, h, :]).then_inc(e_ti, 1)
                    dve.wait_ge(e_ti, t + 1)
                    nc.vector.tensor_copy(tf[:, h, :], ti8[:, h, 0:2]).then_inc(e_tf, 1)
                    dve.wait_ge(e_tf, t + 1)
                    for k in range(2):
                        last = nc.vector.scalar_tensor_tensor(pick[:, h, k, :], iota[:, 0:MH], tf[:, h, k:k + 1],
                                                              cand[:, h, :], ALU.is_equal, ALU.mult,
                                                              accum_out=sel[:, h, k:k + 1])
                    last.then_inc(e_pk, 1)
                    dve.wait_ge(e_pk, t + 1)
                    for k in range(2):
                        last = nc.vector.tensor_scalar(oh[:, h, k, :], iota[:, 0:ME], sel[:, h, k:k + 1], None,
                                                       ALU.is_equal)
                    last.then_inc(e_oh, 1)
                    dve.wait_ge(e_oh, t + 1)
                    since(dve, e_pre, t, 1)
                    nc.vector.tensor_tensor(ohs[:, h, :], oh[:, h, 0, :], oh[:, h, 1, :], ALU.add).then_inc(e_os, 1)
                    dve.wait_ge(e_os, t + 1)
                    nc.vector.tensor_tensor(cum[:, 1 - h, :], cum[:, h, :], ohs[:, h, :], ALU.add).then_inc(e_cu, 1)

                def weigh(g, s, t):
                    h = s % 2
                    dve.wait_ge(e_pre, t + 1)
                    nc.vector.tensor_tensor(pos1[:, h, :], bank[2][:, 0:ME], oh[:, h, 0, :], ALU.add).then_inc(e_p1, 1)
                    nc.vector.scalar_tensor_tensor(keep[:, h, 0, :], bank[2][:, 0:ME], float(CAP), oh[:, h, 0, :],
                                                   ALU.is_lt, ALU.mult).then_inc(e_k0, 1)
                    dve.wait_ge(e_p1, t + 1)
                    nc.vector.scalar_tensor_tensor(keep[:, h, 1, :], pos1[:, h, :], float(CAP), oh[:, h, 1, :],
                                                   ALU.is_lt, ALU.mult).then_inc(e_k1, 1)
                    dve.wait_ge(e_k1, t + 1)
                    dve.wait_ge(e_k0, t + 1)
                    nc.vector.tensor_tensor(pos1[:, h, :], keep[:, h, 0, :], keep[:, h, 1, :], ALU.add)\
                        .then_inc(e_ks, 1)
                    dve.wait_ge(e_ks, t + 1)
                    nc.vector.tensor_scalar_mul(wts[:, bass.ds(t, 1), :].rearrange("p t e -> p (t e)"),
                                                pos1[:, h, :], 0.5).then_inc(e_w, 1)

                steps = ((5, weigh), (4, select), (2, norm), (1, residual), (0, both))

                def body(g, s):
                    for lag, step in steps:
                        if warm(g, s, lag, 4):
                            step(*ago(g, s, lag))

                stream(dve, NT, 4, body, 2)
                for t in range(NT, NT + 5):
                    for lag, step in steps:
                        if t - lag < NT:
                            step(*ago(0, t, lag))
                dve.wait_ge(e_w, NT)

            @block.tensor
            def _(pe):
                def places(g, s, t):
                    h = s % 2
                    pe.wait_ge(e_os, t + 1)
                    pe.wait_ge(e_cu, t + 1)
                    since(pe, e_w, t, 1)
                    nc.tensor.matmul(bank[2][:, 0:ME], tri[:], ohs[:, h, :], start=True, stop=False)
                    nc.tensor.matmul(bank[2][:, 0:ME], onesb[:], cum[:, h, :], start=False, stop=True)\
                        .then_inc(e_pre, 1)

                def logits(g, s, t):
                    pe.wait_ge(e_nT, t + 1)
                    since(pe, e_lc, t, 1)
                    mm4(bank[1][:, 0:MH * ME], n3T[:, s % 2, :, :], hp).then_inc(e_lg, 1)

                def turn(g, s, t):
                    pe.wait_ge(e_n3, t + 1)
                    since(pe, e_nT, t, 1)
                    tr4(bank[0], n3[:, s, :]).then_inc(e_tr, 1)

                steps = ((3, logits), (4, places), (2, turn))

                def body(g, s):
                    for lag, step in steps:
                        if warm(g, s, lag, 4):
                            step(*ago(g, s, lag))

                stream(pe, NT, 4, body, 2)
                for t in range(NT, NT + 4):
                    for lag, step in steps:
                        if t - lag < NT:
                            step(*ago(0, t, lag))

            @block.scalar
            def _(act):
                def copy_logits(g, s, t):
                    act.wait_ge(e_lg, t + 1)
                    since(act, e_i8, t, 2)
                    act.activation(lg[:, s % 2, :], bank[1][:, 0:MH * ME], ACT.Copy).then_inc(e_lc, 1)

                def copy_n(g, s, t):
                    act.wait_ge(e_tr, t + 1)
                    since(act, e_lg, t, 2)
                    act.activation(n3T[:, s % 2, :, :].rearrange("p k n -> p (k n)"), bank[0], ACT.Copy)\
                        .then_inc(e_nT, 1)

                def relu(g, s, t):
                    act.wait_ge(e_y, t + 1)
                    since(act, e_x3, t, 2)
                    act.activation(er[:, s % 2, :], ea2[:, s, :], ACT.Relu, scale=dis[:, bass.ds(t, 1)])\
                        .then_inc(e_r, 1)

                steps = ((3, copy_logits), (2, copy_n), (0, relu))

                def body(g, s):
                    for lag, step in steps:
                        if warm(g, s, lag, 4):
                            step(*ago(g, s, lag))

                stream(act, NT, 4, body, 2)
                for t in range(NT, NT + 3):
                    for lag, step in steps:
                        if t - lag < NT:
                            step(*ago(0, t, lag))
        end_phase(pe_)

        pf_ = ExitStack()
        f3 = sb("f3", [P, 2, D], F32, pf_)
        fn = sb("fn", [P, 2, D], F32, pf_)
        fT = sb("fT", [P, DK, P], F32, pf_)
        fh = sb("fh", [P, MC], F32, pf_)
        fhT = sb("fhT", [P, MC // P, P], F32, pf_)
        fo = sb("fo", [P, 2, D], F32, pf_)
        f_ld, f_st = sems("f_ld", 2), sems("f_st", 2)
        f_tr, f_T, f_up, f_ge, f_w, f_th, f_hT, f_dn, f_o = (
            sem("f_" + n) for n in "tr T up ge w th hT dn o".split())

        with nc.Block() as block:
            @block.sync
            def _(sp):
                def body(g, s):
                    t = g * 2 + s
                    since(sp, f_o, t, 2)
                    sp.dma_start(f3[:, s, :], row(X3, t)).then_inc(f_ld[s], 16)
                    sp.dma_start(fn[:, s, :], row(XN3, t)).then_inc(f_ld[s], 16)
                    if warm(g, s, 1, 2):
                        store(g + (s - 1) // 2, 1 - s, t - 1)

                def store(g, s, t):
                    sp.wait_ge(f_o, t + 1)
                    n = TAIL if isinstance(t, int) and t == NT - 1 else P
                    sp.dma_start(row(out, t, n), fo[0:n, s, :]).then_inc(f_st[s], 16)

                stream(sp, NT, 2, body)
                store(NT // 2, 0, NT - 1)
                for s in range(2):
                    sp.wait_ge(f_st[s], 16 * ((NT + 1 - s) // 2))

            @block.tensor
            def _(pe):
                def body(g, s):
                    t = g * 2 + s
                    pe.wait_ge(f_ld[s], 32 * (g + 1))
                    since(pe, f_hT, t, 1)
                    tr4(bank[0], fn[:, s, :]).then_inc(f_tr, 1)
                    pe.wait_ge(f_T, t + 1)
                    since(pe, f_o, t, 1)
                    for c in range(4):
                        for k in range(DK):
                            last = nc.tensor.matmul(bank[4 + c], fT[:, k, :], m1[:, k, c * 512:(c + 1) * 512],
                                                    start=(k == 0), stop=(k == DK - 1))
                    last.then_inc(f_up, 1)
                    pe.wait_ge(f_w, t + 1)
                    for k in range(MC // P):
                        last = nc.tensor.transpose(bank[k // 4][:, k % 4 * P:(k % 4 + 1) * P],
                                                   fh[:, k * P:(k + 1) * P], ident[:])
                    last.then_inc(f_th, 1)
                    pe.wait_ge(f_hT, t + 1)
                    for k in range(MC // P):
                        last = nc.tensor.matmul(bank[4], fhT[:, k, :], m2[:, k, :], start=(k == 0),
                                                stop=(k == MC // P - 1))
                    last.then_inc(f_dn, 1)

                stream(pe, NT, 2, body)

            @block.scalar
            def _(act):
                def body(g, s):
                    t = g * 2 + s
                    act.wait_ge(f_tr, t + 1)
                    act.activation(fT[:].rearrange("p k n -> p (k n)"), bank[0], ACT.Copy).then_inc(f_T, 1)
                    act.wait_ge(f_up, t + 1)
                    for c in range(4):
                        last = act.activation(fh[:, c * 512:(c + 1) * 512], bank[4 + c], ACT.Gelu)
                    last.then_inc(f_ge, 1)
                    act.wait_ge(f_th, t + 1)
                    for c in range(4):
                        last = act.activation(fhT[:, 4 * c:4 * c + 4, :].rearrange("p k n -> p (k n)"), bank[c],
                                              ACT.Copy)
                    last.then_inc(f_hT, 1)

                stream(act, NT, 2, body)

            @block.vector
            def _(dve):
                def body(g, s):
                    t = g * 2 + s
                    dve.wait_ge(f_ge, t + 1)
                    v = fh[:].rearrange("p (e f) -> p e f", e=ME)
                    nc.vector.tensor_tensor(v, v, wts[:, bass.ds(t, 1), :].rearrange("p t e -> p (t e)")
                                            .unsqueeze(2).to_broadcast([P, ME, MF]), ALU.mult).then_inc(f_w, 1)
                    dve.wait_ge(f_dn, t + 1)
                    if not isinstance(t, int) or t >= 2:
                        dve.wait_ge(f_st[s], 16 * g)
                    nc.vector.tensor_tensor(fo[:, s, :], bank[4], f3[:, s, :], ALU.add).then_inc(f_o, 1)

                stream(dve, NT, 2, body)
        end_phase(pf_)


_INS = ["x", "src", "dst", "Wl", "Wr", "att", "gbias", "Wc0", "b1c", "W2e", "b2e", "WT", "bG", "hashp", "M1", "M2"]


def kernel(x, src, dst, L0_gnn_W_l, L0_gnn_W_r, L0_gnn_att, L0_gnn_bias, L0_ffn_Wr, L0_ffn_br, L0_ffn_W1, L0_ffn_b1,
           L0_ffn_W2, L0_ffn_b2, L1_gnn_W, L1_gnn_b, L1_ffn_hash_proj, L1_ffn_W1, L1_ffn_W2):
    import concourse.bacc as _bacc
    from concourse.bass_utils import run_bass_kernel_spmd as _run

    a = {k: np.asarray(v) for k, v in locals().items() if not k.startswith("_")}
    flat = {
        "x": a["x"], "src": a["src"], "dst": a["dst"], "Wl": a["L0_gnn_W_l"], "Wr": a["L0_gnn_W_r"],
        "att": a["L0_gnn_att"].reshape(D), "gbias": a["L0_gnn_bias"],
        "Wc0": np.concatenate([a["L0_ffn_W1"].transpose(1, 0, 2).reshape(D, FC), a["L0_ffn_Wr"]], axis=1),
        "b1c": np.concatenate([a["L0_ffn_b1"].reshape(FC), a["L0_ffn_br"]]),
        "W2e": a["L0_ffn_W2"].reshape(FC, D), "b2e": a["L0_ffn_b2"],
        "WT": a["L1_gnn_W"].T, "bG": a["L1_gnn_b"],
        "hashp": a["L1_ffn_hash_proj"].transpose(1, 0, 2).reshape(D, MH * ME),
        "M1": a["L1_ffn_W1"].transpose(1, 0, 2).reshape(D, MC), "M2": a["L1_ffn_W2"].reshape(MC, D),
    }
    nc = _bacc.Bacc("TRN2", target_bir_lowering=False, num_devices=1)
    arrays, aps = {}, []
    for name in _INS:
        v = np.ascontiguousarray(flat[name])
        arrays["in_" + name] = v
        aps.append(nc.dram_tensor("in_" + name, v.shape, mybir.dt.from_np(v.dtype), kind="ExternalInput").ap())
    out = nc.dram_tensor("out_0", (N, D), F32, kind="ExternalOutput").ap()
    gnn_ffn(nc, *aps, out)
    r = _run(nc, [arrays], core_ids=[0])
    return r.results[0]["out_0"]
```

```python
import numpy as np
from contextlib import ExitStack

import concourse.bass as bass
from concourse import mybir
from concourse.alu_op_type import AluOpType as ALU

ACT = mybir.ActivationFunctionType
F32 = mybir.dt.float32
BF16 = mybir.dt.bfloat16
I32 = mybir.dt.int32
U32 = mybir.dt.uint32
AX = mybir.AxisListType

P = 128
N, D = 10000, 512
E = 15000
H, C = 8, 64
DK = D // P
NT = -(-N // P)
NP = NT * P
TAIL = N - (NT - 1) * P
CE = C + 1
XE = H * CE
AW = XE + H
W = P - 1
ET = -(-E // W)
EP, EC = 120, E // 120
FL = EP * P
NE, FH = 8, 32
FC = NE * FH
ME, MH, MF = 64, 4, 32
MC = ME * MF
CAP = 4 * N * 2 // ME
SLOTS = -(-CAP // P)
LISTED = (2 * N + ME * (P - 1)) // P
DROPPED = 200000.0
SKIP = 20000.0
BIG = 1.0e30
EPS = 1e-5
SLOPE = 0.2


def stream(eng, n, ring, body, peel=1):
    for g in range(peel):
        for s in range(ring):
            body(g, s)
    with eng.Fori(peel, n // ring) as g:
        for s in range(ring):
            body(g, s)
    for s in range(n % ring):
        body(n // ring, s)


def warm(g, s, lag, ring):
    return not isinstance(g, int) or g * ring + s >= lag


def gnn_ffn(nc, x, src, dst, Wl, Wr, att, gbias, Wc0, b1c, W2e, b2e, WT, bG, hashp, M1, M2, out):
    ctx = ExitStack()
    with ctx:
        def sb(name, shape, dt=F32, on=None):
            return (on or ctx).enter_context(nc.sbuf_tensor(name, shape, dt))

        phase = []

        def sem(name):
            phase.append(nc.alloc_semaphore(name=name))
            return phase[-1]

        def end_phase(buffers):
            buffers.close()
            nc.clear_and_free_semaphores(phase)
            phase.clear()
            nc.all_engine_barrier()

        def sems(name, n):
            return [sem(f"{name}{i}") for i in range(n)]

        psum = ctx.enter_context(nc.psum_tensor("psum", [P, 8, 512], F32))
        bank = [psum[:, i, :] for i in range(8)]
        pair = [psum[:, 4 + 2 * i:6 + 2 * i, 0:XE // 2] for i in range(2)]

        XLE = nc.dram_tensor("xl_ext", [NP, XE], F32).ap()
        XR = nc.dram_tensor("xr_rows", [NP, D], F32).ap()
        AGG = nc.dram_tensor("edge_sums0", [NP, AW], F32).ap()
        X2 = nc.dram_tensor("x2_rows", [NP, D], F32).ap()
        GR = nc.dram_tensor("gcn_rows", [NP, D], F32).ap()
        AG2 = nc.dram_tensor("edge_sums1", [NP, D], F32).ap()
        FD = nc.dram_tensor("flat_dst", [FL], F32).ap()
        FS = nc.dram_tensor("flat_src", [FL], F32).ap()
        MDR = nc.dram_tensor("window_dst", [ET, P], F32).ap()
        RRR = nc.dram_tensor("window_resets", [ET, 2 * P], F32).ap()

        ident = sb("ident", [P, P])
        identb = sb("identb", [P, P], BF16)
        tri = sb("tri", [P, P], BF16)
        onesb = sb("onesb", [P, P], BF16)
        iota = sb("iota", [P, P])
        mhalf = sb("mhalf", [P, NT])
        epst = sb("epst", [P, 1])
        minus1 = sb("minus1", [P, 1])
        one = sb("one", [P, 1])
        att_b = sb("att_b", [P, D])
        gb_b = sb("gb_b", [P, D])
        wl = sb("wl", [P, DK, D])
        wr = sb("wr", [P, DK, D])
        wc = sb("wc", [P, DK, FC + NE])
        w2 = sb("w2", [P, FC // P, D])
        b1b = sb("b1b", [P, FC + NE])
        b2 = sb("b2", [NE, D])
        wg = sb("wg", [P, DK, D])
        bgb = sb("bgb", [P, D])
        hp = sb("hp", [P, DK, MH * ME])
        selfa = sb("selfa", [P, NT, H])
        xsc = sb("xsc", [P, NT, 2])
        dis = sb("dis", [P, NT])
        kd = sb("kd", [P, ET])
        idx = sb("idx", [P, 3, ET], I32)

        slot = sb("slot", [P, 4, 3], I32)
        held = sb("held", [P, 2, 4])

        def hold(pool, site, s, done, t):
            if not isinstance(t, int) or t >= 4:
                pool.wait_ge(done, t - 3)
            pool.tensor_tensor(held[:, site, s:s + 1], mhalf[:, 0:1], mhalf[:, 1:2], ALU.add).then_inc(done, 1)

        consts = sem("consts")
        loaded = sem("loaded")
        c_flat, c_int, c_f32, c_win, c_cmp, c_rows, c_tr, c_idx = (
            sem(n) for n in ("c_flat", "c_int", "c_f32", "c_win", "c_cmp", "c_rows", "c_tr", "c_idx"))
        h_oh, h_mm, h_deg, h_dis, h_init = (sem(n) for n in ("h_oh", "h_mm", "h_deg", "h_dis", "h_init"))

        prep = ExitStack()
        ei = sb("ei", [EP, 2, EC], I32, prep)
        ef = sb("ef", [EP, 2, EC], F32, prep)
        eh = sb("eh", [EP, 2, EC], I32, prep)
        ehf = sb("ehf", [EP, 2, EC], F32, prep)
        ohl = sb("ohl", [EP, 2, P], BF16, prep)
        ohh = sb("ohh", [EP, 2, NT], BF16, prep)
        padt = sb("padt", [EP, P], F32, prep)
        win = sb("win", [ET, 2, P + 2], F32, prep)
        ne = sb("ne", [ET, P], F32, prep)
        rr = sb("rr", [ET, 2, P], F32, prep)
        mdw = sb("mdw", [ET, P], F32, prep)
        wcol = sb("wcol", [ET, 3, P], F32, prep)
        deg1 = sb("deg1", [P, NT], F32, prep)
        zin = sb("zin", [P, AW], F32, prep)

        with nc.Block() as block:
            @block.sync
            def _(sp):
                sp.dma_start(ei[:, 0, :], dst.rearrange("(p c) -> p c", c=EC)).then_inc(c_int, 16)
                sp.dma_start(ei[:, 1, :], src.rearrange("(p c) -> p c", c=EC)).then_inc(c_int, 16)
                sp.wait_ge(consts, 6)
                sp.dma_start(FD.rearrange("(p c) -> p c", c=P), padt[:]).then_inc(c_flat, 16)
                sp.dma_start(FS.rearrange("(p c) -> p c", c=P), padt[:]).then_inc(c_flat, 16)
                sp.wait_ge(c_flat, 32)
                sp.wait_ge(c_f32, 1)
                sp.dma_start(FD[1:1 + E].rearrange("(p c) -> p c", c=EC), ef[:, 0, :]).then_inc(c_flat, 16)
                sp.dma_start(FS[1:1 + E].rearrange("(p c) -> p c", c=EC), ef[:, 1, :]).then_inc(c_flat, 16)
                sp.wait_ge(c_flat, 64)
                for k, f in enumerate((FD, FS)):
                    v = bass.AP(f.tensor, 0, [[W, ET], [1, P + 1]])
                    sp.dma_start(win[:, k, 0:P + 1], v).then_inc(c_win, 16)
                for t, s in ((wl, Wl), (wr, Wr), (wc, Wc0), (wg, WT), (hp, hashp), (w2, W2e)):
                    sp.dma_start(t[:], s.rearrange("(k p) n -> p k n", p=P)).then_inc(loaded, 16)
                for t, s in ((att_b, att), (gb_b, gbias), (b1b, b1c), (bgb, bG)):
                    sp.dma_start(t[:], s.partition_broadcast(P)).then_inc(loaded, 16)
                sp.dma_start(b2[:], b2e).then_inc(loaded, 16)
                sp.dma_start(AGG.rearrange("(t p) c -> p t c", p=P),
                             zin[:].unsqueeze(1).to_broadcast([P, NT, AW])).then_inc(h_init, 16)
                sp.dma_start(AG2.rearrange("(t p) c -> p t c", p=P),
                             zin[:, 0:D].unsqueeze(1).to_broadcast([P, NT, D])).then_inc(h_init, 16)
                sp.wait_ge(c_rows, 1)
                sp.dma_start(MDR, mdw[:]).then_inc(h_init, 16)
                sp.dma_start(RRR, rr[:].rearrange("t a p -> t (a p)")).then_inc(h_init, 16)
                sp.wait_ge(loaded, 11 * 16)
                sp.wait_ge(h_init, 4 * 16)

            @block.gpsimd
            def _(pool):
                pool.memset(padt[:], SKIP).then_inc(consts, 1)
                pool.memset(zin[:, 0:XE], 0.0).then_inc(consts, 1)
                pool.memset(zin[:, XE:AW], -BIG).then_inc(consts, 1)
                pool.memset(mhalf[:], -0.5)
                pool.memset(epst[:], EPS)
                pool.memset(one[:], 1.0)
                pool.memset(minus1[:], -1.0).then_inc(consts, 1)
                pool.memset(onesb[:], 1.0).then_inc(consts, 1)
                pool.iota(iota[:], [[1, P]], base=0, channel_multiplier=0,
                          allow_small_or_imprecise_dtypes=True).then_inc(consts, 1)
                pool.memset(ident[:], 0.0).then_inc(consts, 1)
                pool.memset(identb[:], 0.0).then_inc(consts, 1)
                pool.memset(tri[:], 1.0).then_inc(consts, 1)
                pool.wait_ge(consts, 9)
                for m in (ident, identb):
                    pool.affine_select(out=m[:], in_=m[:], compare_op=ALU.not_equal, fill=1.0, base=0,
                                       pattern=[[-1, P]], channel_multiplier=1).then_inc(consts, 1)
                pool.affine_select(out=tri[:], in_=tri[:], compare_op=ALU.is_gt, fill=0.0, base=0,
                                   pattern=[[1, P]], channel_multiplier=-1).then_inc(consts, 1)
                pool.wait_ge(h_deg, 1)
                pool.wait_ge(consts, 12)
                pool.tensor_tensor(dis[:], deg1[:], mhalf[:], ALU.pow).then_inc(h_dis, 1)
                pool.wait_ge(h_dis, 1)

            @block.vector
            def _(dve):
                dve.wait_ge(c_int, 32)
                nc.vector.tensor_copy(ef[:], ei[:]).then_inc(c_f32, 1)
                nc.vector.tensor_scalar(eh[:, 0, :], ei[:, 1, :], P - 1, None, ALU.bitwise_and).then_inc(c_f32, 1)
                nc.vector.tensor_scalar(eh[:, 1, :], ei[:, 1, :], 7, None,
                                        ALU.logical_shift_right).then_inc(c_f32, 1)
                dve.wait_ge(c_f32, 3)
                nc.vector.tensor_copy(ehf[:], eh[:]).then_inc(c_f32, 1)
                dve.wait_ge(c_f32, 4)
                dve.wait_ge(consts, 12)

                def onehots(g, s):
                    t = g * 2 + s
                    if warm(g, s, 2, 2):
                        dve.wait_ge(h_mm, t - 1)
                    nc.vector.tensor_scalar(ohl[:, s, :], iota[0:EP, :], ehf[:, 0, bass.ds(t, 1)], None,
                                            ALU.is_equal)
                    nc.vector.tensor_scalar(ohh[:, s, :], iota[0:EP, 0:NT], ehf[:, 1, bass.ds(t, 1)], None,
                                            ALU.is_equal).then_inc(h_oh, 1)

                stream(dve, EC, 2, onehots)
                dve.wait_ge(h_mm, EC)
                nc.vector.tensor_scalar_add(deg1[:], bank[0][:, 0:NT], 1.0).then_inc(h_deg, 1)

                dve.wait_ge(c_win, 32)
                nc.vector.memset(win[0:1, 0, 0:1], -1.0).then_inc(c_cmp, 1)
                nc.vector.memset(rr[:], -BIG).then_inc(c_cmp, 1)
                nc.vector.memset(wcol[:], SKIP).then_inc(c_cmp, 1)
                dve.wait_ge(c_cmp, 3)
                nc.vector.tensor_tensor(ne[:], win[:, 0, 1:P + 1], win[:, 0, 0:P], ALU.not_equal).then_inc(c_cmp, 1)
                dve.wait_ge(c_cmp, 4)
                nc.vector.tensor_scalar_mul(rr[:, 0, 1:P], ne[:, 0:P - 1], -BIG).then_inc(c_cmp, 1)
                nc.vector.tensor_scalar_mul(rr[:, 1, 0:P - 1], ne[:, 0:P - 1], -BIG).then_inc(c_cmp, 1)
                nc.vector.tensor_copy(mdw[:, 0:1], win[:, 0, W:P]).then_inc(c_cmp, 1)
                nc.vector.tensor_copy(mdw[:, 1:P], win[:, 0, 1:P]).then_inc(c_cmp, 1)
                nc.vector.tensor_copy(wcol[:, 0, 1:P], win[:, 1, 1:P]).then_inc(c_cmp, 1)
                nc.vector.tensor_copy(wcol[:, 1, 1:P], win[:, 0, 1:P]).then_inc(c_cmp, 1)
                nc.vector.scalar_tensor_tensor(wcol[:, 2, 1:P], win[:, 0, 1:P], -SKIP, ne[:, 1:P],
                                               ALU.add, ALU.mult).then_inc(c_cmp, 1)
                dve.wait_ge(c_cmp, 11)
                nc.vector.tensor_scalar_add(wcol[:, 2, 1:P], wcol[:, 2, 1:P], SKIP).then_inc(c_rows, 1)
                dve.wait_ge(c_tr, 1)
                nc.vector.tensor_copy(kd[:], bank[1][:, 0:ET]).then_inc(c_idx, 1)
                nc.vector.tensor_copy(idx[:], bank[2][:, 0:3 * ET].rearrange("p (a t) -> p a t", a=3))\
                    .then_inc(c_idx, 1)
                dve.wait_ge(c_idx, 2)

            @block.tensor
            def _(pe):
                def count(g, s):
                    t = g * 2 + s
                    pe.wait_ge(h_oh, t + 1)
                    first = isinstance(g, int) and t == 0
                    last = isinstance(g, int) and t == EC - 1
                    nc.tensor.matmul(bank[0][:, 0:NT], ohl[:, s, :], ohh[:, s, :], start=first, stop=last,
                                     skip_group_check=True).then_inc(h_mm, 1)

                stream(pe, EC, 2, count)
                pe.wait_ge(c_rows, 1)
                nc.tensor.transpose(bank[1][:, 0:ET], win[:, 0, 0:P], ident[0:ET, 0:ET])
                for a in range(3):
                    last = nc.tensor.transpose(bank[2][:, a * ET:(a + 1) * ET], wcol[:, a, :], ident[0:ET, 0:ET])
                last.then_inc(c_tr, 1)
        end_phase(prep)

        def mm4(ps, lhs, rhs):
            for k in range(DK):
                last = nc.tensor.matmul(ps, lhs[:, k, :], rhs[:, k, :], start=(k == 0), stop=(k == DK - 1))
            return last

        def tr4(ps, rows, n=DK):
            for k in range(n):
                last = nc.tensor.transpose(ps[:, k * P:(k + 1) * P], rows[:, k * P:(k + 1) * P], ident[:])
            return last

        pa = ExitStack()
        xa = sb("xa", [P, 2, D], F32, pa)
        st6 = sb("st6", [P, 2, 6], F32, pa)
        mv = sb("mv", [P, 2, 2], F32, pa)
        ve = sb("ve", [P, 2, 1], F32, pa)
        rs = sb("rs", [P, 2, 1], F32, pa)
        nm = sb("nm", [P, 2, 1], F32, pa)
        xn = sb("xn", [P, 2, D], F32, pa)
        xT = sb("xT", [P, 2, DK, P], F32, pa)
        xle = sb("xle", [P, 2, XE], F32, pa)
        xr = sb("xr", [P, 2, D], F32, pa)
        mm = sb("mm", [P, 2, D], F32, pa)
        la = sb("la", [P, 2, D], F32, pa)
        a_ld, a_st, a_sr = sems("a_ld", 2), sems("a_st", 2), sems("a_sr", 2)
        (a_bn, a_mv, a_ve, a_rs, a_nm, a_sc, a_norm, a_tr, a_xT, a_mm, a_xl, a_xr, a_m, a_lr, a_la, a_al, a_one) = (
            sem("a_" + n) for n in ("bn", "mv", "ve", "rs", "nm", "sc", "norm", "tr", "xT", "mm", "xl", "xr", "m",
                                    "lr", "la", "al", "one"))

        def heads(a, w=C):
            return a.rearrange("p (h c) -> p h c", h=H)[:, :, 0:w]

        def row(a, t, n=P):
            return a[bass.ds(t * P, n), :]

        with nc.Block() as block:
            @block.sync
            def _(sp):
                def body(g, s):
                    t = g * 2 + s
                    if warm(g, s, 2, 2):
                        sp.wait_ge(a_norm, t - 1)
                    n = TAIL if isinstance(g, int) and t == NT - 1 else P
                    sp.dma_start(xa[0:n, s, :], row(x, t, n)).then_inc(a_ld[s], 16)

                stream(sp, NT, 2, body)

            @block.gpsimd
            def _(pool):
                def body(g, s):
                    t = g * 2 + s
                    pool.wait_ge(a_mv, t + 1)
                    if warm(g, s, 2, 2):
                        pool.wait_ge(a_norm, t - 1)
                    pool.tensor_tensor(ve[:, s, :], mv[:, s, 1:2], epst[:], ALU.add).then_inc(a_ve, 1)
                    pool.wait_ge(a_ve, t + 1)
                    pool.tensor_tensor(rs[:, s, :], ve[:, s, :], mhalf[:, 0:1], ALU.pow).then_inc(a_rs, 1)
                    pool.wait_ge(a_rs, t + 1)
                    pool.tensor_tensor(nm[:, s, :], mv[:, s, 0:1], rs[:, s, :], ALU.mult).then_inc(a_nm, 1)
                    pool.wait_ge(a_nm, t + 1)
                    pool.tensor_tensor(nm[:, s, :], nm[:, s, :], minus1[:], ALU.mult).then_inc(a_sc, 1)
                    pool.wait_ge(a_sc, 2 * t + 1)
                    pool.tensor_copy(xsc[:, bass.ds(t, 1), 0], nm[:, s, :])
                    pool.tensor_tensor(xsc[:, bass.ds(t, 1), 1], rs[:, s, :], one[:], ALU.add).then_inc(a_sc, 1)
                    if warm(g, s, 1, 2):
                        att_mul(t - 1, 1 - s)

                def att_mul(t, s):
                    pool.wait_ge(a_lr, t + 1)
                    if not isinstance(t, int) or t >= 2:
                        pool.wait_ge(a_al, t - 1)
                    pool.tensor_tensor(la[:, s, :], mm[:, s, :], att_b[:], ALU.mult).then_inc(a_la, 1)

                stream(pool, NT, 2, body)
                att_mul(NT - 1, (NT - 1) % 2)
                pool.wait_ge(a_sc, 2 * NT)

            @block.vector
            def _(dve):
                def stats(g, s):
                    t = g * 2 + s
                    dve.wait_ge(a_ld[s], 16 * (g + 1))
                    nc.vector.bn_stats(st6[:, s, :], xa[:, s, :]).then_inc(a_bn, 1)
                    if warm(g, s, 2, 2):
                        dve.wait_ge(a_nm, t - 1)
                    if warm(g, s, 1, 2):
                        norm(t - 1, 1 - s, t)
                    else:
                        dve.wait_ge(a_bn, t + 1)
                    nc.vector.bn_aggr(mv[:, s, :], st6[:, s, :]).then_inc(a_mv, 1)

                def norm(t, s, stats_of=None):
                    dve.wait_ge(a_rs, t + 1)
                    if stats_of is not None:
                        dve.wait_ge(a_bn, stats_of + 1)
                    if not isinstance(t, int) or t >= 2:
                        dve.wait_ge(a_tr, t - 1)
                    nc.vector.tensor_scalar(xn[:, s, :], xa[:, s, :], mv[:, s, 0:1], rs[:, s, :],
                                            ALU.subtract, ALU.mult).then_inc(a_norm, 1)

                def add(t, s):
                    dve.wait_ge(a_mm, t + 1)
                    if not isinstance(t, int) or t >= 2:
                        dve.wait_ge(a_sr[s], 16 * ((t - s) // 2))
                        dve.wait_ge(a_la, t - 1)
                    nc.vector.tensor_copy(xr[:, s, :], bank[4 + s][:]).then_inc(a_xr, 1)
                    dve.wait_ge(a_xl, t + 1)
                    dve.wait_ge(a_xr, t + 1)
                    nc.vector.tensor_tensor(heads(mm[:, s, :]), heads(xle[:, s, :]), heads(xr[:, s, :]), ALU.add)\
                        .then_inc(a_m, 1)
                    dve.wait_ge(a_m, t + 1)
                    nc.vector.scalar_tensor_tensor(mm[:, s, :], mm[:, s, :], SLOPE, mm[:, s, :],
                                                   ALU.mult, ALU.max).then_inc(a_lr, 1)

                def logit(t, s):
                    dve.wait_ge(a_la, t + 1)
                    nc.vector.tensor_reduce(selfa[:, bass.ds(t, 1), :].rearrange("p t h -> p (t h)"),
                                            heads(la[:, s, :]), AX.X, ALU.add).then_inc(a_al, 1)

                def body(g, s):
                    t = g * 2 + s
                    stats(g, s)
                    if warm(g, s, 2, 2):
                        add(t - 2, s)
                    if isinstance(g, int) and t < 3:
                        return
                    logit(t - 3, 1 - s)

                for s in range(2):
                    body(0, s)
                for s in range(2):
                    body(1, s)
                with dve.Fori(2, NT // 2) as g:
                    for s in range(2):
                        body(g, s)
                body(NT // 2, 0)
                norm(NT - 1, 0)
                add(NT - 2, 1)
                logit(NT - 3, 0)
                add(NT - 1, 0)
                logit(NT - 2, 1)
                logit(NT - 1, 0)
                dve.wait_ge(a_al, NT)

            @block.tensor
            def _(pe):
                def project(t, s):
                    pe.wait_ge(a_xT, t + 1)
                    if not isinstance(t, int) or t >= 2:
                        pe.wait_ge(a_xl, t - 1)
                        pe.wait_ge(a_xr, t - 1)
                    mm4(bank[2 + s][:], xT[:, s, :, :], wl)
                    mm4(bank[4 + s][:], xT[:, s, :, :], wr).then_inc(a_mm, 1)

                def body(g, s):
                    t = g * 2 + s
                    pe.wait_ge(a_norm, t + 1)
                    if warm(g, s, 2, 2):
                        pe.wait_ge(a_xT, t - 1)
                    tr4(bank[s], xn[:, s, :]).then_inc(a_tr, 1)
                    if warm(g, s, 1, 2):
                        project(t - 1, 1 - s)

                stream(pe, NT, 2, body)
                project(NT - 1, (NT - 1) % 2)

            @block.scalar
            def _(act):
                act.activation(heads(xle[:, 0, :], CE)[:, :, C:CE], ident[:, 0:H].unsqueeze(2), ACT.Copy,
                               scale=0.0, bias=1.0).then_inc(a_one, 1)
                act.activation(heads(xle[:, 1, :], CE)[:, :, C:CE], ident[:, 0:H].unsqueeze(2), ACT.Copy,
                               scale=0.0, bias=1.0).then_inc(a_one, 1)

                def evac(t, s):
                    act.wait_ge(a_mm, t + 1)
                    if not isinstance(t, int) or t >= 2:
                        act.wait_ge(a_st[s], 16 * ((t - s) // 2))
                        act.wait_ge(a_m, t - 1)
                    act.activation(heads(xle[:, s, :]), heads(bank[2 + s][:]), ACT.Copy).then_inc(a_xl, 1)
                    act.wait_ge(a_xl, t + 1)
                    act.wait_ge(a_one, 2)
                    act.dma_start(row(XLE, t), xle[:, s, :]).then_inc(a_st[s], 16)
                    act.wait_ge(a_xr, t + 1)
                    act.dma_start(row(XR, t), xr[:, s, :]).then_inc(a_sr[s], 16)

                def body(g, s):
                    t = g * 2 + s
                    act.wait_ge(a_tr, t + 1)
                    if warm(g, s, 2, 2):
                        act.wait_ge(a_mm, t - 1)
                    act.activation(xT[:, s, :, :].rearrange("p k n -> p (k n)"), bank[s][:], ACT.Copy)\
                        .then_inc(a_xT, 1)
                    if warm(g, s, 1, 2):
                        evac(t - 1, 1 - s)

                stream(act, NT, 2, body)
                evac(NT - 1, (NT - 1) % 2)
                for s in range(2):
                    act.wait_ge(a_st[s], 16 * ((NT + 1 - s) // 2))
                    act.wait_ge(a_sr[s], 16 * ((NT + 1 - s) // 2))
        end_phase(pa)

        pb = ExitStack()
        gl = sb("gl", [P, 4, XE], F32, pb)
        gr = sb("gr", [P, 4, D], F32, pb)
        md = sb("md", [P, 4, P], F32, pb)
        rst = sb("rst", [H, 4, 2 * P], F32, pb)
        me = sb("me", [P, 2, D], F32, pb)
        al = sb("al", [P, 2, H], F32, pb)
        aT = sb("aT", [H, 2, P], F32, pb)
        pf = sb("pf", [H, 2, P], F32, pb)
        mx = sb("mx", [P, 2, P], F32, pb)
        dd = sb("dd", [H, 2, P], F32, pb)
        ea = sb("ea", [P, 2, P], F32, pb)
        sm = sb("sm", [P, 2, P], F32, pb)
        vv = sb("vv", [P, 2, XE], F32, pb)
        eo = sb("eo", [P, 4, AW], F32, pb)
        b_gl, b_gr, b_md, b_sc = sems("b_gl", 4), sems("b_gr", 4), sems("b_md", 4), sems("b_sc", 4)
        b_h0, b_h1 = sem("b_h0"), sem("b_h1")
        (b_0, b_ix, b_m, b_lr, b_la, b_al, b_at, b_ac, b_pf, b_mx, b_d, b_e, b_et, b_S, b_v, b_s, b_car, b_out) = (
            sem("b_" + n) for n in ("0", "ix", "m", "lr", "la", "al", "at", "ac", "pf", "mx", "d", "e", "et", "S",
                                    "v", "s", "car", "out"))

        def ago(g, s, lag):
            return g + (s - lag) // 4, (s - lag) % 4, g * 4 + s - lag

        with nc.Block() as block:
            @block.sync
            def _(sp):
                def body(g, s):
                    t = g * 4 + s
                    if warm(g, s, 4, 4):
                        sp.wait_ge(b_v, t - 3)
                    sp.dma_start(md[:, s, :], MDR[bass.ds(t, 1), :].to_broadcast([P, P])).then_inc(b_md[s], 16)
                    sp.dma_start(rst[:, s, :], RRR[bass.ds(t, 1), :].to_broadcast([H, 2 * P]))\
                        .then_inc(b_md[s], 16)

                stream(sp, ET, 4, body, 2)

            @block.gpsimd
            def _(pool):
                def scatter(g, s, t):
                    pool.wait_ge(b_out, t + 1)
                    hold(pool, 1, s, b_h1, t)
                    pool.indirect_dma_start(AGG, bass.IndirectOffsetOnAxis(slot[:, s, 2:3], 0), eo[:, s, :], None,
                                            bounds_check=NP - 1, oob_is_err=False).then_inc(b_sc[s], 16)

                def body(g, s):
                    t = g * 4 + s
                    if warm(g, s, 4, 4):
                        pool.wait_ge(b_sc[s], 16 * g)
                        pool.wait_ge(b_v, t - 3)
                    pool.tensor_copy(slot[:, s, :], idx[:, :, bass.ds(t, 1)].rearrange("p a t -> p (a t)"))\
                        .then_inc(b_ix, 1)
                    pool.wait_ge(b_ix, t + 1)
                    pool.wait_ge(b_0, 2)
                    hold(pool, 0, s, b_h0, t)
                    pool.indirect_dma_start(gl[:, s, :], None, XLE, bass.IndirectOffsetOnAxis(slot[:, s, 0:1], 0),
                                            bounds_check=NP - 1, oob_is_err=False).then_inc(b_gl[s], 16)
                    pool.indirect_dma_start(gr[:, s, :], None, XR, bass.IndirectOffsetOnAxis(slot[:, s, 1:2], 0),
                                            bounds_check=NP - 1, oob_is_err=False).then_inc(b_gr[s], 16)
                    if warm(g, s, 3, 4):
                        scatter(*ago(g, s, 3))

                stream(pool, ET, 4, body, 2)
                for t in range(ET - 3, ET):
                    scatter(*ago(0, t, 0))
                for s in range(4):
                    pool.wait_ge(b_sc[s], 16 * ((ET + 3 - s) // 4))

            @block.vector
            def _(dve):
                nc.vector.memset(gl[:], 0.0).then_inc(b_0, 1)
                nc.vector.memset(gr[:], 0.0).then_inc(b_0, 1)
                nc.vector.memset(mx[:], 0.0).then_inc(b_0, 1)
                nc.vector.memset(ea[:], 0.0).then_inc(b_0, 1)
                dve.wait_ge(b_0, 4)

                def logits(g, s, t):
                    h = s % 2
                    dve.wait_ge(b_gl[s], 16 * (g + 1))
                    dve.wait_ge(b_gr[s], 16 * (g + 1))
                    nc.vector.tensor_tensor(heads(me[:, h, :]), heads(gl[:, s, :]), heads(gr[:, s, :]), ALU.add)\
                        .then_inc(b_m, 1)
                    dve.wait_ge(b_m, t + 1)
                    nc.vector.scalar_tensor_tensor(me[:, h, :], me[:, h, :], SLOPE, me[:, h, :],
                                                   ALU.mult, ALU.max).then_inc(b_lr, 1)
                    dve.wait_ge(b_lr, t + 1)
                    nc.vector.tensor_tensor(me[:, h, :], me[:, h, :], att_b[:], ALU.mult).then_inc(b_la, 1)
                    dve.wait_ge(b_la, t + 1)
                    if not isinstance(t, int) or t >= 2:
                        dve.wait_ge(b_at, t - 1)
                    nc.vector.tensor_reduce(al[:, h, :], heads(me[:, h, :]), AX.X, ALU.add).then_inc(b_al, 1)

                def maxima(g, s, t):
                    h = s % 2
                    dve.wait_ge(b_at, t + 1)
                    if isinstance(t, int) and t == 0:
                        nc.vector.memset(aT[:, h, 0:1], 0.0)
                    else:
                        dve.wait_ge(b_mx, t)
                        nc.vector.tensor_copy(aT[:, h, 0:1], mx[0:H, 1 - h, P - 1:P])
                    nc.vector.tensor_copy(aT[:, h, 1:P], bank[h][0:H, 1:P]).then_inc(b_ac, 1)
                    dve.wait_ge(b_md[s], 32 * (g + 1))
                    dve.wait_ge(b_ac, t + 1)
                    nc.vector.tensor_tensor_scan(pf[:, h, :], rst[:, s, 0:P], aT[:, h, :], 0.0,
                                                 ALU.add, ALU.max).then_inc(b_pf, 1)
                    dve.wait_ge(b_pf, t + 1)
                    if not isinstance(t, int) or t >= 2:
                        dve.wait_ge(b_et, t - 1)
                    nc.vector.tensor_tensor_scan(mx[0:H, h, ::-1], rst[:, s, 2 * P - 1:P - 1:-1], pf[:, h, ::-1], 0.0,
                                                 ALU.add, ALU.max).then_inc(b_mx, 1)
                    dve.wait_ge(b_mx, t + 1)
                    if not isinstance(t, int) or t >= 2:
                        dve.wait_ge(b_e, t - 1)
                    nc.vector.tensor_tensor(dd[:, h, :], aT[:, h, :], mx[0:H, h, :], ALU.subtract).then_inc(b_d, 1)

                def weigh(g, s, t):
                    h = s % 2
                    if not isinstance(t, int) or t >= 2:
                        dve.wait_ge(b_s, t - 1)
                    nc.vector.tensor_scalar(sm[:, h, :], md[:, s, :], kd[:, bass.ds(t, 1)], None,
                                            ALU.is_equal).then_inc(b_S, 1)
                    dve.wait_ge(b_et, t + 1)
                    if not isinstance(t, int) or t >= 1:
                        dve.wait_ge(b_car, t)
                    nc.vector.tensor_tensor(heads(vv[:, h, :], CE), heads(gl[:, s, :], CE),
                                            bank[2 + h][:, 0:H].unsqueeze(2).to_broadcast([P, H, CE]),
                                            ALU.mult).then_inc(b_v, 1)

                def body(g, s):
                    logits(*ago(g, s, 0))
                    if warm(g, s, 1, 4):
                        maxima(*ago(g, s, 1))
                    if warm(g, s, 2, 4):
                        weigh(*ago(g, s, 2))

                stream(dve, ET, 4, body, 2)
                maxima(*ago(0, ET, 1))
                weigh(*ago(0, ET, 2))
                weigh(*ago(0, ET, 1))

            @block.tensor
            def _(pe):
                def alphas(g, s, t):
                    h = s % 2
                    pe.wait_ge(b_al, t + 1)
                    if not isinstance(t, int) or t >= 2:
                        pe.wait_ge(b_ac, t - 1)
                    nc.tensor.transpose(bank[h][0:H, 0:P], al[:, h, :], ident[:]).then_inc(b_at, 1)

                def weights(g, s, t):
                    h = s % 2
                    pe.wait_ge(b_e, t + 1)
                    if not isinstance(t, int) or t >= 2:
                        pe.wait_ge(b_out, t - 1)
                    nc.tensor.transpose(bank[2 + h][:, 0:P], ea[:, h, :], ident[:])
                    nc.tensor.transpose(bank[2 + h][:, P:2 * P], mx[:, h, :], ident[:]).then_inc(b_et, 1)

                def sums(g, s, t):
                    h = s % 2
                    pe.wait_ge(b_S, t + 1)
                    pe.wait_ge(b_v, t + 1)
                    for a in range(2):
                        last = nc.tensor.matmul(pair[h][:, a, :], sm[:, h, :], vv[:, h, a * XE // 2:(a + 1) * XE // 2],
                                                start=True, stop=True)
                    last.then_inc(b_s, 1)

                def body(g, s):
                    alphas(*ago(g, s, 0))
                    if warm(g, s, 1, 4):
                        weights(*ago(g, s, 1))
                    if warm(g, s, 2, 4):
                        sums(*ago(g, s, 2))

                stream(pe, ET, 4, body, 2)
                weights(*ago(0, ET, 1))
                sums(*ago(0, ET, 2))
                sums(*ago(0, ET, 1))

            @block.scalar
            def _(act):
                act.wait_ge(b_0, 4)

                def expo(g, s, t):
                    h = s % 2
                    act.wait_ge(b_d, t + 1)
                    if not isinstance(t, int) or t >= 2:
                        act.wait_ge(b_et, t - 1)
                    act.activation(ea[0:H, h, :], dd[:, h, :], ACT.Exp).then_inc(b_e, 1)

                def results(g, s, t, last=False):
                    h = s % 2
                    act.wait_ge(b_s, t + 1)
                    if not last:
                        act.wait_ge(b_m, t + 2)
                        act.activation(gl[0:1, (s + 1) % 4, :].rearrange("p (a c) -> p a c", a=2),
                                       pair[h][0:1, :, :], ACT.Copy).then_inc(b_car, 1)
                    if not isinstance(t, int) or t >= 4:
                        act.wait_ge(b_sc[s], 16 * g)
                    act.activation(eo[:, s, 0:XE].rearrange("p (a c) -> p a c", a=2), pair[h], ACT.Copy)
                    act.activation(eo[:, s, XE:AW], bank[2 + h][:, P:P + H], ACT.Copy).then_inc(b_out, 1)

                def body(g, s):
                    if warm(g, s, 1, 4):
                        expo(*ago(g, s, 1))
                    if warm(g, s, 2, 4):
                        results(*ago(g, s, 2))

                stream(act, ET, 4, body, 2)
                expo(*ago(0, ET, 1))
                results(*ago(0, ET, 2))
                results(*ago(0, ET, 1), last=True)
        end_phase(pb)

        pc = ExitStack()
        xi = sb("xi", [P, 4, D], F32, pc)
        ai = sb("ai", [P, 4, AW], F32, pc)
        li = sb("li", [P, 4, XE], F32, pc)
        mxn = sb("mxn", [P, 2, H], F32, pc)
        df = sb("df", [P, 2, 2, H], F32, pc)
        fe = sb("fe", [P, 2, 2, H], F32, pc)
        rd = sb("rd", [P, 2, H], F32, pc)
        oc = sb("oc", [P, 2, D], F32, pc)
        mi = sb("mi", [P, 2, D], F32, pc)
        xx = sb("xx", [P, 4, D], F32, pc)
        x1 = sb("x1", [P, 4, D], F32, pc)
        cst = sb("cst", [P, 2, 6], F32, pc)
        cmv = sb("cmv", [P, 2, 2], F32, pc)
        cve = sb("cve", [P, 2, 1], F32, pc)
        crs = sb("crs", [P, 2, 1], F32, pc)
        n1 = sb("n1", [P, 2, D], F32, pc)
        n1T = sb("n1T", [P, 2, DK, P], F32, pc)
        hb = sb("hb", [P, 2, FC + NE], F32, pc)
        m8 = sb("m8", [P, 2, 8], F32, pc)
        i8 = sb("i8", [P, 2, 8], U32, pc)
        ix = sb("ix", [P, 2, 1], F32, pc)
        hm = sb("hm", [P, 2, FC + NE], F32, pc)
        hT = sb("hT", [P, 2, 3, P], F32, pc)
        x2 = sb("x2", [P, 4, D], F32, pc)
        st2 = sb("st2", [P, 2, 6], F32, pc)
        mv2 = sb("mv2", [P, 2, 2], F32, pc)
        ve2 = sb("ve2", [P, 2, 1], F32, pc)
        rs2 = sb("rs2", [P, 2, 1], F32, pc)
        n2 = sb("n2", [P, 2, D], F32, pc)
        n2T = sb("n2T", [P, 2, DK, P], F32, pc)
        gb = sb("gb", [P, 2, D], F32, pc)
        gs = sb("gs", [P, 4, D], F32, pc)
        c_hold = sb("c_hold", [P, 4, 2], F32, pc)
        c_ld, c_sx, c_sg = sems("c_ld", 4), sems("c_sx", 4), sems("c_sg", 4)
        (c_mn, c_df, c_f, c_t1, c_t2, c_s, c_den, c_rd, c_o, c_ob, c_mi, c_ex, c_xx, c_r, c_x1, c_bn, c_mv, c_ve, c_rs,
         c_n1, c_tr1, c_n1T, c_up, c_hb, c_m8, c_i8, c_ix, c_oh, c_hm, c_trh, c_hT, c_dn, c_x2, c_bn2, c_mv2, c_ve2,
         c_rs2, c_n2, c_tr2, c_n2T, c_g, c_gb, c_gs, c_hd1, c_hd2) = (
            sem("c_" + n) for n in ("mn df f t1 t2 s den rd o ob mi ex xx r x1 bn mv ve rs n1 tr1 n1T up hb m8 i8 ix "
                                    "oh hm trh hT dn x2 bn2 mv2 ve2 rs2 n2 tr2 n2T g gb gs hd1 hd2").split())

        def since(eng, done, t, lag):
            if not isinstance(t, int) or t >= lag:
                eng.wait_ge(done, t - lag + 1)

        with nc.Block() as block:
            @block.sync
            def _(sp):
                def store_x2(g, s, t):
                    sp.wait_ge(c_x2, t + 1)
                    sp.dma_start(row(X2, t), x2[:, s, :]).then_inc(c_sx[s], 16)

                def store_g(g, s, t):
                    sp.wait_ge(c_gs, t + 1)
                    sp.dma_start(row(GR, t), gs[:, s, :]).then_inc(c_sg[s], 16)

                def body(g, s):
                    t = g * 4 + s
                    since(sp, c_xx, t, 4)
                    since(sp, c_o, t, 4)
                    n = TAIL if isinstance(g, int) and t == NT - 1 else P
                    sp.dma_start(xi[0:n, s, :], row(x, t, n)).then_inc(c_ld[s], 16)
                    sp.dma_start(ai[:, s, :], row(AGG, t)).then_inc(c_ld[s], 16)
                    sp.dma_start(li[:, s, :], row(XLE, t)).then_inc(c_ld[s], 16)
                    if warm(g, s, 7, 4):
                        store_x2(*ago(g, s, 7))
                    if warm(g, s, 9, 4):
                        store_g(*ago(g, s, 9))

                stream(sp, NT, 4, body, 3)
                for t in range(NT, NT + 9):
                    if t - 7 < NT:
                        store_x2(*ago(0, t, 7))
                    store_g(*ago(0, t, 9))
                for s in range(4):
                    sp.wait_ge(c_sx[s], 16 * ((NT + 3 - s) // 4))
                    sp.wait_ge(c_sg[s], 16 * ((NT + 3 - s) // 4))

            @block.gpsimd
            def _(pool):
                def self_part(g, s, t):
                    h = s % 2
                    pool.wait_ge(c_ld[s], 48 * (g + 1))
                    pool.wait_ge(c_f, t + 1)
                    pool.tensor_tensor(heads(li[:, s, :], CE), heads(li[:, s, :], CE),
                                       fe[:, h, 1, :].unsqueeze(2).to_broadcast([P, H, CE]), ALU.mult)\
                        .then_inc(c_t2, 1)

                def root(t, h, mv_, ve_, rs_, d_mv, d_ve, d_rs, d_n):
                    pool.wait_ge(d_mv, t + 1)
                    pool.tensor_tensor(ve_[:, h, :], mv_[:, h, 1:2], epst[:], ALU.add).then_inc(d_ve, 1)
                    since(pool, d_n, t, 2)
                    pool.wait_ge(d_ve, t + 1)
                    pool.tensor_tensor(rs_[:, h, :], ve_[:, h, :], mhalf[:, 0:1], ALU.pow).then_inc(d_rs, 1)

                def body(g, s):
                    self_part(*ago(g, s, 0))
                    if warm(g, s, 5, 4):
                        root(g * 4 + s - 5, (s + 1) % 2, mv2, ve2, rs2, c_mv2, c_ve2, c_rs2, c_n2)
                    if warm(g, s, 2, 4):
                        root(g * 4 + s - 2, s % 2, cmv, cve, crs, c_mv, c_ve, c_rs, c_n1)

                stream(pool, NT, 4, body, 2)
                for t in range(NT, NT + 5):
                    root(t - 5, (t - 5) % 2, mv2, ve2, rs2, c_mv2, c_ve2, c_rs2, c_n2)
                    if t - 2 < NT:
                        root(t - 2, t % 2, cmv, cve, crs, c_mv, c_ve, c_rs, c_n1)

            @block.vector
            def _(dve):
                def shifts(g, s, t):
                    h = s % 2
                    dve.wait_ge(c_ld[s], 48 * (g + 1))
                    own = selfa[:, bass.ds(t, 1), :].rearrange("p t h -> p (t h)")
                    nc.vector.tensor_tensor(mxn[:, h, :], ai[:, s, XE:AW], own, ALU.max).then_inc(c_mn, 1)
                    since(dve, c_f, t, 2)
                    dve.wait_ge(c_mn, t + 1)
                    nc.vector.tensor_tensor(df[:, h, 0, :], ai[:, s, XE:AW], mxn[:, h, :], ALU.subtract)
                    nc.vector.tensor_tensor(df[:, h, 1, :], own, mxn[:, h, :], ALU.subtract).then_inc(c_df, 1)

                def average(g, s, t):
                    h = s % 2
                    dve.wait_ge(c_f, t + 1)
                    nc.vector.tensor_tensor(heads(ai[:, s, 0:XE], CE), heads(ai[:, s, 0:XE], CE),
                                            fe[:, h, 0, :].unsqueeze(2).to_broadcast([P, H, CE]), ALU.mult)\
                        .then_inc(c_t1, 1)
                    dve.wait_ge(c_t1, t + 1)
                    dve.wait_ge(c_t2, t + 1)
                    nc.vector.tensor_tensor(ai[:, s, 0:XE], ai[:, s, 0:XE], li[:, s, :], ALU.add).then_inc(c_s, 1)
                    dve.wait_ge(c_s, t + 1)
                    nc.vector.tensor_scalar_max(rd[:, h, :], heads(ai[:, s, 0:XE], CE)[:, :, C:CE].rearrange(
                        "p h c -> p (h c)"), 1e-16).then_inc(c_den, 1)
                    dve.wait_ge(c_den, t + 1)
                    nc.vector.reciprocal(rd[:, h, :], rd[:, h, :]).then_inc(c_rd, 1)
                    dve.wait_ge(c_rd, t + 1)
                    nc.vector.tensor_tensor(heads(oc[:, h, :]), heads(ai[:, s, 0:XE], CE)[:, :, 0:C],
                                            rd[:, h, :].unsqueeze(2).to_broadcast([P, H, C]), ALU.mult)\
                        .then_inc(c_o, 1)
                    dve.wait_ge(c_o, t + 1)
                    nc.vector.tensor_tensor(oc[:, h, :], oc[:, h, :], gb_b[:], ALU.add).then_inc(c_ob, 1)
                    dve.wait_ge(c_ob, t + 1)
                    nc.vector.tensor_scalar_min(mi[:, h, :], oc[:, h, :], 0.0).then_inc(c_mi, 1)

                def elu(g, s, t):
                    h = s % 2
                    dve.wait_ge(c_ex, t + 1)
                    nc.vector.scalar_tensor_tensor(mi[:, h, :], oc[:, h, :], 0.0, mi[:, h, :],
                                                   ALU.max, ALU.add).then_inc(c_r, 1)
                    dve.wait_ge(c_xx, t + 1)
                    dve.wait_ge(c_r, t + 1)
                    nc.vector.scalar_tensor_tensor(x1[:, s, :], mi[:, h, :], -1.0, xx[:, s, :],
                                                   ALU.add, ALU.add).then_inc(c_x1, 1)
                    dve.wait_ge(c_x1, t + 1)
                    nc.vector.bn_stats(cst[:, h, :], x1[:, s, :]).then_inc(c_bn, 1)
                    dve.wait_ge(c_bn, t + 1)
                    nc.vector.memset(c_hold[:, s, 0:1], 0.0)
                    nc.vector.bn_aggr(cmv[:, h, :], cst[:, h, :]).then_inc(c_mv, 1)

                def norm1(g, s, t):
                    h = s % 2
                    dve.wait_ge(c_rs, t + 1)
                    since(dve, c_tr1, t, 2)
                    nc.vector.tensor_scalar(n1[:, h, :], x1[:, s, :], cmv[:, h, 0:1], crs[:, h, :],
                                            ALU.subtract, ALU.mult).then_inc(c_n1, 1)

                def route(g, s, t):
                    h = s % 2
                    dve.wait_ge(c_up, t + 1)
                    nc.vector.tensor_tensor(hb[:, h, :], bank[1][:, 0:FC + NE], b1b[:], ALU.add).then_inc(c_hb, 1)
                    dve.wait_ge(c_hb, t + 1)
                    nc.vector.memset(c_hold[:, s, 1:2], 0.0)
                    nc.vector.max(m8[:, h, :], hb[:, h, FC:FC + NE]).then_inc(c_m8, 1)
                    dve.wait_ge(c_m8, t + 1)
                    nc.vector.memset(c_hold[:, s, 1:2], 0.0)
                    nc.vector.max_index(i8[:, h, :], m8[:, h, :], hb[:, h, FC:FC + NE]).then_inc(c_i8, 1)
                    dve.wait_ge(c_i8, t + 1)
                    nc.vector.tensor_copy(ix[:, h, :], i8[:, h, 0:1]).then_inc(c_ix, 1)
                    since(dve, c_trh, t, 2)
                    dve.wait_ge(c_ix, t + 1)
                    nc.vector.tensor_scalar(hm[:, h, FC:FC + NE], iota[:, 0:NE], ix[:, h, :], None,
                                            ALU.is_equal).then_inc(c_oh, 1)
                    dve.wait_ge(c_oh, t + 1)
                    nc.vector.scalar_tensor_tensor(
                        hm[:, h, 0:FC].rearrange("p (e f) -> p e f", e=NE),
                        hb[:, h, 0:FC].rearrange("p (e f) -> p e f", e=NE), 0.0,
                        hm[:, h, FC:FC + NE].unsqueeze(2).to_broadcast([P, NE, FH]), ALU.max, ALU.mult)\
                        .then_inc(c_hm, 1)

                def add_experts(g, s, t):
                    h = s % 2
                    if not isinstance(t, int) or t >= 4:
                        dve.wait_ge(c_sx[s], 16 * g)
                    dve.wait_ge(c_dn, t + 1)
                    nc.vector.tensor_tensor(x2[:, s, :], bank[3], x1[:, s, :], ALU.add).then_inc(c_x2, 1)
                    dve.wait_ge(c_x2, t + 1)
                    nc.vector.bn_stats(st2[:, h, :], x2[:, s, :]).then_inc(c_bn2, 1)
                    dve.wait_ge(c_bn2, t + 1)
                    nc.vector.memset(c_hold[:, s, 0:1], 0.0)
                    nc.vector.bn_aggr(mv2[:, h, :], st2[:, h, :]).then_inc(c_mv2, 1)

                def norm2(g, s, t):
                    h = s % 2
                    dve.wait_ge(c_rs2, t + 1)
                    since(dve, c_tr2, t, 2)
                    nc.vector.tensor_scalar(n2[:, h, :], x2[:, s, :], mv2[:, h, 0:1], rs2[:, h, :],
                                            ALU.subtract, ALU.mult).then_inc(c_n2, 1)

                def gcn_bias(g, s, t):
                    h = s % 2
                    dve.wait_ge(c_g, t + 1)
                    since(dve, c_gs, t, 2)
                    nc.vector.tensor_tensor(gb[:, h, :], bank[5], bgb[:], ALU.add).then_inc(c_gb, 1)

                steps = ((7, gcn_bias), (6, norm2), (5, add_experts), (4, route), (3, norm1), (2, elu), (1, average))

                def body(g, s):
                    for lag, step in steps:
                        if warm(g, s, lag, 4):
                            step(*ago(g, s, lag))
                    shifts(*ago(g, s, 0))

                stream(dve, NT, 4, body, 2)
                for t in range(NT, NT + 7):
                    for lag, step in steps:
                        if t - lag < NT:
                            step(*ago(0, t, lag))

            @block.tensor
            def _(pe):
                def up(g, s, t):
                    pe.wait_ge(c_n1T, t + 1)
                    since(pe, c_hb, t, 1)
                    mm4(bank[1][:, 0:FC + NE], n1T[:, s % 2, :, :], wc).then_inc(c_up, 1)

                def down(g, s, t):
                    h = s % 2
                    pe.wait_ge(c_hT, t + 1)
                    since(pe, c_x2, t, 1)
                    for k in range(FC // P):
                        nc.tensor.matmul(bank[3], hT[:, h, k, :], w2[:, k, :], start=(k == 0), stop=False)
                    nc.tensor.matmul(bank[3], hT[0:NE, h, 2, :], b2[:], start=False, stop=True).then_inc(c_dn, 1)

                def gcn(g, s, t):
                    pe.wait_ge(c_n2T, t + 1)
                    since(pe, c_gb, t, 1)
                    mm4(bank[5], n2T[:, s % 2, :, :], wg).then_inc(c_g, 1)

                def turn2(g, s, t):
                    pe.wait_ge(c_n2, t + 1)
                    since(pe, c_n2T, t, 1)
                    tr4(bank[4], n2[:, s % 2, :]).then_inc(c_tr2, 1)

                def turn_h(g, s, t):
                    h = s % 2
                    pe.wait_ge(c_hm, t + 1)
                    since(pe, c_hT, t, 1)
                    tr4(bank[2], hm[:, h, :], FC // P)
                    nc.tensor.transpose(bank[2][0:NE, FC:FC + P], hm[:, h, FC:FC + NE], ident[:]).then_inc(c_trh, 1)

                def turn1(g, s, t):
                    pe.wait_ge(c_n1, t + 1)
                    since(pe, c_n1T, t, 1)
                    tr4(bank[0], n1[:, s % 2, :]).then_inc(c_tr1, 1)

                steps = ((7, gcn), (5, down), (4, up), (6, turn2), (4, turn_h), (3, turn1))

                def body(g, s):
                    for lag, step in steps:
                        if warm(g, s, lag, 4):
                            step(*ago(g, s, lag))

                stream(pe, NT, 4, body, 2)
                for t in range(NT, NT + 7):
                    for lag, step in steps:
                        if t - lag < NT:
                            step(*ago(0, t, lag))

            @block.scalar
            def _(act):
                def scaled(g, s, t):
                    act.wait_ge(c_gb, t + 1)
                    if not isinstance(t, int) or t >= 4:
                        act.wait_ge(c_sg[s], 16 * g)
                    act.activation(gs[:, s, :], gb[:, s % 2, :], ACT.Copy, scale=dis[:, bass.ds(t, 1)])\
                        .then_inc(c_gs, 1)

                def copy2(g, s, t):
                    act.wait_ge(c_tr2, t + 1)
                    since(act, c_g, t, 2)
                    act.activation(n2T[:, s % 2, :, :].rearrange("p k n -> p (k n)"), bank[4], ACT.Copy)\
                        .then_inc(c_n2T, 1)

                def copy_h(g, s, t):
                    h = s % 2
                    act.wait_ge(c_trh, t + 1)
                    since(act, c_dn, t, 2)
                    act.activation(hT[:, h, 0:2, :].rearrange("p k n -> p (k n)"), bank[2][:, 0:FC], ACT.Copy)
                    act.activation(hT[0:NE, h, 2, :], bank[2][0:NE, FC:FC + P], ACT.Copy).then_inc(c_hT, 1)

                def copy1(g, s, t):
                    act.wait_ge(c_tr1, t + 1)
                    since(act, c_up, t, 2)
                    act.activation(n1T[:, s % 2, :, :].rearrange("p k n -> p (k n)"), bank[0], ACT.Copy)\
                        .then_inc(c_n1T, 1)

                def exp_min(g, s, t):
                    act.wait_ge(c_mi, t + 1)
                    act.activation(mi[:, s % 2, :], mi[:, s % 2, :], ACT.Exp).then_inc(c_ex, 1)

                def exp_shift(g, s, t):
                    h = s % 2
                    act.wait_ge(c_ld[s], 48 * (g + 1))
                    since(act, c_x1, t, 4)
                    act.activation(xx[:, s, :], xi[:, s, :], ACT.Identity, scale=xsc[:, bass.ds(t, 1), 1],
                                   bias=xsc[:, bass.ds(t, 1), 0]).then_inc(c_xx, 1)
                    act.wait_ge(c_df, t + 1)
                    since(act, c_t1, t, 2)
                    since(act, c_t2, t, 2)
                    act.activation(fe[:, h, :, :], df[:, h, :, :], ACT.Exp).then_inc(c_f, 1)

                steps = ((7, scaled), (6, copy2), (4, copy_h), (3, copy1), (1, exp_min))

                def body(g, s):
                    for lag, step in steps:
                        if warm(g, s, lag, 4):
                            step(*ago(g, s, lag))
                    exp_shift(*ago(g, s, 0))

                stream(act, NT, 4, body, 2)
                for t in range(NT, NT + 7):
                    for lag, step in steps:
                        if t - lag < NT:
                            step(*ago(0, t, lag))
        end_phase(pc)

        pd = ExitStack()
        gg = sb("gg", [P, 4, D], F32, pd)
        md2 = sb("md2", [P, 4, P], F32, pd)
        sm2 = sb("sm2", [P, 2, P], F32, pd)
        go = sb("go", [P, 4, D], F32, pd)
        d_ld, d_md, d_sc = sems("d_ld", 4), sems("d_md", 4), sems("d_sc", 4)
        d_0, d_ix, d_S, d_s, d_car, d_out, d_h0, d_h1 = (
            sem("d_" + n) for n in ("0", "ix", "S", "s", "car", "out", "h0", "h1"))

        with nc.Block() as block:
            @block.sync
            def _(sp):
                def body(g, s):
                    t = g * 4 + s
                    since(sp, d_S, t, 4)
                    sp.dma_start(md2[:, s, :], MDR[bass.ds(t, 1), :].to_broadcast([P, P])).then_inc(d_md[s], 16)

                stream(sp, ET, 4, body)

            @block.gpsimd
            def _(pool):
                def scatter(g, s, t):
                    pool.wait_ge(d_out, t + 1)
                    hold(pool, 1, s, d_h1, t)
                    pool.indirect_dma_start(AG2, bass.IndirectOffsetOnAxis(slot[:, s, 2:3], 0), go[:, s, :], None,
                                            bounds_check=NP - 1, oob_is_err=False).then_inc(d_sc[s], 16)

                def body(g, s):
                    t = g * 4 + s
                    if warm(g, s, 4, 4):
                        pool.wait_ge(d_sc[s], 16 * g)
                        pool.wait_ge(d_s, t - 3)
                    pool.tensor_copy(slot[:, s, :], idx[:, :, bass.ds(t, 1)].rearrange("p a t -> p (a t)"))\
                        .then_inc(d_ix, 1)
                    pool.wait_ge(d_ix, t + 1)
                    pool.wait_ge(d_0, 1)
                    hold(pool, 0, s, d_h0, t)
                    pool.indirect_dma_start(gg[:, s, :], None, GR, bass.IndirectOffsetOnAxis(slot[:, s, 0:1], 0),
                                            bounds_check=NP - 1, oob_is_err=False).then_inc(d_ld[s], 16)
                    if warm(g, s, 3, 4):
                        scatter(*ago(g, s, 3))

                stream(pool, ET, 4, body, 2)
                for t in range(ET - 3, ET):
                    scatter(*ago(0, t, 0))
                for s in range(4):
                    pool.wait_ge(d_sc[s], 16 * ((ET + 3 - s) // 4))

            @block.vector
            def _(dve):
                nc.vector.memset(gg[:], 0.0).then_inc(d_0, 1)

                def results(g, s, t):
                    dve.wait_ge(d_s, t + 1)
                    if not isinstance(t, int) or t < ET - 1:
                        dve.wait_ge(d_car, t + 1)
                    if not isinstance(t, int) or t >= 4:
                        dve.wait_ge(d_sc[s], 16 * g)
                    nc.vector.tensor_copy(go[:, s, :], bank[s % 2]).then_inc(d_out, 1)

                def body(g, s):
                    t = g * 4 + s
                    dve.wait_ge(d_md[s], 16 * (g + 1))
                    since(dve, d_s, t, 2)
                    nc.vector.tensor_scalar(sm2[:, s % 2, :], md2[:, s, :], kd[:, bass.ds(t, 1)], None,
                                            ALU.is_equal).then_inc(d_S, 1)
                    if warm(g, s, 1, 4):
                        results(*ago(g, s, 1))

                stream(dve, ET, 4, body, 2)
                results(*ago(0, ET, 1))

            @block.tensor
            def _(pe):
                def body(g, s):
                    t = g * 4 + s
                    pe.wait_ge(d_S, t + 1)
                    pe.wait_ge(d_ld[s], 16 * (g + 1))
                    since(pe, d_car, t, 1)
                    since(pe, d_out, t, 2)
                    nc.tensor.matmul(bank[s % 2], sm2[:, s % 2, :], gg[:, s, :], start=True, stop=True)\
                        .then_inc(d_s, 1)

                stream(pe, ET, 4, body)

            @block.scalar
            def _(act):
                def body(g, s):
                    t = g * 4 + s
                    if isinstance(g, int) and t == ET - 1:
                        return
                    act.wait_ge(d_s, t + 1)
                    n = s + 1
                    act.wait_ge(d_ld[n % 4], 16 * (g + 1 + n // 4))
                    act.activation(gg[0:1, n % 4, :], bank[s % 2][0:1, :], ACT.Copy).then_inc(d_car, 1)

                stream(act, ET, 4, body)
        end_phase(pd)

        X3 = nc.dram_tensor("x3_rows", [NP, D], F32).ap()
        XN3 = nc.dram_tensor("n3_rows", [NP, D], F32).ap()
        IDX = nc.dram_tensor("slot_tokens", [(ME * SLOTS + LISTED), P], I32).ap()
        IDXF = IDX.rearrange("r (p o) -> (r p) o", o=1)
        w12 = sb("w12", [P, NT, 2])
        sl3 = sb("sl3", [P, 3, NT], I32)
        mask = sb("mask", [P, 1])
        prow = sb("prow", [P, 1])
        cnt = sb("cnt", [P, ME])
        cbase = sb("cbase", [P, ME])
        selk = sb("selk", [P, NT, 2])
        plk = sb("plk", [P, NT, 2])
        pe_ = ExitStack()
        ex2 = sb("ex2", [P, 4, D], F32, pe_)
        eg = sb("eg", [P, 4, D], F32, pe_)
        ea2 = sb("ea2", [P, 4, D], F32, pe_)
        er = sb("er", [P, 2, D], F32, pe_)
        x3 = sb("x3", [P, 4, D], F32, pe_)
        est = sb("est", [P, 2, 6], F32, pe_)
        emv = sb("emv", [P, 2, 2], F32, pe_)
        eve = sb("eve", [P, 2, 1], F32, pe_)
        ers = sb("ers", [P, 2, 1], F32, pe_)
        n3 = sb("n3", [P, 4, D], F32, pe_)
        n3T = sb("n3T", [P, 2, DK, P], F32, pe_)
        lg = sb("lg", [P, 2, MH * ME], F32, pe_)
        hm8 = sb("hm8", [P, 2, MH, 8], F32, pe_)
        hi8 = sb("hi8", [P, 2, MH, 8], U32, pe_)
        sc8 = sb("sc8", [P, 2, 8], F32, pe_)
        cand = sb("cand", [P, 2, MH], F32, pe_)
        tm8 = sb("tm8", [P, 2, 8], F32, pe_)
        ti8 = sb("ti8", [P, 2, 8], U32, pe_)
        tf = sb("tf", [P, 2, 2], F32, pe_)
        pick = sb("pick", [P, 2, 2, MH], F32, pe_)
        sel = sb("sel", [P, 2, 2], F32, pe_)
        oh = sb("oh", [P, 2, 2, ME], BF16, pe_)
        ohs = sb("ohs", [P, 2, ME], BF16, pe_)
        cum = sb("cum", [P, 2, ME], BF16, pe_)
        pos1 = sb("pos1", [P, 2, ME], F32, pe_)
        junk = sb("junk", [P, 2, 2, ME], F32, pe_)
        place = sb("place", [P, 2, 2], F32, pe_)
        keep = sb("keep", [P, 2, 2], F32, pe_)
        slf = sb("slf", [P, 2, 2], F32, pe_)
        plf = sb("plf", [P, 2, 2], F32, pe_)
        skipi = sb("skipi", [P, ME * SLOTS + LISTED], I32, pe_)
        slot3 = sb("slot3", [P, 4, 3], I32, pe_)
        ehold = sb("ehold", [P, 4, 8], F32, pe_)
        e_ld, e_s3, e_sn, e_id = sems("e_ld", 4), sems("e_s3", 4), sems("e_sn", 4), sems("e_id", 4)
        (e_0, e_y, e_r, e_x3, e_bn, e_mv, e_ve, e_rs, e_n3, e_tr, e_nT, e_lg, e_lc, e_m8, e_i8, e_sc, e_tm, e_ti, e_tf,
         e_pk, e_oh, e_os, e_cu, e_pre, e_p1, e_k0, e_k1, e_ks, e_w, e_i, e_ix, e_hd, e_vm, e_is, e_tot, e_pf) = (
            sem("e_" + n) for n in ("0 y r x3 bn mv ve rs n3 tr nT lg lc m8 i8 sc tm ti tf pk oh os cu pre p1 k0 k1 ks "
                                    "w i ix hd vm is tot pf").split())

        with nc.Block() as block:
            @block.sync
            def _(sp):
                def store(g, s, t):
                    sp.wait_ge(e_x3, t + 1)
                    sp.dma_start(row(X3, t), x3[:, s, :]).then_inc(e_s3[s], 16)
                    sp.wait_ge(e_n3, t + 1)
                    sp.dma_start(row(XN3, t), n3[:, s, :]).then_inc(e_sn[s], 16)

                def body(g, s):
                    t = g * 4 + s
                    since(sp, e_x3, t, 4)
                    sp.dma_start(ex2[:, s, :], row(X2, t)).then_inc(e_ld[s], 16)
                    sp.dma_start(eg[:, s, :], row(GR, t)).then_inc(e_ld[s], 16)
                    sp.dma_start(ea2[:, s, :], row(AG2, t)).then_inc(e_ld[s], 16)
                    if warm(g, s, 4, 4):
                        store(*ago(g, s, 4))

                sp.wait_ge(e_i, 5)
                sp.dma_start(IDX.rearrange("r c -> (r c)").rearrange("(p c) -> p c", p=P), skipi[:])\
                    .then_inc(e_is, 16)
                stream(sp, NT, 4, body, 2)
                for t in range(NT, NT + 4):
                    store(*ago(0, t, 4))
                for s in range(4):
                    sp.wait_ge(e_s3[s], 16 * ((NT + 3 - s) // 4))
                    sp.wait_ge(e_sn[s], 16 * ((NT + 3 - s) // 4))

            @block.gpsimd
            def _(pool):
                pool.iota(sl3[:, 2, :], [[P, NT]], base=0, channel_multiplier=1).then_inc(e_i, 1)
                pool.iota(prow[:], [[0, 1]], base=0, channel_multiplier=1,
                          allow_small_or_imprecise_dtypes=True).then_inc(e_i, 1)
                pool.memset(skipi[:], int(SKIP)).then_inc(e_i, 1)
                pool.memset(mask[:], 1.0).then_inc(e_i, 1)
                pool.wait_ge(e_i, 4)
                pool.affine_select(out=mask[:], in_=mask[:], compare_op=ALU.is_gt, fill=0.0, base=TAIL,
                                   pattern=[[0, 1]], channel_multiplier=-1).then_inc(e_i, 1)
                pool.wait_ge(e_i, 5)

                def enter(g, s, t):
                    pool.wait_ge(e_w, t + 1)
                    if not isinstance(t, int) or t >= 4:
                        pool.wait_ge(e_id[s], 32 * g)
                    pool.tensor_copy(slot3[:, s, :], sl3[:, :, bass.ds(t, 1)].rearrange("p a t -> p (a t)"))\
                        .then_inc(e_ix, 1)
                    pool.wait_ge(e_ix, t + 1)
                    pool.wait_ge(e_is, 16)
                    hold(pool, 0, s, e_hd, t)
                    for k in range(2):
                        pool.indirect_dma_start(IDXF, bass.IndirectOffsetOnAxis(slot3[:, s, k:k + 1], 0),
                                                slot3[:, s, 2:3], None, bounds_check=ME * SLOTS * P - 1,
                                                oob_is_err=False).then_inc(e_id[s], 16)

                def body(g, s):
                    t, h = g * 4 + s, s % 2
                    if warm(g, s, 6, 4):
                        enter(*ago(g, s, 6))
                    pool.wait_ge(e_mv, t + 1)
                    pool.tensor_tensor(eve[:, h, :], emv[:, h, 1:2], epst[:], ALU.add).then_inc(e_ve, 1)
                    since(pool, e_n3, t, 2)
                    pool.wait_ge(e_ve, t + 1)
                    pool.tensor_tensor(ers[:, h, :], eve[:, h, :], mhalf[:, 0:1], ALU.pow).then_inc(e_rs, 1)

                stream(pool, NT, 4, body, 3)
                for t in range(NT - 6, NT):
                    enter(*ago(0, t, 0))
                for s in range(4):
                    pool.wait_ge(e_id[s], 32 * ((NT + 3 - s) // 4))

            @block.vector
            def _(dve):
                nc.vector.memset(cum[:], 0.0).then_inc(e_0, 1)
                nc.vector.memset(sc8[:], -BIG).then_inc(e_0, 1)
                dve.wait_ge(e_0, 2)
                dve.wait_ge(e_i, 5)

                def hold_dve(s, k):
                    nc.vector.memset(ehold[:, s, k:k + 1], 0.0)

                def both(g, s, t):
                    dve.wait_ge(e_ld[s], 48 * (g + 1))
                    nc.vector.tensor_tensor(ea2[:, s, :], ea2[:, s, :], eg[:, s, :], ALU.add).then_inc(e_y, 1)

                def residual(g, s, t):
                    h = s % 2
                    dve.wait_ge(e_r, t + 1)
                    if not isinstance(t, int) or t >= 4:
                        dve.wait_ge(e_s3[s], 16 * g)
                    nc.vector.tensor_tensor(x3[:, s, :], er[:, h, :], ex2[:, s, :], ALU.add).then_inc(e_x3, 1)
                    dve.wait_ge(e_x3, t + 1)
                    nc.vector.bn_stats(est[:, h, :], x3[:, s, :]).then_inc(e_bn, 1)
                    dve.wait_ge(e_bn, t + 1)
                    hold_dve(s, 0)
                    nc.vector.bn_aggr(emv[:, h, :], est[:, h, :]).then_inc(e_mv, 1)

                def norm(g, s, t):
                    h = s % 2
                    dve.wait_ge(e_rs, t + 1)
                    since(dve, e_tr, t, 4)
                    if not isinstance(t, int) or t >= 4:
                        dve.wait_ge(e_sn[s], 16 * g)
                    nc.vector.tensor_scalar(n3[:, s, :], x3[:, s, :], emv[:, h, 0:1], ers[:, h, :],
                                            ALU.subtract, ALU.mult).then_inc(e_n3, 1)

                def select(g, s, t):
                    h = s % 2
                    dve.wait_ge(e_lc, t + 1)
                    hold_dve(s, 1)
                    for k in range(MH):
                        last = nc.vector.max(hm8[:, h, k, :], lg[:, h, k * ME:(k + 1) * ME])
                    last.then_inc(e_m8, 1)
                    dve.wait_ge(e_m8, t + 1)
                    hold_dve(s, 2)
                    for k in range(MH):
                        last = nc.vector.max_index(hi8[:, h, k, :], hm8[:, h, k, :], lg[:, h, k * ME:(k + 1) * ME])
                    last.then_inc(e_i8, 1)
                    nc.vector.tensor_copy(sc8[:, h, 0:MH], hm8[:, h, :, 0]).then_inc(e_sc, 1)
                    dve.wait_ge(e_i8, t + 1)
                    nc.vector.tensor_copy(cand[:, h, :], hi8[:, h, :, 0]).then_inc(e_sc, 1)
                    dve.wait_ge(e_sc, 2 * t + 2)
                    hold_dve(s, 3)
                    nc.vector.max(tm8[:, h, :], sc8[:, h, :]).then_inc(e_tm, 1)
                    dve.wait_ge(e_tm, t + 1)
                    hold_dve(s, 4)
                    nc.vector.max_index(ti8[:, h, :], tm8[:, h, :], sc8[:, h, :]).then_inc(e_ti, 1)
                    dve.wait_ge(e_ti, t + 1)
                    nc.vector.tensor_copy(tf[:, h, :], ti8[:, h, 0:2]).then_inc(e_tf, 1)
                    dve.wait_ge(e_tf, t + 1)
                    for k in range(2):
                        last = nc.vector.scalar_tensor_tensor(pick[:, h, k, :], iota[:, 0:MH], tf[:, h, k:k + 1],
                                                              cand[:, h, :], ALU.is_equal, ALU.mult,
                                                              accum_out=sel[:, h, k:k + 1])
                    last.then_inc(e_pk, 1)
                    dve.wait_ge(e_pk, t + 1)
                    for k in range(2):
                        last = nc.vector.tensor_scalar(oh[:, h, k, :], iota[:, 0:ME], sel[:, h, k:k + 1], None,
                                                       ALU.is_equal)
                    last.then_inc(e_oh, 1)
                    dve.wait_ge(e_oh, t + 1)
                    if isinstance(t, int) and t == NT - 1:
                        nc.vector.tensor_scalar(oh[:, h, :, :], oh[:, h, :, :], mask[:], None, ALU.mult)\
                            .then_inc(e_vm, 1)
                        dve.wait_ge(e_vm, 1)
                    since(dve, e_pre, t, 1)
                    nc.vector.tensor_tensor(ohs[:, h, :], oh[:, h, 0, :], oh[:, h, 1, :], ALU.add).then_inc(e_os, 1)
                    dve.wait_ge(e_os, t + 1)
                    nc.vector.tensor_tensor(cum[:, 1 - h, :], cum[:, h, :], ohs[:, h, :], ALU.add).then_inc(e_cu, 1)

                def weigh(g, s, t):
                    h = s % 2
                    dve.wait_ge(e_pre, t + 1)
                    nc.vector.tensor_tensor(pos1[:, h, :], bank[2][:, 0:ME], oh[:, h, 0, :], ALU.add).then_inc(e_p1, 1)
                    nc.vector.scalar_tensor_tensor(junk[:, h, 0, :], bank[2][:, 0:ME], 1.0, oh[:, h, 0, :],
                                                   ALU.mult, ALU.mult, accum_out=place[:, h, 0:1]).then_inc(e_k0, 1)
                    dve.wait_ge(e_p1, t + 1)
                    nc.vector.scalar_tensor_tensor(junk[:, h, 1, :], pos1[:, h, :], 1.0, oh[:, h, 1, :],
                                                   ALU.mult, ALU.mult, accum_out=place[:, h, 1:2]).then_inc(e_k0, 1)
                    dve.wait_ge(e_k0, 2 * t + 2)
                    nc.vector.tensor_scalar(keep[:, h, :], place[:, h, :], float(CAP), None, ALU.is_lt)\
                        .then_inc(e_k1, 1)
                    nc.vector.scalar_tensor_tensor(slf[:, h, :], sel[:, h, :], float(SLOTS * P), place[:, h, :],
                                                   ALU.mult, ALU.add).then_inc(e_k1, 1)
                    dve.wait_ge(e_k1, 2 * t + 2)
                    if isinstance(t, int) and t == NT - 1:
                        nc.vector.tensor_scalar(keep[:, h, :], keep[:, h, :], mask[:], None, ALU.mult)\
                            .then_inc(e_vm, 1)
                        dve.wait_ge(e_vm, 2)
                    nc.vector.tensor_copy(selk[:, bass.ds(t, 1), :].rearrange("p t a -> p (t a)"), sel[:, h, :])
                    nc.vector.scalar_tensor_tensor(plf[:, h, :], place[:, h, :], -DROPPED, keep[:, h, :],
                                                   ALU.add, ALU.mult).then_inc(e_pf, 1)
                    nc.vector.scalar_tensor_tensor(slf[:, h, :], slf[:, h, :], -DROPPED, keep[:, h, :],
                                                   ALU.add, ALU.mult).then_inc(e_ks, 1)
                    dve.wait_ge(e_ks, t + 1)
                    dve.wait_ge(e_pf, t + 1)
                    nc.vector.tensor_scalar(plk[:, bass.ds(t, 1), :].rearrange("p t a -> p (t a)"), plf[:, h, :],
                                            DROPPED, None, ALU.add)
                    nc.vector.tensor_scalar(sl3[:, 0:2, bass.ds(t, 1)].rearrange("p a t -> p (a t)"), slf[:, h, :],
                                            DROPPED, None, ALU.add)
                    nc.vector.tensor_scalar(w12[:, bass.ds(t, 1), :].rearrange("p t a -> p (t a)"), keep[:, h, :],
                                            0.5, None, ALU.mult).then_inc(e_w, 1)

                steps = ((5, weigh), (4, select), (2, norm), (1, residual), (0, both))

                def body(g, s):
                    for lag, step in steps:
                        if warm(g, s, lag, 4):
                            step(*ago(g, s, lag))

                stream(dve, NT, 4, body, 2)
                for t in range(NT, NT + 5):
                    for lag, step in steps:
                        if t - lag < NT:
                            step(*ago(0, t, lag))
                dve.wait_ge(e_w, NT)
                dve.wait_ge(e_tot, 1)
                nc.vector.tensor_copy(cnt[:], bank[2][:, 0:ME]).then_inc(e_tot, 1)
                dve.wait_ge(e_tot, 2)

            @block.tensor
            def _(pe):
                def places(g, s, t):
                    h = s % 2
                    pe.wait_ge(e_os, t + 1)
                    pe.wait_ge(e_cu, t + 1)
                    since(pe, e_w, t, 1)
                    nc.tensor.matmul(bank[2][:, 0:ME], tri[:], ohs[:, h, :], start=True, stop=False)
                    nc.tensor.matmul(bank[2][:, 0:ME], onesb[:], cum[:, h, :], start=False, stop=True)\
                        .then_inc(e_pre, 1)

                def logits(g, s, t):
                    pe.wait_ge(e_nT, t + 1)
                    since(pe, e_lc, t, 1)
                    mm4(bank[1][:, 0:MH * ME], n3T[:, s % 2, :, :], hp).then_inc(e_lg, 1)

                def turn(g, s, t):
                    pe.wait_ge(e_n3, t + 1)
                    since(pe, e_nT, t, 1)
                    tr4(bank[0], n3[:, s, :]).then_inc(e_tr, 1)

                steps = ((3, logits), (4, places), (2, turn))

                def body(g, s):
                    for lag, step in steps:
                        if warm(g, s, lag, 4):
                            step(*ago(g, s, lag))

                stream(pe, NT, 4, body, 2)
                for t in range(NT, NT + 4):
                    for lag, step in steps:
                        if t - lag < NT:
                            step(*ago(0, t, lag))
                pe.wait_ge(e_w, NT)
                nc.tensor.matmul(bank[2][:, 0:ME], onesb[:], cum[:, NT % 2, :], start=True, stop=True)\
                    .then_inc(e_tot, 1)

            @block.scalar
            def _(act):
                def copy_logits(g, s, t):
                    act.wait_ge(e_lg, t + 1)
                    since(act, e_i8, t, 2)
                    act.activation(lg[:, s % 2, :], bank[1][:, 0:MH * ME], ACT.Copy).then_inc(e_lc, 1)

                def copy_n(g, s, t):
                    act.wait_ge(e_tr, t + 1)
                    since(act, e_lg, t, 2)
                    act.activation(n3T[:, s % 2, :, :].rearrange("p k n -> p (k n)"), bank[0], ACT.Copy)\
                        .then_inc(e_nT, 1)

                def relu(g, s, t):
                    act.wait_ge(e_y, t + 1)
                    since(act, e_x3, t, 2)
                    act.activation(er[:, s % 2, :], ea2[:, s, :], ACT.Relu, scale=dis[:, bass.ds(t, 1)])\
                        .then_inc(e_r, 1)

                steps = ((3, copy_logits), (2, copy_n), (0, relu))

                def body(g, s):
                    for lag, step in steps:
                        if warm(g, s, lag, 4):
                            step(*ago(g, s, lag))

                stream(act, NT, 4, body, 2)
                for t in range(NT, NT + 3):
                    for lag, step in steps:
                        if t - lag < NT:
                            step(*ago(0, t, lag))
        end_phase(pe_)

        YL = nc.dram_tensor("slot_outputs", [LISTED * P, D], F32).ap()
        pt = ExitStack()
        lim = sb("lim", [P, SLOTS], F32, pt)
        cc = sb("cc", [P, ME], F32, pt)
        gt = sb("gt", [P, ME, SLOTS], F32, pt)
        ntl = sb("ntl", [P, ME], F32, pt)
        incl = sb("incl", [P, ME], F32, pt)
        le = sb("le", [P, 2, ME], F32, pt)
        lm = sb("lm", [P, 2, ME], F32, pt)
        tt = sb("tt", [P, 2, 3], F32, pt)
        tab = sb("tab", [P, 4], F32, pt)
        tid = sb("tid", [P, 2], I32, pt)
        trow = sb("trow", [1, 4 * P], I32, pt)
        idr = sb("idr", [P, 2, P], I32, pt)
        idf = sb("idf", [P, 2, P], F32, pt)
        ids = sb("ids", [P, 2 * P], I32, pt)
        g_c = sem("g_c")
        g_ld, g_t, g_tr, g_rw, g_rw2 = (sem(n) for n in ("g_ld", "g_t", "g_tr", "g_rw", "g_rw2"))

        with nc.Block() as block:
            @block.vector
            def _(dve):
                n = [0]

                def then(ins):
                    n[0] += 1
                    ins.then_inc(g_c, 1)
                    dve.wait_ge(g_c, n[0])

                then(nc.vector.tensor_scalar_mul(lim[:], iota[:, 0:SLOTS], float(P)))
                then(nc.vector.tensor_scalar_min(cc[:], cnt[:], float(CAP)))
                then(nc.vector.tensor_tensor(gt[:], cc[:].unsqueeze(2).to_broadcast([P, ME, SLOTS]),
                                             lim[:].unsqueeze(1).to_broadcast([P, ME, SLOTS]), ALU.is_gt))
                then(nc.vector.tensor_reduce(ntl[:], gt[:], AX.X, ALU.add))
                then(nc.vector.memset(cc[:], 1.0))
                then(nc.vector.tensor_tensor_scan(incl[:], cc[:], ntl[:], 0.0, ALU.mult, ALU.add))
                then(nc.vector.tensor_tensor(ntl[:], incl[:], ntl[:], ALU.subtract))
                then(nc.vector.tensor_scalar_mul(cbase[:], ntl[:], float(P)))
                for c in range(2):
                    then(nc.vector.tensor_scalar(ntl[:, c:c + 1], prow[:], float(c * P), None, ALU.add))
                    then(nc.vector.tensor_scalar(le[:, c, :], incl[:], ntl[:, c:c + 1], None, ALU.is_le))
                    then(nc.vector.tensor_tensor(lm[:, c, :], le[:, c, :], incl[:], ALU.mult))
                    then(nc.vector.tensor_reduce(tt[:, c, 0:1], le[:, c, :], AX.X, ALU.add))
                    then(nc.vector.tensor_reduce(tt[:, c, 1:2], lm[:, c, :], AX.X, ALU.max))
                    then(nc.vector.tensor_tensor(tt[:, c, 2:3], ntl[:, c:c + 1], tt[:, c, 1:2], ALU.subtract))
                    then(nc.vector.scalar_tensor_tensor(tab[:, c:c + 1], tt[:, c, 0:1], float(SLOTS), tt[:, c, 2:3],
                                                        ALU.mult, ALU.add))
                    then(nc.vector.tensor_scalar_min(tab[:, 2 + c:3 + c], tt[:, c, 0:1], float(ME - 1)))
                nc.vector.tensor_copy(tid[:], tab[:, 0:2]).then_inc(g_t, 1)
                dve.wait_ge(g_tr, 1)
                nc.vector.tensor_copy(trow[:], bank[0][0:1, 0:4 * P]).then_inc(g_rw, 1)
                dve.wait_ge(g_ld, 32)
                nc.vector.tensor_copy(idf[:], idr[:]).then_inc(g_t, 1)
                dve.wait_ge(g_tr, 2)
                nc.vector.tensor_copy(ids[:], bank[1][:, 0:2 * P]).then_inc(g_rw, 1)
                dve.wait_ge(g_rw, 2)

            @block.gpsimd
            def _(pool):
                pool.memset(idr[:], 0).then_inc(g_rw2, 1)
                pool.wait_ge(g_rw2, 1)
                pool.wait_ge(g_t, 1)
                for c in range(2):
                    pool.indirect_dma_start(idr[:, c, :], None, IDX, bass.IndirectOffsetOnAxis(tid[:, c:c + 1], 0),
                                            bounds_check=ME * SLOTS + LISTED - 1, oob_is_err=False)\
                        .then_inc(g_ld, 16)

            @block.tensor
            def _(pe):
                pe.wait_ge(g_t, 1)
                for k in range(4):
                    last = nc.tensor.matmul(bank[0][0:1, k * P:(k + 1) * P], tab[:, k:k + 1], ident[:],
                                            start=True, stop=True)
                last.then_inc(g_tr, 1)
                pe.wait_ge(g_t, 2)
                for c in range(2):
                    last = nc.tensor.transpose(bank[1][:, c * P:(c + 1) * P], idf[:, c, :], ident[:])
                last.then_inc(g_tr, 1)

        xg = sb("xg", [P, 4, D], F32, pt)
        gT = sb("gT", [P, 2, DK, P], F32, pt)
        we1 = sb("we1", [P, 4, DK * MF], F32, pt)
        we2 = sb("we2", [MF, 4, D], F32, pt)
        hg = sb("hg", [MF, 2, P], F32, pt)
        yo = sb("yo", [P, 4, D], F32, pt)
        sg = sb("sg", [P, 4, 1], I32, pt)
        p_ld, p_w, p_st = sems("p_ld", 4), sems("p_w", 4), sems("p_st", 4)
        p_0, p_ix, p_hd, p_tr, p_T, p_up, p_h, p_dn, p_y = (
            sem("p_" + n) for n in "0 ix hd tr T up h dn y".split())

        with nc.Block() as block:
            @block.sync
            def _(sp):
                def store(g, s, t):
                    sp.wait_ge(p_y, t + 1)
                    sp.dma_start(row(YL, t), yo[:, s, :]).then_inc(p_st[s], 16)

                def body(g, s):
                    t = g * 4 + s
                    e = sp.value_load(trow[0:1, bass.ds(t + 2 * P, 1)], min_val=0, max_val=ME - 1)
                    since(sp, p_dn, t, 4)
                    sp.dma_start(we1[:, s, :], M1[bass.ds(e * P, P), :]).then_inc(p_w[s], 16)
                    sp.dma_start(we2[:, s, :], M2[bass.ds(e * MF, MF), :]).then_inc(p_w[s], 16)
                    if warm(g, s, 3, 4):
                        store(*ago(g, s, 3))

                stream(sp, LISTED, 4, body)
                for t in range(LISTED - 3, LISTED):
                    store(*ago(0, t, 0))
                for s in range(4):
                    sp.wait_ge(p_st[s], 16 * ((LISTED + 3 - s) // 4))

            @block.gpsimd
            def _(pool):
                pool.memset(xg[:], 0.0).then_inc(p_0, 1)

                def body(g, s):
                    t = g * 4 + s
                    since(pool, p_tr, t, 4)
                    pool.tensor_copy(sg[:, s, :], ids[:, bass.ds(t, 1)]).then_inc(p_ix, 1)
                    pool.wait_ge(p_ix, t + 1)
                    pool.wait_ge(p_0, 1)
                    hold(pool, 0, s, p_hd, t)
                    pool.indirect_dma_start(xg[:, s, :], None, XN3, bass.IndirectOffsetOnAxis(sg[:, s, 0:1], 0),
                                            bounds_check=NP - 1, oob_is_err=False).then_inc(p_ld[s], 16)

                stream(pool, LISTED, 4, body)

            @block.tensor
            def _(pe):
                def turn(g, s, t):
                    pe.wait_ge(p_ld[s], 16 * (g + 1))
                    since(pe, p_T, t, 2)
                    tr4(bank[s % 2], xg[:, s, :]).then_inc(p_tr, 1)

                def up(g, s, t):
                    h = s % 2
                    pe.wait_ge(p_T, t + 1)
                    pe.wait_ge(p_w[s], 32 * (g + 1))
                    since(pe, p_h, t, 2)
                    for k in range(DK):
                        last = nc.tensor.matmul(bank[2 + h][0:MF, 0:P], we1[:, s, k * MF:(k + 1) * MF],
                                                gT[:, h, k, :], start=(k == 0), stop=(k == DK - 1))
                    last.then_inc(p_up, 1)

                def down(g, s, t):
                    h = s % 2
                    pe.wait_ge(p_h, t + 1)
                    since(pe, p_y, t, 2)
                    nc.tensor.matmul(bank[4 + h], hg[:, h, :], we2[:, s, :], start=True, stop=True).then_inc(p_dn, 1)

                steps = ((2, down), (1, up), (0, turn))

                def body(g, s):
                    for lag, step in steps:
                        if warm(g, s, lag, 4):
                            step(*ago(g, s, lag))

                stream(pe, LISTED, 4, body)
                for t in range(LISTED, LISTED + 2):
                    for lag, step in steps:
                        if t - lag < LISTED:
                            step(*ago(0, t, lag))

            @block.scalar
            def _(act):
                def gelu(g, s, t):
                    h = s % 2
                    act.wait_ge(p_up, t + 1)
                    since(act, p_dn, t, 2)
                    act.activation(hg[:, h, :], bank[2 + h][0:MF, 0:P], ACT.Gelu).then_inc(p_h, 1)

                def copy(g, s, t):
                    act.wait_ge(p_tr, t + 1)
                    since(act, p_up, t, 2)
                    act.activation(gT[:, s % 2, :, :].rearrange("p k n -> p (k n)"), bank[s % 2], ACT.Copy)\
                        .then_inc(p_T, 1)

                steps = ((1, gelu), (0, copy))

                def body(g, s):
                    for lag, step in steps:
                        if warm(g, s, lag, 4):
                            step(*ago(g, s, lag))

                stream(act, LISTED, 4, body)
                gelu(*ago(0, LISTED, 1))

            @block.vector
            def _(dve):
                def body(g, s):
                    t = g * 4 + s
                    if warm(g, s, 4, 4):
                        dve.wait_ge(p_st[s], 16 * g)
                    dve.wait_ge(p_dn, t + 1)
                    nc.vector.tensor_copy(yo[:, s, :], bank[4 + s % 2]).then_inc(p_y, 1)

                stream(dve, LISTED, 4, body)
        end_phase(pt)

        pq = ExitStack()
        qx = sb("qx", [P, 4, D], F32, pq)
        q0 = sb("q0", [P, 4, 2, D], F32, pq)
        qs = sb("qs", [P, 4, 2], I32, pq)
        qj = sb("qj", [P, 4, 2, ME], F32, pq)
        qf = sb("qf", [P, 4, 2], F32, pq)
        q_ld, q_x, q_st = sems("q_ld", 4), sems("q_x", 4), sems("q_st", 4)
        q_0, q_ix, q_hd, q_a, q_b, q_f = (sem("q_" + n) for n in "0 ix hd a b f".split())

        with nc.Block() as block:
            @block.sync
            def _(sp):
                def store(g, s, t):
                    sp.wait_ge(q_b, t + 1)
                    n = TAIL if isinstance(t, int) and t == NT - 1 else P
                    sp.dma_start(row(out, t, n), qx[0:n, s, :]).then_inc(q_st[s], 16)

                def body(g, s):
                    t = g * 4 + s
                    if warm(g, s, 4, 4):
                        sp.wait_ge(q_st[s], 16 * g)
                    sp.dma_start(qx[:, s, :], row(X3, t)).then_inc(q_x[s], 16)
                    if warm(g, s, 2, 4):
                        store(*ago(g, s, 2))

                stream(sp, NT, 4, body)
                for t in range(NT - 2, NT):
                    store(*ago(0, t, 0))
                for s in range(4):
                    sp.wait_ge(q_st[s], 16 * ((NT + 3 - s) // 4))

            @block.gpsimd
            def _(pool):
                def body(g, s):
                    t = g * 4 + s
                    since(pool, q_b, t, 4)
                    pool.wait_ge(q_ix, t + 1)
                    pool.wait_ge(q_0, 1)
                    hold(pool, 0, s, q_hd, t)
                    for k in range(2):
                        pool.indirect_dma_start(q0[:, s, k, :], None, YL,
                                                bass.IndirectOffsetOnAxis(qs[:, s, k:k + 1], 0),
                                                bounds_check=LISTED * P - 1, oob_is_err=False)\
                            .then_inc(q_ld[s], 16)

                stream(pool, NT, 4, body)

            @block.vector
            def _(dve):
                nc.vector.memset(q0[:], 0.0).then_inc(q_0, 1)

                def find(g, s, t):
                    if not isinstance(t, int) or t >= 4:
                        dve.wait_ge(q_ld[s], 32 * g)
                    for k in range(2):
                        last = nc.vector.scalar_tensor_tensor(
                            qj[:, s, k, :], iota[:, 0:ME], selk[:, bass.ds(t, 1), k], cbase[:], ALU.is_equal,
                            ALU.mult, accum_out=qf[:, s, k:k + 1])
                    last.then_inc(q_f, 1)
                    dve.wait_ge(q_f, t + 1)
                    nc.vector.tensor_tensor(qs[:, s, :], qf[:, s, :],
                                            plk[:, bass.ds(t, 1), :].rearrange("p t a -> p (t a)"), ALU.add)\
                        .then_inc(q_ix, 1)

                def combine(g, s, t):
                    dve.wait_ge(q_x[s], 16 * (g + 1))
                    dve.wait_ge(q_ld[s], 32 * (g + 1))
                    w = w12[:, bass.ds(t, 1), :].rearrange("p t a -> p (t a)")
                    nc.vector.scalar_tensor_tensor(q0[:, s, 0, :], q0[:, s, 0, :], w[:, 0:1], qx[:, s, :],
                                                   ALU.mult, ALU.add).then_inc(q_a, 1)
                    dve.wait_ge(q_a, t + 1)
                    nc.vector.scalar_tensor_tensor(qx[:, s, :], q0[:, s, 1, :], w[:, 1:2], q0[:, s, 0, :],
                                                   ALU.mult, ALU.add).then_inc(q_b, 1)

                def body(g, s):
                    find(*ago(g, s, 0))
                    if warm(g, s, 3, 4):
                        combine(*ago(g, s, 3))

                stream(dve, NT, 4, body, 2)
                for t in range(NT - 3, NT):
                    combine(*ago(0, t, 0))
        end_phase(pq)


_INS = ["x", "src", "dst", "Wl", "Wr", "att", "gbias", "Wc0", "b1c", "W2e", "b2e", "WT", "bG", "hashp", "M1", "M2"]


def kernel(x, src, dst, L0_gnn_W_l, L0_gnn_W_r, L0_gnn_att, L0_gnn_bias, L0_ffn_Wr, L0_ffn_br, L0_ffn_W1, L0_ffn_b1,
           L0_ffn_W2, L0_ffn_b2, L1_gnn_W, L1_gnn_b, L1_ffn_hash_proj, L1_ffn_W1, L1_ffn_W2):
    import concourse.bacc as _bacc
    from concourse.bass_utils import run_bass_kernel_spmd as _run

    a = {k: np.asarray(v) for k, v in locals().items() if not k.startswith("_")}
    flat = {
        "x": a["x"], "src": a["src"], "dst": a["dst"], "Wl": a["L0_gnn_W_l"], "Wr": a["L0_gnn_W_r"],
        "att": a["L0_gnn_att"].reshape(D), "gbias": a["L0_gnn_bias"],
        "Wc0": np.concatenate([a["L0_ffn_W1"].transpose(1, 0, 2).reshape(D, FC), a["L0_ffn_Wr"]], axis=1),
        "b1c": np.concatenate([a["L0_ffn_b1"].reshape(FC), a["L0_ffn_br"]]),
        "W2e": a["L0_ffn_W2"].reshape(FC, D), "b2e": a["L0_ffn_b2"],
        "WT": a["L1_gnn_W"].T, "bG": a["L1_gnn_b"],
        "hashp": a["L1_ffn_hash_proj"].transpose(1, 0, 2).reshape(D, MH * ME),
        "M1": a["L1_ffn_W1"].reshape(ME, DK, P, MF).transpose(0, 2, 1, 3).reshape(ME * P, DK * MF),
        "M2": a["L1_ffn_W2"].reshape(MC, D),
    }
    nc = _bacc.Bacc("TRN2", target_bir_lowering=False, num_devices=1)
    arrays, aps = {}, []
    for name in _INS:
        v = np.ascontiguousarray(flat[name])
        arrays["in_" + name] = v
        aps.append(nc.dram_tensor("in_" + name, v.shape, mybir.dt.from_np(v.dtype), kind="ExternalInput").ap())
    out = nc.dram_tensor("out_0", (N, D), F32, kind="ExternalOutput").ap()
    gnn_ffn(nc, *aps, out)
    r = _run(nc, [arrays], core_ids=[0])
    return r.results[0]["out_0"]
```

```python
import numpy as np
from contextlib import ExitStack

import concourse.bass as bass
from concourse import mybir
from concourse.alu_op_type import AluOpType as ALU

ACT = mybir.ActivationFunctionType
F32 = mybir.dt.float32
BF16 = mybir.dt.bfloat16
I32 = mybir.dt.int32
U32 = mybir.dt.uint32
AX = mybir.AxisListType

P = 128
N, D = 10000, 512
E = 15000
H, C = 8, 64
DK = D // P
NT = -(-N // P)
NP = NT * P
TAIL = N - (NT - 1) * P
CE = C + 1
XE = H * CE
AW = XE + H
W = P - 1
ET = -(-E // W)
EP, EC = 120, E // 120
FL = EP * P
NE, FH = 8, 32
FC = NE * FH
ME, MH, MF = 64, 4, 32
MC = ME * MF
CAP = 4 * N * 2 // ME
SLOTS = -(-CAP // P)
LISTED = (2 * N + ME * (P - 1)) // P
DROPPED = 200000.0
SKIP = 20000.0
BIG = 1.0e30
EPS = 1e-5
SLOPE = 0.2


def stream(eng, n, ring, body, peel=1):
    for g in range(peel):
        for s in range(ring):
            body(g, s)
    with eng.Fori(peel, n // ring) as g:
        for s in range(ring):
            body(g, s)
    for s in range(n % ring):
        body(n // ring, s)


def warm(g, s, lag, ring):
    return not isinstance(g, int) or g * ring + s >= lag


def gnn_ffn(nc, x, src, dst, Wl, Wr, att, gbias, Wc0, b1c, W2e, b2e, WT, bG, hashp, M1, M2, out):
    ctx = ExitStack()
    with ctx:
        def sb(name, shape, dt=F32, on=None):
            return (on or ctx).enter_context(nc.sbuf_tensor(name, shape, dt))

        phase = []

        def sem(name):
            phase.append(nc.alloc_semaphore(name=name))
            return phase[-1]

        def end_phase(buffers):
            buffers.close()
            nc.clear_and_free_semaphores(phase)
            phase.clear()
            nc.all_engine_barrier()

        def sems(name, n):
            return [sem(f"{name}{i}") for i in range(n)]

        psum = ctx.enter_context(nc.psum_tensor("psum", [P, 8, 512], F32))
        bank = [psum[:, i, :] for i in range(8)]
        pair = [psum[:, 4 + 2 * i:6 + 2 * i, 0:XE // 2] for i in range(2)]

        XLE = nc.dram_tensor("xl_ext", [NP, XE], F32).ap()
        XR = nc.dram_tensor("xr_rows", [NP, D], F32).ap()
        AGG = nc.dram_tensor("edge_sums0", [NP, AW], F32).ap()
        X2 = nc.dram_tensor("x2_rows", [NP, D], F32).ap()
        GR = nc.dram_tensor("gcn_rows", [NP, D], F32).ap()
        AG2 = nc.dram_tensor("edge_sums1", [NP, D], F32).ap()
        FD = nc.dram_tensor("flat_dst", [FL], F32).ap()
        FS = nc.dram_tensor("flat_src", [FL], F32).ap()
        MDR = nc.dram_tensor("window_dst", [ET, P], F32).ap()
        RRR = nc.dram_tensor("window_resets", [ET, 2 * P], F32).ap()

        ident = sb("ident", [P, P])
        identb = sb("identb", [P, P], BF16)
        tri = sb("tri", [P, P], BF16)
        onesb = sb("onesb", [P, P], BF16)
        iota = sb("iota", [P, P])
        mhalf = sb("mhalf", [P, NT])
        epst = sb("epst", [P, 1])
        minus1 = sb("minus1", [P, 1])
        one = sb("one", [P, 1])
        att_b = sb("att_b", [P, D])
        gb_b = sb("gb_b", [P, D])
        wl = sb("wl", [P, DK, D])
        wr = sb("wr", [P, DK, D])
        wc = sb("wc", [P, DK, FC + NE])
        w2 = sb("w2", [P, FC // P, D])
        b1b = sb("b1b", [P, FC + NE])
        b2 = sb("b2", [P, D])
        b2p = sb("b2p", [P, D], BF16)
        iota3 = sb("iota3", [P, P])
        wg = sb("wg", [P, DK, D])
        bgb = sb("bgb", [P, D])
        hp = sb("hp", [P, DK, MH * ME])
        selfa = sb("selfa", [P, NT, H])
        xsc = sb("xsc", [P, NT, 2])
        deg1 = sb("deg1", [P, NT])
        dis = sb("dis", [P, NT])
        kd = sb("kd", [P, ET])
        zin = sb("zin", [P, AW])
        idx = sb("idx", [P, 3, ET], I32)

        slot = sb("slot", [P, 4, 3], I32)
        held = sb("held", [P, 2, 4])

        def hold(pool, site, s, done, t):
            if not isinstance(t, int) or t >= 4:
                pool.wait_ge(done, t - 3)
            pool.tensor_tensor(held[:, site, s:s + 1], mhalf[:, 0:1], mhalf[:, 1:2], ALU.add).then_inc(done, 1)

        w_att, w_proj, w_rest, h_init = (nc.alloc_semaphore(name=n) for n in ("w_att", "w_proj", "w_rest", "h_init"))
        consts = sem("consts")
        c_mr = sem("c_mr")
        c_flat, c_int, c_f32, c_win, c_cmp, c_rows, c_tr, c_idx = (
            sem(n) for n in ("c_flat", "c_int", "c_f32", "c_win", "c_cmp", "c_rows", "c_tr", "c_idx"))
        h_oh, h_mm, h_deg = (sem(n) for n in ("h_oh", "h_mm", "h_deg"))

        prep = ExitStack()
        ei = sb("ei", [EP, 2, EC], I32, prep)
        ef = sb("ef", [EP, 2, EC], F32, prep)
        eh = sb("eh", [EP, 2, EC], I32, prep)
        ehf = sb("ehf", [EP, 2, EC], F32, prep)
        ohl = sb("ohl", [EP, 4, P], BF16, prep)
        ohh = sb("ohh", [EP, 4, NT], BF16, prep)
        padt = sb("padt", [EP, P], F32, prep)
        win = sb("win", [ET, 2, P + 2], F32, prep)
        ne = sb("ne", [ET, P], F32, prep)
        rr = sb("rr", [ET, 2, P], F32, prep)
        mdw = sb("mdw", [ET, P], F32, prep)
        wcol = sb("wcol", [ET, 3, P], F32, prep)

        with nc.Block() as block:
            @block.sync
            def _(sp):
                sp.dma_start(ei[:, 0, :], dst.rearrange("(p c) -> p c", c=EC)).then_inc(c_int, 16)
                sp.dma_start(ei[:, 1, :], src.rearrange("(p c) -> p c", c=EC)).then_inc(c_int, 16)
                sp.wait_ge(consts, 6)
                sp.dma_start(FD.rearrange("(p c) -> p c", c=P), padt[:]).then_inc(c_flat, 16)
                sp.dma_start(FS.rearrange("(p c) -> p c", c=P), padt[:]).then_inc(c_flat, 16)
                sp.wait_ge(c_flat, 32)
                sp.wait_ge(c_f32, 1)
                sp.dma_start(FD[1:1 + E].rearrange("(p c) -> p c", c=EC), ef[:, 0, :]).then_inc(c_flat, 16)
                sp.dma_start(FS[1:1 + E].rearrange("(p c) -> p c", c=EC), ef[:, 1, :]).then_inc(c_flat, 16)
                sp.wait_ge(c_flat, 64)
                for k, f in enumerate((FD, FS)):
                    v = bass.AP(f.tensor, 0, [[W, ET], [1, P + 1]])
                    sp.dma_start(win[:, k, 0:P + 1], v).then_inc(c_win, 16)
                sp.wait_ge(c_rows, 1)
                sp.dma_start(MDR, mdw[:]).then_inc(c_mr, 16)
                sp.dma_start(RRR, rr[:].rearrange("t a p -> t (a p)")).then_inc(c_mr, 16)
                sp.wait_ge(c_mr, 32)

            @block.scalar
            def _(act):
                act.dma_start(wl[:], Wl.rearrange("(k p) n -> p k n", p=P)).then_inc(w_proj, 16)
                act.dma_start(wr[:], Wr.rearrange("(k p) n -> p k n", p=P)).then_inc(w_proj, 16)
                act.dma_start(att_b[:], att.partition_broadcast(P)).then_inc(w_att, 16)
                for t, s in ((wc, Wc0), (wg, WT), (hp, hashp), (w2, W2e)):
                    act.dma_start(t[:], s.rearrange("(k p) n -> p k n", p=P)).then_inc(w_rest, 16)
                for t, s in ((gb_b, gbias), (b1b, b1c), (bgb, bG)):
                    act.dma_start(t[:], s.partition_broadcast(P)).then_inc(w_rest, 16)
                act.wait_ge(consts, 6)
                for k in range(3):
                    act.dma_start(b2[32 * k:32 * k + NE, :], b2e).then_inc(w_rest, 16)

            @block.gpsimd
            def _(pool):
                pool.memset(padt[:], SKIP).then_inc(consts, 1)
                pool.memset(zin[:, 0:XE], 0.0).then_inc(consts, 1)
                pool.memset(zin[:, XE:AW], -BIG).then_inc(consts, 1)
                pool.memset(mhalf[:], -0.5)
                pool.iota(iota3[:].rearrange("p (a b) -> p a b", b=32), [[0, P // 32], [1, 32]], base=0,
                          channel_multiplier=0, allow_small_or_imprecise_dtypes=True)
                pool.memset(b2[:], 0.0)
                pool.memset(epst[:], EPS)
                pool.memset(one[:], 1.0)
                pool.memset(minus1[:], -1.0).then_inc(consts, 1)
                pool.memset(onesb[:], 1.0).then_inc(consts, 1)
                pool.iota(iota[:], [[1, P]], base=0, channel_multiplier=0,
                          allow_small_or_imprecise_dtypes=True).then_inc(consts, 1)
                pool.memset(ident[:], 0.0).then_inc(consts, 1)
                pool.memset(identb[:], 0.0).then_inc(consts, 1)
                pool.memset(tri[:], 1.0).then_inc(consts, 1)
                pool.wait_ge(consts, 9)
                for m in (ident, identb):
                    pool.affine_select(out=m[:], in_=m[:], compare_op=ALU.not_equal, fill=1.0, base=0,
                                       pattern=[[-1, P]], channel_multiplier=1).then_inc(consts, 1)
                pool.affine_select(out=tri[:], in_=tri[:], compare_op=ALU.is_gt, fill=0.0, base=0,
                                   pattern=[[1, P]], channel_multiplier=-1).then_inc(consts, 1)
                pool.wait_ge(consts, 12)

            @block.vector
            def _(dve):
                dve.wait_ge(c_int, 32)
                nc.vector.tensor_copy(ef[:], ei[:]).then_inc(c_f32, 1)
                nc.vector.tensor_scalar(eh[:, 0, :], ei[:, 1, :], P - 1, None, ALU.bitwise_and).then_inc(c_f32, 1)
                nc.vector.tensor_scalar(eh[:, 1, :], ei[:, 1, :], 7, None,
                                        ALU.logical_shift_right).then_inc(c_f32, 1)
                dve.wait_ge(c_f32, 3)
                nc.vector.tensor_copy(ehf[:], eh[:]).then_inc(c_f32, 1)
                dve.wait_ge(c_f32, 4)
                dve.wait_ge(consts, 12)

                def onehots(g, s):
                    t = g * 4 + s
                    if warm(g, s, 4, 4):
                        dve.wait_ge(h_mm, t - 3)
                    nc.vector.tensor_scalar(ohl[:, s, :], iota[0:EP, :], ehf[:, 0, bass.ds(t, 1)], None,
                                            ALU.is_equal)
                    nc.vector.tensor_scalar(ohh[:, s, :], iota[0:EP, 0:NT], ehf[:, 1, bass.ds(t, 1)], None,
                                            ALU.is_equal).then_inc(h_oh, 1)

                stream(dve, EC, 4, onehots)
                dve.wait_ge(h_mm, EC)
                nc.vector.tensor_scalar_add(deg1[:], bank[0][:, 0:NT], 1.0).then_inc(h_deg, 1)

                dve.wait_ge(c_win, 32)
                nc.vector.memset(win[0:1, 0, 0:1], -1.0).then_inc(c_cmp, 1)
                nc.vector.memset(rr[:], -BIG).then_inc(c_cmp, 1)
                nc.vector.memset(wcol[:], SKIP).then_inc(c_cmp, 1)
                dve.wait_ge(c_cmp, 3)
                nc.vector.tensor_tensor(ne[:], win[:, 0, 1:P + 1], win[:, 0, 0:P], ALU.not_equal).then_inc(c_cmp, 1)
                dve.wait_ge(c_cmp, 4)
                nc.vector.tensor_scalar_mul(rr[:, 0, 1:P], ne[:, 0:P - 1], -BIG).then_inc(c_cmp, 1)
                nc.vector.tensor_scalar_mul(rr[:, 1, 0:P - 1], ne[:, 0:P - 1], -BIG).then_inc(c_cmp, 1)
                nc.vector.tensor_copy(mdw[:, 0:1], win[:, 0, W:P]).then_inc(c_cmp, 1)
                nc.vector.tensor_copy(mdw[:, 1:P], win[:, 0, 1:P]).then_inc(c_cmp, 1)
                nc.vector.tensor_copy(wcol[:, 0, 1:P], win[:, 1, 1:P]).then_inc(c_cmp, 1)
                nc.vector.tensor_copy(wcol[:, 1, 1:P], win[:, 0, 1:P]).then_inc(c_cmp, 1)
                nc.vector.scalar_tensor_tensor(wcol[:, 2, 1:P], win[:, 0, 1:P], -SKIP, ne[:, 1:P],
                                               ALU.add, ALU.mult).then_inc(c_cmp, 1)
                dve.wait_ge(c_cmp, 11)
                nc.vector.tensor_scalar_add(wcol[:, 2, 1:P], wcol[:, 2, 1:P], SKIP).then_inc(c_rows, 1)
                dve.wait_ge(c_tr, 1)
                nc.vector.tensor_copy(kd[:], bank[1][:, 0:ET]).then_inc(c_idx, 1)
                nc.vector.tensor_copy(idx[:], bank[2][:, 0:3 * ET].rearrange("p (a t) -> p a t", a=3))\
                    .then_inc(c_idx, 1)
                dve.wait_ge(c_idx, 2)

            @block.tensor
            def _(pe):
                def count(g, s):
                    t = g * 4 + s
                    pe.wait_ge(h_oh, t + 1)
                    first = isinstance(g, int) and t == 0
                    last = isinstance(g, int) and t == EC - 1
                    nc.tensor.matmul(bank[0][:, 0:NT], ohl[:, s, :], ohh[:, s, :], start=first, stop=last,
                                     skip_group_check=True).then_inc(h_mm, 1)

                stream(pe, EC, 4, count)
                pe.wait_ge(c_rows, 1)
                nc.tensor.transpose(bank[1][:, 0:ET], win[:, 0, 0:P], ident[0:ET, 0:ET])
                for a in range(3):
                    last = nc.tensor.transpose(bank[2][:, a * ET:(a + 1) * ET], wcol[:, a, :], ident[0:ET, 0:ET])
                last.then_inc(c_tr, 1)
        end_phase(prep)

        def mm4(ps, lhs, rhs):
            for k in range(DK):
                last = nc.tensor.matmul(ps, lhs[:, k, :], rhs[:, k, :], start=(k == 0), stop=(k == DK - 1))
            return last

        def tr4(ps, rows, n=DK):
            for k in range(n):
                last = nc.tensor.transpose(ps[:, k * P:(k + 1) * P], rows[:, k * P:(k + 1) * P], ident[:])
            return last

        pa = ExitStack()
        xa = sb("xa", [P, 4, D], F32, pa)
        st6 = sb("st6", [P, 4, 6], F32, pa)
        mv = sb("mv", [P, 2, 2], F32, pa)
        ve = sb("ve", [P, 2, 1], F32, pa)
        rs = sb("rs", [P, 2, 1], F32, pa)
        nm = sb("nm", [P, 2, 1], F32, pa)
        xn = sb("xn", [P, 2, D], F32, pa)
        xT = sb("xT", [P, 2, DK, P], F32, pa)
        xle = sb("xle", [P, 4, XE], F32, pa)
        xr = sb("xr", [P, 4, D], F32, pa)
        mm = sb("mm", [P, 2, D], F32, pa)
        la = sb("la", [P, 2, D], F32, pa)
        ahold = sb("ahold", [P, 4], F32, pa)
        a_ld, a_st, a_sr = sems("a_ld", 4), sems("a_st", 4), sems("a_sr", 4)
        (a_bn, a_mv, a_ve, a_rs, a_nm, a_sc, a_norm, a_tr, a_xT, a_mm, a_xl, a_xr, a_m, a_lr, a_la, a_al, a_one, a_dis) = (
            sem("a_" + n) for n in ("bn", "mv", "ve", "rs", "nm", "sc", "norm", "tr", "xT", "mm", "xl", "xr", "m",
                                    "lr", "la", "al", "one", "dis"))

        def heads(a, w=C):
            return a.rearrange("p (h c) -> p h c", h=H)[:, :, 0:w]

        def row(a, t, n=P):
            return a[bass.ds(t * P, n), :]

        def ago(g, s, lag):
            return g + (s - lag) // 4, (s - lag) % 4, g * 4 + s - lag

        def since(eng, done, t, lag):
            if not isinstance(t, int) or t >= lag:
                eng.wait_ge(done, t - lag + 1)

        def run(eng, n, steps, peel=2):
            def body(g, s):
                for lag, step in steps:
                    if warm(g, s, lag, 4):
                        step(*ago(g, s, lag))

            stream(eng, n, 4, body, peel)
            for t in range(n, n + max(lag for lag, _ in steps)):
                for lag, step in steps:
                    if t - lag < n:
                        step(*ago(0, t, lag))

        with nc.Block() as block:
            @block.sync
            def _(sp):
                def load(g, s, t):
                    since(sp, a_norm, t, 4)
                    n = TAIL if isinstance(g, int) and t == NT - 1 else P
                    sp.dma_start(xa[0:n, s, :], row(x, t, n)).then_inc(a_ld[s], 16)

                def store(g, s, t):
                    sp.wait_ge(a_xl, t + 1)
                    sp.dma_start(row(XLE, t), xle[:, s, :]).then_inc(a_st[s], 16)
                    sp.wait_ge(a_xr, t + 1)
                    sp.dma_start(row(XR, t), xr[:, s, :]).then_inc(a_sr[s], 16)

                def clear(g, s, t):
                    sp.dma_start(row(AGG, t), zin[:]).then_inc(h_init, 16)
                    sp.dma_start(row(AG2, t), zin[:, 0:D]).then_inc(h_init, 16)

                run(sp, NT, ((0, load), (0, clear), (5, store)))
                sp.wait_ge(w_rest, 10 * 16)
                sp.wait_ge(h_init, 32 * NT)
                for s in range(4):
                    sp.wait_ge(a_st[s], 16 * ((NT + 3 - s) // 4))
                    sp.wait_ge(a_sr[s], 16 * ((NT + 3 - s) // 4))

            @block.gpsimd
            def _(pool):
                def root(g, s, t):
                    h = s % 2
                    pool.wait_ge(a_mv, t + 1)
                    since(pool, a_norm, t, 2)
                    pool.tensor_tensor(ve[:, h, :], mv[:, h, 1:2], epst[:], ALU.add).then_inc(a_ve, 1)
                    pool.wait_ge(a_ve, t + 1)
                    pool.tensor_tensor(rs[:, h, :], ve[:, h, :], mhalf[:, 0:1], ALU.pow).then_inc(a_rs, 1)
                    pool.wait_ge(a_rs, t + 1)
                    pool.tensor_tensor(nm[:, h, :], mv[:, h, 0:1], rs[:, h, :], ALU.mult).then_inc(a_nm, 1)
                    pool.wait_ge(a_nm, t + 1)
                    pool.tensor_tensor(xsc[:, bass.ds(t, 1), 0], minus1[:], nm[:, h, :], ALU.subtract)
                    pool.tensor_tensor(xsc[:, bass.ds(t, 1), 1], rs[:, h, :], one[:], ALU.add).then_inc(a_sc, 1)
                    pool.tensor_tensor(dis[:, bass.ds(t, 1)], deg1[:, bass.ds(t, 1)], mhalf[:, 0:1], ALU.pow)\
                        .then_inc(a_dis, 1)

                def att_mul(g, s, t):
                    h = s % 2
                    pool.wait_ge(a_lr, t + 1)
                    since(pool, a_al, t, 2)
                    pool.tensor_tensor(la[:, h, :], mm[:, h, :], att_b[:], ALU.mult).then_inc(a_la, 1)

                pool.wait_ge(w_att, 16)
                run(pool, NT, ((0, root), (4, att_mul)))
                pool.wait_ge(a_sc, NT)
                pool.wait_ge(a_dis, NT)

            @block.vector
            def _(dve):
                nc.vector.memset(xle[:], 1.0).then_inc(a_one, 1)

                def stats(g, s, t):
                    dve.wait_ge(a_ld[s], 16 * (g + 1))
                    nc.vector.bn_stats(st6[:, s, :], xa[:, s, :]).then_inc(a_bn, 1)

                def norm(g, s, t):
                    h = s % 2
                    dve.wait_ge(a_rs, t + 1)
                    since(dve, a_tr, t, 2)
                    nc.vector.tensor_scalar(xn[:, h, :], xa[:, s, :], mv[:, h, 0:1], rs[:, h, :],
                                            ALU.subtract, ALU.mult).then_inc(a_norm, 1)

                def gather_stats(g, s, t):
                    since(dve, a_nm, t, 2)
                    dve.wait_ge(a_bn, t + 1)
                    nc.vector.memset(ahold[:, s:s + 1], 0.0)
                    nc.vector.bn_aggr(mv[:, s % 2, :], st6[:, s, :]).then_inc(a_mv, 1)

                def add(g, s, t):
                    h = s % 2
                    dve.wait_ge(a_mm, t + 1)
                    since(dve, a_la, t, 2)
                    if not isinstance(t, int) or t >= 4:
                        dve.wait_ge(a_sr[s], 16 * g)
                    nc.vector.tensor_copy(xr[:, s, :], bank[4 + h]).then_inc(a_xr, 1)
                    dve.wait_ge(a_xl, t + 1)
                    dve.wait_ge(a_xr, t + 1)
                    nc.vector.tensor_tensor(heads(mm[:, h, :]), heads(xle[:, s, :]), heads(xr[:, s, :]), ALU.add)\
                        .then_inc(a_m, 1)
                    dve.wait_ge(a_m, t + 1)
                    nc.vector.scalar_tensor_tensor(mm[:, h, :], mm[:, h, :], SLOPE, mm[:, h, :],
                                                   ALU.mult, ALU.max).then_inc(a_lr, 1)

                def logit(g, s, t):
                    dve.wait_ge(a_la, t + 1)
                    nc.vector.tensor_reduce(selfa[:, bass.ds(t, 1), :].rearrange("p t h -> p (t h)"),
                                            heads(la[:, s % 2, :]), AX.X, ALU.add).then_inc(a_al, 1)

                run(dve, NT, ((0, stats), (1, norm), (0, gather_stats), (3, add), (5, logit)))
                dve.wait_ge(a_al, NT)

            @block.tensor
            def _(pe):
                def project(g, s, t):
                    h = s % 2
                    pe.wait_ge(a_xT, t + 1)
                    since(pe, a_xl, t, 2)
                    since(pe, a_xr, t, 2)
                    mm4(bank[2 + h], xT[:, h, :, :], wl)
                    mm4(bank[4 + h], xT[:, h, :, :], wr).then_inc(a_mm, 1)

                def turn(g, s, t):
                    h = s % 2
                    pe.wait_ge(a_norm, t + 1)
                    tr4(bank[h], xn[:, h, :]).then_inc(a_tr, 1)

                pe.wait_ge(w_proj, 32)
                run(pe, NT, ((1, turn), (2, project)))

            @block.scalar
            def _(act):
                act.wait_ge(a_one, 1)

                def copy(g, s, t):
                    h = s % 2
                    act.wait_ge(a_tr, t + 1)
                    since(act, a_mm, t, 2)
                    act.activation(xT[:, h, :, :].rearrange("p k n -> p (k n)"), bank[h], ACT.Copy)\
                        .then_inc(a_xT, 1)

                def evac(g, s, t):
                    h = s % 2
                    act.wait_ge(a_mm, t + 1)
                    since(act, a_m, t, 4)
                    if not isinstance(t, int) or t >= 4:
                        act.wait_ge(a_st[s], 16 * g)
                    act.activation(heads(xle[:, s, :], CE)[:, :, 0:C], heads(bank[2 + h]), ACT.Copy).then_inc(a_xl, 1)

                run(act, NT, ((1, copy), (3, evac)))
        end_phase(pa)

        pb = ExitStack()
        gl = sb("gl", [P, 4, XE], F32, pb)
        gr = sb("gr", [P, 4, D], F32, pb)
        md = sb("md", [P, 4, P], F32, pb)
        rst = sb("rst", [H, 4, 2 * P], F32, pb)
        me = sb("me", [P, 2, D], F32, pb)
        al = sb("al", [P, 2, H], F32, pb)
        aT = sb("aT", [H, 2, P], F32, pb)
        pf = sb("pf", [H, 2, P], F32, pb)
        mx = sb("mx", [P, 2, P], F32, pb)
        dd = sb("dd", [H, 2, P], F32, pb)
        ea = sb("ea", [P, 2, P], F32, pb)
        sm = sb("sm", [P, 2, P], F32, pb)
        vv = sb("vv", [P, 2, XE], F32, pb)
        eo = sb("eo", [P, 4, AW], F32, pb)
        b_gl, b_gr, b_md, b_sc = sems("b_gl", 4), sems("b_gr", 4), sems("b_md", 4), sems("b_sc", 4)
        b_h0, b_h1, b_i2 = sem("b_h0"), sem("b_h1"), sem("b_i2")
        (b_0, b_ix, b_m, b_lr, b_la, b_al, b_at, b_ac, b_pf, b_mx, b_d, b_e, b_et, b_S, b_v, b_s, b_car, b_out) = (
            sem("b_" + n) for n in ("0", "ix", "m", "lr", "la", "al", "at", "ac", "pf", "mx", "d", "e", "et", "S",
                                    "v", "s", "car", "out"))

        with nc.Block() as block:
            @block.sync
            def _(sp):
                def body(g, s):
                    t = g * 4 + s
                    if warm(g, s, 4, 4):
                        sp.wait_ge(b_v, t - 3)
                    sp.dma_start(md[:, s, :], MDR[bass.ds(t, 1), :].to_broadcast([P, P])).then_inc(b_md[s], 16)
                    sp.dma_start(rst[:, s, :], RRR[bass.ds(t, 1), :].to_broadcast([H, 2 * P]))\
                        .then_inc(b_md[s], 16)

                stream(sp, ET, 4, body, 2)

            @block.gpsimd
            def _(pool):
                def scatter(g, s, t):
                    if not isinstance(t, int) or t >= 4:
                        pool.wait_ge(b_sc[s], 16 * g)
                    pool.tensor_copy(slot[:, s, 2:3], idx[:, 2, bass.ds(t, 1)]).then_inc(b_i2, 1)
                    pool.wait_ge(b_i2, t + 1)
                    pool.wait_ge(b_out, t + 1)
                    hold(pool, 1, s, b_h1, t)
                    pool.indirect_dma_start(AGG, bass.IndirectOffsetOnAxis(slot[:, s, 2:3], 0), eo[:, s, :], None,
                                            bounds_check=NP - 1, oob_is_err=False).then_inc(b_sc[s], 16)

                def gather(g, s, t):
                    since(pool, b_v, t, 4)
                    pool.tensor_copy(slot[:, s, 0:2], idx[:, 0:2, bass.ds(t, 1)].rearrange("p a t -> p (a t)"))\
                        .then_inc(b_ix, 1)
                    pool.wait_ge(b_ix, t + 1)
                    pool.wait_ge(b_0, 2)
                    hold(pool, 0, s, b_h0, t)
                    pool.indirect_dma_start(gl[:, s, :], None, XLE, bass.IndirectOffsetOnAxis(slot[:, s, 0:1], 0),
                                            bounds_check=NP - 1, oob_is_err=False).then_inc(b_gl[s], 16)
                    pool.indirect_dma_start(gr[:, s, :], None, XR, bass.IndirectOffsetOnAxis(slot[:, s, 1:2], 0),
                                            bounds_check=NP - 1, oob_is_err=False).then_inc(b_gr[s], 16)

                run(pool, ET, ((0, gather), (5, scatter)), 3)
                for s in range(4):
                    pool.wait_ge(b_sc[s], 16 * ((ET + 3 - s) // 4))

            @block.vector
            def _(dve):
                nc.vector.memset(gl[:], 0.0).then_inc(b_0, 1)
                nc.vector.memset(gr[:], 0.0).then_inc(b_0, 1)
                nc.vector.memset(mx[:], 0.0).then_inc(b_0, 1)
                nc.vector.memset(ea[:], 0.0).then_inc(b_0, 1)
                dve.wait_ge(b_0, 4)

                def both(g, s, t):
                    h = s % 2
                    dve.wait_ge(b_gl[s], 16 * (g + 1))
                    dve.wait_ge(b_gr[s], 16 * (g + 1))
                    nc.vector.tensor_tensor(heads(me[:, h, :]), heads(gl[:, s, :]), heads(gr[:, s, :]), ALU.add)\
                        .then_inc(b_m, 1)

                def leaky(g, s, t):
                    h = s % 2
                    dve.wait_ge(b_m, t + 1)
                    nc.vector.scalar_tensor_tensor(me[:, h, :], me[:, h, :], SLOPE, me[:, h, :],
                                                   ALU.mult, ALU.max).then_inc(b_lr, 1)

                def attend(g, s, t):
                    h = s % 2
                    dve.wait_ge(b_lr, t + 1)
                    nc.vector.tensor_tensor(me[:, h, :], me[:, h, :], att_b[:], ALU.mult).then_inc(b_la, 1)

                def logits(g, s, t):
                    h = s % 2
                    dve.wait_ge(b_la, t + 1)
                    if not isinstance(t, int) or t >= 2:
                        dve.wait_ge(b_at, t - 1)
                    nc.vector.tensor_reduce(al[:, h, :], heads(me[:, h, :]), AX.X, ALU.add).then_inc(b_al, 1)

                def turned(g, s, t):
                    h = s % 2
                    dve.wait_ge(b_at, t + 1)
                    if isinstance(t, int) and t == 0:
                        nc.vector.memset(aT[:, h, 0:1], 0.0)
                    else:
                        dve.wait_ge(b_mx, t)
                        nc.vector.tensor_copy(aT[:, h, 0:1], mx[0:H, 1 - h, P - 1:P])
                    nc.vector.tensor_copy(aT[:, h, 1:P], bank[h][0:H, 1:P]).then_inc(b_ac, 1)

                def prefix(g, s, t):
                    h = s % 2
                    dve.wait_ge(b_md[s], 32 * (g + 1))
                    dve.wait_ge(b_ac, t + 1)
                    nc.vector.tensor_tensor_scan(pf[:, h, :], rst[:, s, 0:P], aT[:, h, :], 0.0,
                                                 ALU.add, ALU.max).then_inc(b_pf, 1)

                def maxima(g, s, t):
                    h = s % 2
                    dve.wait_ge(b_pf, t + 1)
                    if not isinstance(t, int) or t >= 2:
                        dve.wait_ge(b_et, t - 1)
                    nc.vector.tensor_tensor_scan(mx[0:H, h, ::-1], rst[:, s, 2 * P - 1:P - 1:-1], pf[:, h, ::-1], 0.0,
                                                 ALU.add, ALU.max).then_inc(b_mx, 1)

                def below(g, s, t):
                    h = s % 2
                    dve.wait_ge(b_mx, t + 1)
                    if not isinstance(t, int) or t >= 2:
                        dve.wait_ge(b_e, t - 1)
                    nc.vector.tensor_tensor(dd[:, h, :], aT[:, h, :], mx[0:H, h, :], ALU.subtract).then_inc(b_d, 1)

                def same_run(g, s, t):
                    h = s % 2
                    if not isinstance(t, int) or t >= 2:
                        dve.wait_ge(b_s, t - 1)
                    nc.vector.tensor_scalar(sm[:, h, :], md[:, s, :], kd[:, bass.ds(t, 1)], None,
                                            ALU.is_equal).then_inc(b_S, 1)

                def weigh(g, s, t):
                    h = s % 2
                    dve.wait_ge(b_et, t + 1)
                    if not isinstance(t, int) or t >= 2:
                        dve.wait_ge(b_s, t - 1)
                    if not isinstance(t, int) or t >= 1:
                        dve.wait_ge(b_car, t)
                    nc.vector.tensor_tensor(heads(vv[:, h, :], CE), heads(gl[:, s, :], CE),
                                            bank[2 + h][:, 0:H].unsqueeze(2).to_broadcast([P, H, CE]),
                                            ALU.mult).then_inc(b_v, 1)

                run(dve, ET, ((2, weigh), (1, turned), (0, both), (1, prefix), (0, leaky), (1, maxima), (1, same_run),
                              (1, below), (0, attend), (0, logits)), 2)

            @block.tensor
            def _(pe):
                def alphas(g, s, t):
                    h = s % 2
                    pe.wait_ge(b_al, t + 1)
                    if not isinstance(t, int) or t >= 2:
                        pe.wait_ge(b_ac, t - 1)
                    nc.tensor.transpose(bank[h][0:H, 0:P], al[:, h, :], ident[:]).then_inc(b_at, 1)

                def weights(g, s, t):
                    h = s % 2
                    pe.wait_ge(b_e, t + 1)
                    if not isinstance(t, int) or t >= 2:
                        pe.wait_ge(b_out, t - 1)
                    nc.tensor.transpose(bank[2 + h][:, 0:P], ea[:, h, :], ident[:])
                    nc.tensor.transpose(bank[2 + h][:, P:2 * P], mx[:, h, :], ident[:]).then_inc(b_et, 1)

                def sums(g, s, t):
                    h = s % 2
                    pe.wait_ge(b_S, t + 1)
                    pe.wait_ge(b_v, t + 1)
                    for a in range(2):
                        last = nc.tensor.matmul(pair[h][:, a, :], sm[:, h, :], vv[:, h, a * XE // 2:(a + 1) * XE // 2],
                                                start=True, stop=True)
                    last.then_inc(b_s, 1)

                run(pe, ET, ((2, sums), (1, weights), (0, alphas)), 2)

            @block.scalar
            def _(act):
                act.wait_ge(b_0, 4)

                def expo(g, s, t):
                    h = s % 2
                    act.wait_ge(b_d, t + 1)
                    if not isinstance(t, int) or t >= 2:
                        act.wait_ge(b_et, t - 1)
                    act.activation(ea[0:H, h, :], dd[:, h, :], ACT.Exp).then_inc(b_e, 1)

                def results(g, s, t):
                    h = s % 2
                    act.wait_ge(b_s, t + 1)
                    if not (isinstance(t, int) and t == ET - 1):
                        act.wait_ge(b_m, t + 2)
                        act.activation(gl[0:1, (s + 1) % 4, :].rearrange("p (a c) -> p a c", a=2),
                                       pair[h][0:1, :, :], ACT.Copy).then_inc(b_car, 1)
                    if not isinstance(t, int) or t >= 4:
                        act.wait_ge(b_sc[s], 16 * g)
                    act.activation(eo[:, s, 0:XE].rearrange("p (a c) -> p a c", a=2), pair[h], ACT.Copy)
                    act.activation(eo[:, s, XE:AW], bank[2 + h][:, P:P + H], ACT.Copy).then_inc(b_out, 1)

                run(act, ET, ((1, expo), (2, results)))
        end_phase(pb)

        pc = ExitStack()
        xi = sb("xi", [P, 4, D], F32, pc)
        ai = sb("ai", [P, 4, AW], F32, pc)
        li = sb("li", [P, 4, XE], F32, pc)
        mxn = sb("mxn", [P, 2, H], F32, pc)
        df = sb("df", [P, 2, 2, H], F32, pc)
        fe = sb("fe", [P, 2, 2, H], F32, pc)
        rd = sb("rd", [P, 2, H], F32, pc)
        oc = sb("oc", [P, 2, D], F32, pc)
        mi = sb("mi", [P, 2, D], F32, pc)
        xx = sb("xx", [P, 4, D], F32, pc)
        x1 = sb("x1", [P, 4, D], F32, pc)
        cst = sb("cst", [P, 2, 6], F32, pc)
        cmv = sb("cmv", [P, 2, 2], F32, pc)
        cve = sb("cve", [P, 2, 1], F32, pc)
        crs = sb("crs", [P, 2, 1], F32, pc)
        n1 = sb("n1", [P, 2, D], F32, pc)
        n1T = sb("n1T", [P, 2, DK, P], F32, pc)
        hb = sb("hb", [P, 2, FC + NE], F32, pc)
        m8 = sb("m8", [P, 2, 8], F32, pc)
        i8 = sb("i8", [P, 2, 8], U32, pc)
        ix = sb("ix", [P, 2, 1], F32, pc)
        hm = sb("hm", [P, 2, FC + P], F32, pc)
        hT = sb("hT", [P, 2, FC // P, P], F32, pc)
        hTb = sb("hTb", [P, 2, P], BF16, pc)
        b2r = sb("b2r", [P, D], F32, pc)
        b2m = sb("b2m", [P, D], BF16, pc)
        x2 = sb("x2", [P, 4, D], F32, pc)
        st2 = sb("st2", [P, 2, 6], F32, pc)
        mv2 = sb("mv2", [P, 2, 2], F32, pc)
        ve2 = sb("ve2", [P, 2, 1], F32, pc)
        rs2 = sb("rs2", [P, 2, 1], F32, pc)
        n2 = sb("n2", [P, 2, D], F32, pc)
        n2T = sb("n2T", [P, 2, DK, P], F32, pc)
        gb = sb("gb", [P, 2, D], F32, pc)
        gs = sb("gs", [P, 4, D], F32, pc)
        c_hold = sb("c_hold", [P, 4, 2], F32, pc)
        c_ld, c_sx, c_sg = sems("c_ld", 4), sems("c_sx", 4), sems("c_sg", 4)
        (c_mn, c_df, c_f, c_t1, c_t0, c_t2, c_s, c_ds, c_den, c_rd, c_w, c_o, c_mi, c_ex, c_xx, c_px, c_x1, c_bn, c_mv, c_ve, c_rs,
         c_n1, c_tr1, c_n1T, c_up, c_hb, c_m8, c_i8, c_ix, c_oh, c_hm, c_trh, c_hT, c_dn, c_x2, c_bn2, c_mv2, c_ve2,
         c_rs2, c_n2, c_tr2, c_n2T, c_g, c_gb, c_gs, c_b2) = (
            sem("c_" + n) for n in ("mn df f t1 t0 t2 s ds den rd w o mi ex xx px x1 bn mv ve rs n1 tr1 n1T up hb m8 i8 ix "
                                    "oh hm trh hT dn x2 bn2 mv2 ve2 rs2 n2 tr2 n2T g gb gs b2").split())

        with nc.Block() as block:
            @block.sync
            def _(sp):
                def store_x2(g, s, t):
                    sp.wait_ge(c_x2, t + 1)
                    sp.dma_start(row(X2, t), x2[:, s, :]).then_inc(c_sx[s], 16)

                def store_g(g, s, t):
                    sp.wait_ge(c_gs, t + 1)
                    sp.dma_start(row(GR, t), gs[:, s, :]).then_inc(c_sg[s], 16)

                def load(g, s, t):
                    since(sp, c_xx, t, 4)
                    since(sp, c_o, t, 4)
                    n = TAIL if isinstance(g, int) and t == NT - 1 else P
                    sp.dma_start(xi[0:n, s, :], row(x, t, n)).then_inc(c_ld[s], 16)
                    sp.dma_start(ai[:, s, :], row(AGG, t)).then_inc(c_ld[s], 16)
                    sp.dma_start(li[:, s, :], row(XLE, t)).then_inc(c_ld[s], 16)

                run(sp, NT, ((0, load), (8, store_x2), (11, store_g)), 3)
                for s in range(4):
                    sp.wait_ge(c_sx[s], 16 * ((NT + 3 - s) // 4))
                    sp.wait_ge(c_sg[s], 16 * ((NT + 3 - s) // 4))

            @block.gpsimd
            def _(pool):
                def self_part(g, s, t):
                    h = s % 2
                    own = heads(li[:, s, :], CE)[:, :, 0:C]
                    pool.wait_ge(c_ld[s], 48 * (g + 1))
                    pool.wait_ge(c_w, t + 1)
                    pool.tensor_tensor(own, own, fe[:, h, 1, :].unsqueeze(2).to_broadcast([P, H, C]), ALU.mult)\
                        .then_inc(c_t0, 1)
                    pool.wait_ge(c_t0, t + 1)
                    pool.tensor_tensor(own, own, heads(gb_b[:]), ALU.add).then_inc(c_t2, 1)

                def add_exp(g, s, t):
                    pool.wait_ge(c_xx, t + 1)
                    pool.wait_ge(c_ex, t + 1)
                    pool.tensor_tensor(xx[:, s, :], xx[:, s, :], mi[:, s % 2, :], ALU.add).then_inc(c_px, 1)

                def root(t, h, mv_, ve_, rs_, d_mv, d_ve, d_rs, d_n):
                    pool.wait_ge(d_mv, t + 1)
                    pool.tensor_tensor(ve_[:, h, :], mv_[:, h, 1:2], epst[:], ALU.add).then_inc(d_ve, 1)
                    since(pool, d_n, t, 2)
                    pool.wait_ge(d_ve, t + 1)
                    pool.tensor_tensor(rs_[:, h, :], ve_[:, h, :], mhalf[:, 0:1], ALU.pow).then_inc(d_rs, 1)

                def root1(g, s, t):
                    root(t, s % 2, cmv, cve, crs, c_mv, c_ve, c_rs, c_n1)

                def root2(g, s, t):
                    root(t, s % 2, mv2, ve2, rs2, c_mv2, c_ve2, c_rs2, c_n2)

                run(pool, NT, ((1, self_part), (3, root1), (6, root2), (2, add_exp)), 3)

            @block.vector
            def _(dve):
                nc.vector.tensor_copy(b2p[:], b2[:]).then_inc(c_b2, 1)
                dve.wait_ge(c_b2, 1)
                nc.vector.tensor_tensor(b2r[:], b2[:], b2p[:], ALU.subtract).then_inc(c_b2, 1)
                dve.wait_ge(c_b2, 2)
                nc.vector.tensor_copy(b2m[:], b2r[:]).then_inc(c_b2, 1)
                dve.wait_ge(c_b2, 3)
                nc.vector.tensor_copy(b2p[32:64, :], b2m[32:64, :]).then_inc(c_b2, 1)
                nc.vector.tensor_tensor(b2r[64:96, :], b2r[64:96, :], b2m[64:96, :], ALU.subtract).then_inc(c_b2, 1)
                dve.wait_ge(c_b2, 5)
                nc.vector.tensor_copy(b2p[64:96, :], b2r[64:96, :]).then_inc(c_b2, 1)

                def larger(g, s, t):
                    h = s % 2
                    dve.wait_ge(c_ld[s], 48 * (g + 1))
                    own = selfa[:, bass.ds(t, 1), :].rearrange("p t h -> p (t h)")
                    nc.vector.tensor_tensor(mxn[:, h, :], ai[:, s, XE:AW], own, ALU.max).then_inc(c_mn, 1)

                def below(g, s, t):
                    h = s % 2
                    own = selfa[:, bass.ds(t, 1), :].rearrange("p t h -> p (t h)")
                    since(dve, c_f, t, 2)
                    dve.wait_ge(c_mn, t + 1)
                    nc.vector.tensor_tensor(df[:, h, 0, :], ai[:, s, XE:AW], mxn[:, h, :], ALU.subtract)
                    nc.vector.tensor_tensor(df[:, h, 1, :], own, mxn[:, h, :], ALU.subtract).then_inc(c_df, 1)

                def listed_weight(g, s, t):
                    h = s % 2
                    dve.wait_ge(c_f, t + 1)
                    nc.vector.tensor_tensor(rd[:, h, :], heads(ai[:, s, 0:XE], CE)[:, :, C:CE].rearrange(
                        "p h c -> p (h c)"), fe[:, h, 0, :], ALU.mult).then_inc(c_s, 1)

                def weight_sum(g, s, t):
                    h = s % 2
                    dve.wait_ge(c_s, t + 1)
                    nc.vector.tensor_tensor(rd[:, h, :], rd[:, h, :], fe[:, h, 1, :], ALU.add).then_inc(c_ds, 1)

                def guarded(g, s, t):
                    h = s % 2
                    dve.wait_ge(c_ds, t + 1)
                    nc.vector.tensor_scalar_max(rd[:, h, :], rd[:, h, :], 1e-16).then_inc(c_den, 1)

                def inverse(g, s, t):
                    h = s % 2
                    dve.wait_ge(c_den, t + 1)
                    nc.vector.reciprocal(rd[:, h, :], rd[:, h, :]).then_inc(c_rd, 1)

                def shares(g, s, t):
                    h = s % 2
                    dve.wait_ge(c_rd, t + 1)
                    nc.vector.tensor_tensor(fe[:, h, :, :], fe[:, h, :, :],
                                            rd[:, h, :].unsqueeze(1).to_broadcast([P, 2, H]), ALU.mult)\
                        .then_inc(c_w, 1)

                def listed_part(g, s, t):
                    h = s % 2
                    dve.wait_ge(c_w, t + 1)
                    listed = heads(ai[:, s, 0:XE], CE)[:, :, 0:C]
                    nc.vector.tensor_tensor(listed, listed,
                                            fe[:, h, 0, :].unsqueeze(2).to_broadcast([P, H, C]), ALU.mult)\
                        .then_inc(c_t1, 1)

                def average(g, s, t):
                    h = s % 2
                    dve.wait_ge(c_t1, t + 1)
                    dve.wait_ge(c_t2, t + 1)
                    since(dve, c_x1, t, 2)
                    nc.vector.tensor_tensor(heads(oc[:, h, :]), heads(ai[:, s, 0:XE], CE)[:, :, 0:C],
                                            heads(li[:, s, :], CE)[:, :, 0:C], ALU.add).then_inc(c_o, 1)

                def elu(g, s, t):
                    h = s % 2
                    dve.wait_ge(c_px, t + 1)
                    nc.vector.scalar_tensor_tensor(x1[:, s, :], oc[:, h, :], 0.0, xx[:, s, :],
                                                   ALU.max, ALU.add).then_inc(c_x1, 1)

                def sums1(g, s, t):
                    h = s % 2
                    dve.wait_ge(c_x1, t + 1)
                    nc.vector.bn_stats(cst[:, h, :], x1[:, s, :]).then_inc(c_bn, 1)

                def mean1(g, s, t):
                    h = s % 2
                    dve.wait_ge(c_bn, t + 1)
                    nc.vector.memset(c_hold[:, s, 0:1], 0.0)
                    nc.vector.bn_aggr(cmv[:, h, :], cst[:, h, :]).then_inc(c_mv, 1)

                def norm1(g, s, t):
                    h = s % 2
                    dve.wait_ge(c_rs, t + 1)
                    since(dve, c_tr1, t, 2)
                    nc.vector.tensor_scalar(n1[:, h, :], x1[:, s, :], cmv[:, h, 0:1], crs[:, h, :],
                                            ALU.subtract, ALU.mult).then_inc(c_n1, 1)

                def hidden(g, s, t):
                    h = s % 2
                    dve.wait_ge(c_up, t + 1)
                    nc.vector.tensor_tensor(hb[:, h, :], bank[1][:, 0:FC + NE], b1b[:], ALU.add).then_inc(c_hb, 1)

                def best(g, s, t):
                    h = s % 2
                    dve.wait_ge(c_hb, t + 1)
                    nc.vector.memset(c_hold[:, s, 1:2], 0.0)
                    nc.vector.max(m8[:, h, :], hb[:, h, FC:FC + NE]).then_inc(c_m8, 1)

                def its_number(g, s, t):
                    h = s % 2
                    dve.wait_ge(c_m8, t + 1)
                    nc.vector.memset(c_hold[:, s, 1:2], 0.0)
                    nc.vector.max_index(i8[:, h, :], m8[:, h, :], hb[:, h, FC:FC + NE]).then_inc(c_i8, 1)

                def number_f(g, s, t):
                    h = s % 2
                    dve.wait_ge(c_i8, t + 1)
                    nc.vector.tensor_copy(ix[:, h, :], i8[:, h, 0:1]).then_inc(c_ix, 1)

                def one_hot(g, s, t):
                    h = s % 2
                    since(dve, c_trh, t, 2)
                    dve.wait_ge(c_ix, t + 1)
                    nc.vector.tensor_scalar(hm[:, h, FC:FC + P], iota3[:], ix[:, h, :], None,
                                            ALU.is_equal).then_inc(c_oh, 1)

                def routed(g, s, t):
                    h = s % 2
                    dve.wait_ge(c_oh, t + 1)
                    nc.vector.scalar_tensor_tensor(
                        hm[:, h, 0:FC].rearrange("p (e f) -> p e f", e=NE),
                        hb[:, h, 0:FC].rearrange("p (e f) -> p e f", e=NE), 0.0,
                        hm[:, h, FC:FC + NE].unsqueeze(2).to_broadcast([P, NE, FH]), ALU.max, ALU.mult)\
                        .then_inc(c_hm, 1)

                def add_experts(g, s, t):
                    h = s % 2
                    if not isinstance(t, int) or t >= 4:
                        dve.wait_ge(c_sx[s], 16 * g)
                    dve.wait_ge(c_dn, t + 1)
                    nc.vector.tensor_tensor(x2[:, s, :], bank[3], x1[:, s, :], ALU.add).then_inc(c_x2, 1)

                def sums2(g, s, t):
                    h = s % 2
                    dve.wait_ge(c_x2, t + 1)
                    nc.vector.bn_stats(st2[:, h, :], x2[:, s, :]).then_inc(c_bn2, 1)

                def mean2(g, s, t):
                    h = s % 2
                    dve.wait_ge(c_bn2, t + 1)
                    nc.vector.memset(c_hold[:, s, 0:1], 0.0)
                    nc.vector.bn_aggr(mv2[:, h, :], st2[:, h, :]).then_inc(c_mv2, 1)

                def norm2(g, s, t):
                    h = s % 2
                    dve.wait_ge(c_rs2, t + 1)
                    since(dve, c_tr2, t, 2)
                    nc.vector.tensor_scalar(n2[:, h, :], x2[:, s, :], mv2[:, h, 0:1], rs2[:, h, :],
                                            ALU.subtract, ALU.mult).then_inc(c_n2, 1)

                def gcn_bias(g, s, t):
                    h = s % 2
                    dve.wait_ge(c_g, t + 1)
                    since(dve, c_gs, t, 2)
                    nc.vector.tensor_tensor(gb[:, h, :], bank[5], bgb[:], ALU.add).then_inc(c_gb, 1)

                steps = ((4, norm1), (9, gcn_bias), (1, listed_weight), (7, norm2), (1, weight_sum), (3, elu),
                         (1, guarded), (5, hidden), (1, inverse), (3, sums1), (1, shares), (5, best), (3, mean1),
                         (5, its_number), (1, listed_part), (5, number_f), (0, larger), (5, one_hot), (6, add_experts),
                         (5, routed), (0, below), (6, sums2), (2, average), (6, mean2))

                run(dve, NT, steps, 3)

            @block.tensor
            def _(pe):
                pe.wait_ge(c_b2, 6)

                def up(g, s, t):
                    pe.wait_ge(c_n1T, t + 1)
                    mm4(bank[1][:, 0:FC + NE], n1T[:, s % 2, :, :], wc).then_inc(c_up, 1)

                def down(g, s, t):
                    h = s % 2
                    pe.wait_ge(c_hT, t + 1)
                    since(pe, c_x2, t, 1)
                    for k in range(FC // P):
                        nc.tensor.matmul(bank[3], hT[:, h, k, :], w2[:, k, :], start=(k == 0), stop=False)
                    nc.tensor.matmul(bank[3], hTb[:, h, :], b2p[:], start=False, stop=True).then_inc(c_dn, 1)

                def gcn(g, s, t):
                    pe.wait_ge(c_n2T, t + 1)
                    since(pe, c_gb, t, 1)
                    mm4(bank[5], n2T[:, s % 2, :, :], wg).then_inc(c_g, 1)

                def turn2(g, s, t):
                    pe.wait_ge(c_n2, t + 1)
                    tr4(bank[4], n2[:, s % 2, :]).then_inc(c_tr2, 1)

                def turn_h(g, s, t):
                    h = s % 2
                    pe.wait_ge(c_hm, t + 1)
                    tr4(bank[2], hm[:, h, :], FC // P + 1).then_inc(c_trh, 1)

                def turn1(g, s, t):
                    pe.wait_ge(c_n1, t + 1)
                    tr4(bank[0], n1[:, s % 2, :]).then_inc(c_tr1, 1)

                steps = ((5, up), (6, down), (4, turn1), (8, gcn), (5, turn_h), (7, turn2))

                run(pe, NT, steps, 3)

            @block.scalar
            def _(act):
                def scaled(g, s, t):
                    act.wait_ge(c_gb, t + 1)
                    if not isinstance(t, int) or t >= 4:
                        act.wait_ge(c_sg[s], 16 * g)
                    act.activation(gs[:, s, :], gb[:, s % 2, :], ACT.Copy, scale=dis[:, bass.ds(t, 1)])\
                        .then_inc(c_gs, 1)

                def copy2(g, s, t):
                    act.wait_ge(c_tr2, t + 1)
                    since(act, c_g, t, 2)
                    act.activation(n2T[:, s % 2, :, :].rearrange("p k n -> p (k n)"), bank[4], ACT.Copy)\
                        .then_inc(c_n2T, 1)

                def copy_h(g, s, t):
                    h = s % 2
                    act.wait_ge(c_trh, t + 1)
                    since(act, c_dn, t, 2)
                    act.activation(hT[:, h, :, :].rearrange("p k n -> p (k n)"), bank[2][:, 0:FC], ACT.Copy)
                    act.activation(hTb[:, h, :], bank[2][:, FC:FC + P], ACT.Copy).then_inc(c_hT, 1)

                def copy1(g, s, t):
                    act.wait_ge(c_tr1, t + 1)
                    since(act, c_up, t, 2)
                    act.activation(n1T[:, s % 2, :, :].rearrange("p k n -> p (k n)"), bank[0], ACT.Copy)\
                        .then_inc(c_n1T, 1)

                def exp_min(g, s, t):
                    h = s % 2
                    act.wait_ge(c_o, t + 1)
                    since(act, c_px, t, 2)
                    act.activation(mi[:, h, :], oc[:, h, :], ACT.Relu, scale=-1.0).then_inc(c_mi, 1)
                    act.wait_ge(c_mi, t + 1)
                    act.activation(mi[:, h, :], mi[:, h, :], ACT.Exp, scale=-1.0).then_inc(c_ex, 1)

                def residual(g, s, t):
                    act.wait_ge(c_ld[s], 48 * (g + 1))
                    since(act, c_x1, t, 4)
                    act.activation(xx[:, s, :], xi[:, s, :], ACT.Identity, scale=xsc[:, bass.ds(t, 1), 1],
                                   bias=xsc[:, bass.ds(t, 1), 0]).then_inc(c_xx, 1)

                def exp_shift(g, s, t):
                    h = s % 2
                    act.wait_ge(c_df, t + 1)
                    since(act, c_t1, t, 2)
                    since(act, c_t2, t, 2)
                    act.activation(fe[:, h, :, :], df[:, h, :, :], ACT.Exp).then_inc(c_f, 1)

                steps = ((0, residual), (9, scaled), (4, copy1), (0, exp_shift), (2, exp_min), (5, copy_h), (7, copy2))

                run(act, NT, steps, 4)
        end_phase(pc)

        pd = ExitStack()
        gg = sb("gg", [P, 4, D], F32, pd)
        md2 = sb("md2", [P, 4, P], F32, pd)
        sm2 = sb("sm2", [P, 2, P], F32, pd)
        go = sb("go", [P, 4, D], F32, pd)
        d_ld, d_md, d_sc = sems("d_ld", 4), sems("d_md", 4), sems("d_sc", 4)
        d_car = sems("d_car", 2)
        d_0, d_ix, d_S, d_s0, d_s, d_out, d_h0, d_h1 = (
            sem("d_" + n) for n in ("0", "ix", "S", "s0", "s", "out", "h0", "h1"))

        with nc.Block() as block:
            @block.sync
            def _(sp):
                def body(g, s):
                    t = g * 4 + s
                    since(sp, d_S, t, 4)
                    sp.dma_start(md2[:, s, :], MDR[bass.ds(t, 1), :].to_broadcast([P, P])).then_inc(d_md[s], 16)

                stream(sp, ET, 4, body)

            @block.gpsimd
            def _(pool):
                def scatter(g, s, t):
                    pool.wait_ge(d_out, t + 1)
                    hold(pool, 1, s, d_h1, t)
                    pool.indirect_dma_start(AG2, bass.IndirectOffsetOnAxis(slot[:, s, 2:3], 0), go[:, s, :], None,
                                            bounds_check=NP - 1, oob_is_err=False).then_inc(d_sc[s], 16)

                def gather(g, s, t):
                    pool.wait_ge(d_ix, t + 1)
                    pool.wait_ge(d_0, 1)
                    hold(pool, 0, s, d_h0, t)
                    pool.indirect_dma_start(gg[:, s, :], None, GR, bass.IndirectOffsetOnAxis(slot[:, s, 0:1], 0),
                                            bounds_check=NP - 1, oob_is_err=False).then_inc(d_ld[s], 16)

                run(pool, ET, ((0, gather), (5, scatter)), 3)
                for s in range(4):
                    pool.wait_ge(d_sc[s], 16 * ((ET + 3 - s) // 4))

            @block.vector
            def _(dve):
                nc.vector.memset(gg[:], 0.0).then_inc(d_0, 1)

                def results(g, s, t):
                    dve.wait_ge(d_s, t + 1)
                    if not isinstance(t, int) or t < ET - 1:
                        for a in range(2):
                            dve.wait_ge(d_car[a], t + 1)
                    if not isinstance(t, int) or t >= 4:
                        dve.wait_ge(d_sc[s], 16 * g)
                    nc.vector.tensor_copy(slot[:, s, 2:3], idx[:, 2, bass.ds(t, 1)])
                    nc.vector.tensor_copy(go[:, s, :].rearrange("p (a c) -> p a c", a=2),
                                          psum[:, 2 * (s % 2):2 * (s % 2) + 2, 0:D // 2]).then_inc(d_out, 1)

                def indices(g, s, t):
                    since(dve, d_s, t, 4)
                    nc.vector.tensor_copy(slot[:, s, 0:1], idx[:, 0, bass.ds(t, 1)]).then_inc(d_ix, 1)

                def mask(g, s, t):
                    dve.wait_ge(d_md[s], 16 * (g + 1))
                    since(dve, d_s, t, 2)
                    nc.vector.tensor_scalar(sm2[:, s % 2, :], md2[:, s, :], kd[:, bass.ds(t, 1)], None,
                                            ALU.is_equal).then_inc(d_S, 1)

                run(dve, ET, ((3, mask), (4, results), (0, indices)), 3)

            @block.tensor
            def _(pe):
                def body(g, s):
                    t = g * 4 + s
                    pe.wait_ge(d_S, t + 1)
                    pe.wait_ge(d_ld[s], 16 * (g + 1))
                    since(pe, d_out, t, 2)
                    for a in range(2):
                        since(pe, d_car[a], t, 1)
                        nc.tensor.matmul(bank[2 * (s % 2) + a][:, 0:D // 2], sm2[:, s % 2, :],
                                         gg[:, s, a * D // 2:(a + 1) * D // 2], start=True, stop=True)\
                            .then_inc((d_s0, d_s)[a], 1)

                stream(pe, ET, 4, body)

            @block.scalar
            def _(act):
                def body(g, s):
                    t = g * 4 + s
                    if isinstance(g, int) and t == ET - 1:
                        return
                    n = s + 1
                    act.wait_ge(d_ld[n % 4], 16 * (g + 1 + n // 4))
                    for a in range(2):
                        act.wait_ge((d_s0, d_s)[a], t + 1)
                        act.activation(gg[0:1, n % 4, a * D // 2:(a + 1) * D // 2],
                                       bank[2 * (s % 2) + a][0:1, 0:D // 2], ACT.Copy).then_inc(d_car[a], 1)

                stream(act, ET, 4, body)
        end_phase(pd)

        X3 = nc.dram_tensor("x3_rows", [NP, D], F32).ap()
        XN3 = nc.dram_tensor("n3_rows", [NP, D], F32).ap()
        IDX = nc.dram_tensor("slot_tokens", [(ME * SLOTS + LISTED), P], I32).ap()
        IDXF = IDX.rearrange("r (p o) -> (r p) o", o=1)
        w12 = sb("w12", [P, NT, 2])
        sl3 = sb("sl3", [P, 3, NT], I32)
        mask = sb("mask", [P, 1])
        prow = sb("prow", [P, 1])
        cnt = sb("cnt", [P, ME])
        cbase = sb("cbase", [P, ME])
        selk = sb("selk", [P, NT, 2])
        plk = sb("plk", [P, NT, 2])
        pe_ = ExitStack()
        ex2 = sb("ex2", [P, 4, D], F32, pe_)
        eg = sb("eg", [P, 4, D], F32, pe_)
        ea2 = sb("ea2", [P, 4, D], F32, pe_)
        er = sb("er", [P, 2, D], F32, pe_)
        x3 = sb("x3", [P, 4, D], F32, pe_)
        est = sb("est", [P, 2, 6], F32, pe_)
        emv = sb("emv", [P, 2, 2], F32, pe_)
        eve = sb("eve", [P, 2, 1], F32, pe_)
        ers = sb("ers", [P, 2, 1], F32, pe_)
        n3 = sb("n3", [P, 4, D], F32, pe_)
        n3T = sb("n3T", [P, 2, DK, P], F32, pe_)
        lg = sb("lg", [P, 2, MH * ME], F32, pe_)
        hm8 = sb("hm8", [P, 2, MH, 8], F32, pe_)
        hi8 = sb("hi8", [P, 2, MH, 8], U32, pe_)
        sc8 = sb("sc8", [P, 2, 8], F32, pe_)
        cand = sb("cand", [P, 2, MH], F32, pe_)
        tm8 = sb("tm8", [P, 2, 8], F32, pe_)
        ti8 = sb("ti8", [P, 2, 8], U32, pe_)
        tf = sb("tf", [P, 2, 2], F32, pe_)
        pick = sb("pick", [P, 2, 2, MH], F32, pe_)
        sel = sb("sel", [P, 2, 2], F32, pe_)
        oh = sb("oh", [P, 2, 2, ME], BF16, pe_)
        ohs = sb("ohs", [P, 2, ME], BF16, pe_)
        cum = sb("cum", [P, 2, ME], BF16, pe_)
        pos1 = sb("pos1", [P, 2, ME], F32, pe_)
        junk = sb("junk", [P, 2, 2, ME], F32, pe_)
        place = sb("place", [P, 2, 2], F32, pe_)
        keep = sb("keep", [P, 2, 2], F32, pe_)
        slf = sb("slf", [P, 2, 2], F32, pe_)
        plf = sb("plf", [P, 2, 2], F32, pe_)
        skipi = sb("skipi", [P, ME * SLOTS + LISTED], I32, pe_)
        slot3 = sb("slot3", [P, 4, 3], I32, pe_)
        ehold = sb("ehold", [P, 4, 8], F32, pe_)
        e_ld, e_s3, e_sn, e_id = sems("e_ld", 4), sems("e_s3", 4), sems("e_sn", 4), sems("e_id", 4)
        (e_0, e_y, e_r, e_x3, e_bn, e_mv, e_ve, e_rs, e_n3, e_tr, e_nT, e_lg, e_lc, e_m8, e_i8, e_sc, e_tm, e_ti, e_tf,
         e_pk, e_oh, e_os, e_cu, e_pre, e_p1, e_k0, e_k1, e_ks, e_w, e_i, e_ix, e_hd, e_vm, e_is, e_tot, e_pf) = (
            sem("e_" + n) for n in ("0 y r x3 bn mv ve rs n3 tr nT lg lc m8 i8 sc tm ti tf pk oh os cu pre p1 k0 k1 ks "
                                    "w i ix hd vm is tot pf").split())

        with nc.Block() as block:
            @block.sync
            def _(sp):
                def store(g, s, t):
                    sp.wait_ge(e_x3, t + 1)
                    sp.dma_start(row(X3, t), x3[:, s, :]).then_inc(e_s3[s], 16)
                    sp.wait_ge(e_n3, t + 1)
                    sp.dma_start(row(XN3, t), n3[:, s, :]).then_inc(e_sn[s], 16)

                def body(g, s):
                    t = g * 4 + s
                    since(sp, e_x3, t, 4)
                    sp.dma_start(ex2[:, s, :], row(X2, t)).then_inc(e_ld[s], 16)
                    sp.dma_start(eg[:, s, :], row(GR, t)).then_inc(e_ld[s], 16)
                    sp.dma_start(ea2[:, s, :], row(AG2, t)).then_inc(e_ld[s], 16)
                    if warm(g, s, 4, 4):
                        store(*ago(g, s, 4))

                sp.wait_ge(e_i, 5)
                sp.dma_start(IDX.rearrange("r c -> (r c)").rearrange("(p c) -> p c", p=P), skipi[:])\
                    .then_inc(e_is, 16)
                stream(sp, NT, 4, body, 2)
                for t in range(NT, NT + 4):
                    store(*ago(0, t, 4))
                for s in range(4):
                    sp.wait_ge(e_s3[s], 16 * ((NT + 3 - s) // 4))
                    sp.wait_ge(e_sn[s], 16 * ((NT + 3 - s) // 4))

            @block.gpsimd
            def _(pool):
                pool.iota(sl3[:, 2, :], [[P, NT]], base=0, channel_multiplier=1).then_inc(e_i, 1)
                pool.iota(prow[:], [[0, 1]], base=0, channel_multiplier=1,
                          allow_small_or_imprecise_dtypes=True).then_inc(e_i, 1)
                pool.memset(skipi[:], int(SKIP)).then_inc(e_i, 1)
                pool.memset(mask[:], 1.0).then_inc(e_i, 1)
                pool.wait_ge(e_i, 4)
                pool.affine_select(out=mask[:], in_=mask[:], compare_op=ALU.is_gt, fill=0.0, base=TAIL,
                                   pattern=[[0, 1]], channel_multiplier=-1).then_inc(e_i, 1)
                pool.wait_ge(e_i, 5)

                def enter(g, s, t):
                    pool.wait_ge(e_w, t + 1)
                    if not isinstance(t, int) or t >= 4:
                        pool.wait_ge(e_id[s], 32 * g)
                    pool.tensor_copy(slot3[:, s, :], sl3[:, :, bass.ds(t, 1)].rearrange("p a t -> p (a t)"))\
                        .then_inc(e_ix, 1)
                    pool.wait_ge(e_ix, t + 1)
                    pool.wait_ge(e_is, 16)
                    hold(pool, 0, s, e_hd, t)
                    for k in range(2):
                        pool.indirect_dma_start(IDXF, bass.IndirectOffsetOnAxis(slot3[:, s, k:k + 1], 0),
                                                slot3[:, s, 2:3], None, bounds_check=ME * SLOTS * P - 1,
                                                oob_is_err=False).then_inc(e_id[s], 16)

                def both(g, s, t):
                    pool.wait_ge(e_ld[s], 48 * (g + 1))
                    pool.tensor_tensor(ea2[:, s, :], ea2[:, s, :], eg[:, s, :], ALU.add).then_inc(e_y, 1)

                def root(g, s, t):
                    h = s % 2
                    pool.wait_ge(e_mv, t + 1)
                    pool.tensor_tensor(eve[:, h, :], emv[:, h, 1:2], epst[:], ALU.add).then_inc(e_ve, 1)
                    since(pool, e_n3, t, 2)
                    pool.wait_ge(e_ve, t + 1)
                    pool.tensor_tensor(ers[:, h, :], eve[:, h, :], mhalf[:, 0:1], ALU.pow).then_inc(e_rs, 1)

                run(pool, NT, ((1, root), (0, both), (7, enter)), 3)
                for s in range(4):
                    pool.wait_ge(e_id[s], 32 * ((NT + 3 - s) // 4))

            @block.vector
            def _(dve):
                nc.vector.memset(cum[:], 0.0).then_inc(e_0, 1)
                nc.vector.memset(sc8[:], -BIG).then_inc(e_0, 1)
                dve.wait_ge(e_0, 2)
                dve.wait_ge(e_i, 5)

                def hold_dve(s, k):
                    nc.vector.memset(ehold[:, s, k:k + 1], 0.0)

                def residual(g, s, t):
                    dve.wait_ge(e_ld[s], 48 * (g + 1))
                    h = s % 2
                    dve.wait_ge(e_r, t + 1)
                    if not isinstance(t, int) or t >= 4:
                        dve.wait_ge(e_s3[s], 16 * g)
                    nc.vector.tensor_tensor(x3[:, s, :], er[:, h, :], ex2[:, s, :], ALU.add).then_inc(e_x3, 1)

                def sums(g, s, t):
                    h = s % 2
                    dve.wait_ge(e_x3, t + 1)
                    nc.vector.bn_stats(est[:, h, :], x3[:, s, :]).then_inc(e_bn, 1)

                def mean(g, s, t):
                    h = s % 2
                    dve.wait_ge(e_bn, t + 1)
                    hold_dve(s, 0)
                    nc.vector.bn_aggr(emv[:, h, :], est[:, h, :]).then_inc(e_mv, 1)

                def norm(g, s, t):
                    h = s % 2
                    dve.wait_ge(e_rs, t + 1)
                    since(dve, e_tr, t, 4)
                    if not isinstance(t, int) or t >= 4:
                        dve.wait_ge(e_sn[s], 16 * g)
                    nc.vector.tensor_scalar(n3[:, s, :], x3[:, s, :], emv[:, h, 0:1], ers[:, h, :],
                                            ALU.subtract, ALU.mult).then_inc(e_n3, 1)

                def best_expert(g, s, t):
                    h = s % 2
                    dve.wait_ge(e_lc, t + 1)
                    hold_dve(s, 1)
                    for k in range(MH):
                        last = nc.vector.max(hm8[:, h, k, :], lg[:, h, k * ME:(k + 1) * ME])
                    last.then_inc(e_m8, 1)

                def its_number(g, s, t):
                    h = s % 2
                    dve.wait_ge(e_m8, t + 1)
                    hold_dve(s, 2)
                    for k in range(MH):
                        last = nc.vector.max_index(hi8[:, h, k, :], hm8[:, h, k, :], lg[:, h, k * ME:(k + 1) * ME])
                    last.then_inc(e_i8, 1)
                    nc.vector.tensor_copy(sc8[:, h, 0:MH], hm8[:, h, :, 0]).then_inc(e_sc, 1)

                def number_f(g, s, t):
                    h = s % 2
                    dve.wait_ge(e_i8, t + 1)
                    nc.vector.tensor_copy(cand[:, h, :], hi8[:, h, :, 0]).then_inc(e_sc, 1)

                def best_hashes(g, s, t):
                    h = s % 2
                    dve.wait_ge(e_sc, 2 * t + 2)
                    hold_dve(s, 3)
                    nc.vector.max(tm8[:, h, :], sc8[:, h, :]).then_inc(e_tm, 1)

                def their_numbers(g, s, t):
                    h = s % 2
                    dve.wait_ge(e_tm, t + 1)
                    hold_dve(s, 4)
                    nc.vector.max_index(ti8[:, h, :], tm8[:, h, :], sc8[:, h, :]).then_inc(e_ti, 1)

                def numbers_f(g, s, t):
                    h = s % 2
                    dve.wait_ge(e_ti, t + 1)
                    nc.vector.tensor_copy(tf[:, h, :], ti8[:, h, 0:2]).then_inc(e_tf, 1)

                def chosen(g, s, t):
                    h = s % 2
                    dve.wait_ge(e_tf, t + 1)
                    for k in range(2):
                        last = nc.vector.scalar_tensor_tensor(pick[:, h, k, :], iota[:, 0:MH], tf[:, h, k:k + 1],
                                                              cand[:, h, :], ALU.is_equal, ALU.mult,
                                                              accum_out=sel[:, h, k:k + 1])
                    last.then_inc(e_pk, 1)

                def one_hot(g, s, t):
                    h = s % 2
                    dve.wait_ge(e_pk, t + 1)
                    for k in range(2):
                        last = nc.vector.tensor_scalar(oh[:, h, k, :], iota[:, 0:ME], sel[:, h, k:k + 1], None,
                                                       ALU.is_equal)
                    last.then_inc(e_oh, 1)

                def choices(g, s, t):
                    h = s % 2
                    dve.wait_ge(e_oh, t + 1)
                    if isinstance(t, int) and t == NT - 1:
                        nc.vector.tensor_scalar(oh[:, h, :, :], oh[:, h, :, :], mask[:], None, ALU.mult)\
                            .then_inc(e_vm, 1)
                        dve.wait_ge(e_vm, 1)
                    since(dve, e_pre, t, 1)
                    nc.vector.tensor_tensor(ohs[:, h, :], oh[:, h, 0, :], oh[:, h, 1, :], ALU.add).then_inc(e_os, 1)

                def count_up(g, s, t):
                    h = s % 2
                    dve.wait_ge(e_os, t + 1)
                    nc.vector.tensor_tensor(cum[:, 1 - h, :], cum[:, h, :], ohs[:, h, :], ALU.add).then_inc(e_cu, 1)

                def place_a(g, s, t):
                    h = s % 2
                    dve.wait_ge(e_pre, t + 1)
                    nc.vector.tensor_tensor(pos1[:, h, :], bank[2 + h][:, 0:ME], oh[:, h, 0, :], ALU.add).then_inc(e_p1, 1)
                    nc.vector.scalar_tensor_tensor(junk[:, h, 0, :], bank[2 + h][:, 0:ME], 1.0, oh[:, h, 0, :],
                                                   ALU.mult, ALU.mult, accum_out=place[:, h, 0:1]).then_inc(e_k0, 1)

                def place_b(g, s, t):
                    h = s % 2
                    dve.wait_ge(e_p1, t + 1)
                    nc.vector.scalar_tensor_tensor(junk[:, h, 1, :], pos1[:, h, :], 1.0, oh[:, h, 1, :],
                                                   ALU.mult, ALU.mult, accum_out=place[:, h, 1:2]).then_inc(e_k0, 1)

                def kept(g, s, t):
                    h = s % 2
                    dve.wait_ge(e_k0, 2 * t + 2)
                    nc.vector.tensor_scalar(keep[:, h, :], place[:, h, :], float(CAP), None, ALU.is_lt)\
                        .then_inc(e_k1, 1)
                    nc.vector.scalar_tensor_tensor(slf[:, h, :], sel[:, h, :], float(SLOTS * P), place[:, h, :],
                                                   ALU.mult, ALU.add).then_inc(e_k1, 1)

                def masked(g, s, t):
                    h = s % 2
                    dve.wait_ge(e_k1, 2 * t + 2)
                    if isinstance(t, int) and t == NT - 1:
                        nc.vector.tensor_scalar(keep[:, h, :], keep[:, h, :], mask[:], None, ALU.mult)\
                            .then_inc(e_vm, 1)
                        dve.wait_ge(e_vm, 2)
                    nc.vector.tensor_copy(selk[:, bass.ds(t, 1), :].rearrange("p t a -> p (t a)"), sel[:, h, :])
                    nc.vector.scalar_tensor_tensor(plf[:, h, :], place[:, h, :], -DROPPED, keep[:, h, :],
                                                   ALU.add, ALU.mult).then_inc(e_pf, 1)
                    nc.vector.scalar_tensor_tensor(slf[:, h, :], slf[:, h, :], -DROPPED, keep[:, h, :],
                                                   ALU.add, ALU.mult).then_inc(e_ks, 1)

                def weigh(g, s, t):
                    h = s % 2
                    dve.wait_ge(e_ks, t + 1)
                    dve.wait_ge(e_pf, t + 1)
                    nc.vector.tensor_scalar(plk[:, bass.ds(t, 1), :].rearrange("p t a -> p (t a)"), plf[:, h, :],
                                            DROPPED, None, ALU.add)
                    nc.vector.tensor_scalar(sl3[:, 0:2, bass.ds(t, 1)].rearrange("p a t -> p (a t)"), slf[:, h, :],
                                            DROPPED, None, ALU.add)
                    nc.vector.tensor_scalar(w12[:, bass.ds(t, 1), :].rearrange("p t a -> p (t a)"), keep[:, h, :],
                                            0.5, None, ALU.mult).then_inc(e_w, 1)

                steps = ((4, best_expert), (1, residual), (4, its_number), (1, sums), (4, number_f), (6, place_a),
                         (1, mean), (4, best_hashes), (6, place_b), (4, their_numbers), (6, kept), (6, masked),
                         (4, numbers_f), (6, weigh), (4, chosen), (1, norm), (4, one_hot), (4, choices), (4, count_up))

                run(dve, NT, steps, 3)
                dve.wait_ge(e_w, NT)
                dve.wait_ge(e_tot, 1)
                nc.vector.tensor_copy(cnt[:], bank[2][:, 0:ME]).then_inc(e_tot, 1)
                dve.wait_ge(e_tot, 2)

            @block.tensor
            def _(pe):
                def places(g, s, t):
                    h = s % 2
                    pe.wait_ge(e_os, t + 1)
                    pe.wait_ge(e_cu, t + 1)
                    since(pe, e_w, t, 2)
                    nc.tensor.matmul(bank[2 + h][:, 0:ME], tri[:], ohs[:, h, :], start=True, stop=False)
                    nc.tensor.matmul(bank[2 + h][:, 0:ME], onesb[:], cum[:, h, :], start=False, stop=True)\
                        .then_inc(e_pre, 1)

                def logits(g, s, t):
                    pe.wait_ge(e_nT, t + 1)
                    since(pe, e_lc, t, 1)
                    mm4(bank[1][:, 0:MH * ME], n3T[:, s % 2, :, :], hp).then_inc(e_lg, 1)

                def turn(g, s, t):
                    pe.wait_ge(e_n3, t + 1)
                    since(pe, e_nT, t, 1)
                    tr4(bank[0], n3[:, s, :]).then_inc(e_tr, 1)

                steps = ((3, logits), (5, places), (2, turn))

                run(pe, NT, steps, 3)
                pe.wait_ge(e_w, NT)
                nc.tensor.matmul(bank[2][:, 0:ME], onesb[:], cum[:, NT % 2, :], start=True, stop=True)\
                    .then_inc(e_tot, 1)

            @block.scalar
            def _(act):
                def copy_logits(g, s, t):
                    act.wait_ge(e_lg, t + 1)
                    since(act, e_i8, t, 2)
                    act.activation(lg[:, s % 2, :], bank[1][:, 0:MH * ME], ACT.Copy).then_inc(e_lc, 1)

                def copy_n(g, s, t):
                    act.wait_ge(e_tr, t + 1)
                    since(act, e_lg, t, 2)
                    act.activation(n3T[:, s % 2, :, :].rearrange("p k n -> p (k n)"), bank[0], ACT.Copy)\
                        .then_inc(e_nT, 1)

                def relu(g, s, t):
                    act.wait_ge(e_y, t + 1)
                    since(act, e_x3, t, 2)
                    act.activation(er[:, s % 2, :], ea2[:, s, :], ACT.Relu, scale=dis[:, bass.ds(t, 1)])\
                        .then_inc(e_r, 1)

                steps = ((3, copy_logits), (2, copy_n), (0, relu))

                run(act, NT, steps, 3)
        end_phase(pe_)

        YL = nc.dram_tensor("slot_outputs", [LISTED * P, D], F32).ap()
        pt = ExitStack()
        lim = sb("lim", [P, SLOTS], F32, pt)
        cc = sb("cc", [P, ME], F32, pt)
        gt = sb("gt", [P, ME, SLOTS], F32, pt)
        ntl = sb("ntl", [P, ME], F32, pt)
        incl = sb("incl", [P, ME], F32, pt)
        le = sb("le", [P, 2, ME], F32, pt)
        lm = sb("lm", [P, 2, ME], F32, pt)
        tt = sb("tt", [P, 2, 3], F32, pt)
        tab = sb("tab", [P, 4], F32, pt)
        tid = sb("tid", [P, 2], I32, pt)
        trow = sb("trow", [1, 4 * P], I32, pt)
        idr = sb("idr", [P, 2, P], I32, pt)
        idf = sb("idf", [P, 2, P], F32, pt)
        ids = sb("ids", [P, 2 * P], I32, pt)
        g_c = sem("g_c")
        g_ld, g_t, g_tr, g_rw, g_rw2 = (sem(n) for n in ("g_ld", "g_t", "g_tr", "g_rw", "g_rw2"))

        with nc.Block() as block:
            @block.vector
            def _(dve):
                n = [0]

                def then(ins):
                    n[0] += 1
                    ins.then_inc(g_c, 1)
                    dve.wait_ge(g_c, n[0])

                then(nc.vector.tensor_scalar_mul(lim[:], iota[:, 0:SLOTS], float(P)))
                then(nc.vector.tensor_scalar_min(cc[:], cnt[:], float(CAP)))
                then(nc.vector.tensor_tensor(gt[:], cc[:].unsqueeze(2).to_broadcast([P, ME, SLOTS]),
                                             lim[:].unsqueeze(1).to_broadcast([P, ME, SLOTS]), ALU.is_gt))
                then(nc.vector.tensor_reduce(ntl[:], gt[:], AX.X, ALU.add))
                then(nc.vector.memset(cc[:], 1.0))
                then(nc.vector.tensor_tensor_scan(incl[:], cc[:], ntl[:], 0.0, ALU.mult, ALU.add))
                then(nc.vector.tensor_tensor(ntl[:], incl[:], ntl[:], ALU.subtract))
                then(nc.vector.tensor_scalar_mul(cbase[:], ntl[:], float(P)))
                for c in range(2):
                    then(nc.vector.tensor_scalar(ntl[:, c:c + 1], prow[:], float(c * P), None, ALU.add))
                    then(nc.vector.tensor_scalar(le[:, c, :], incl[:], ntl[:, c:c + 1], None, ALU.is_le))
                    then(nc.vector.tensor_tensor(lm[:, c, :], le[:, c, :], incl[:], ALU.mult))
                    then(nc.vector.tensor_reduce(tt[:, c, 0:1], le[:, c, :], AX.X, ALU.add))
                    then(nc.vector.tensor_reduce(tt[:, c, 1:2], lm[:, c, :], AX.X, ALU.max))
                    then(nc.vector.tensor_tensor(tt[:, c, 2:3], ntl[:, c:c + 1], tt[:, c, 1:2], ALU.subtract))
                    then(nc.vector.scalar_tensor_tensor(tab[:, c:c + 1], tt[:, c, 0:1], float(SLOTS), tt[:, c, 2:3],
                                                        ALU.mult, ALU.add))
                    then(nc.vector.tensor_scalar_min(tab[:, 2 + c:3 + c], tt[:, c, 0:1], float(ME - 1)))
                nc.vector.tensor_copy(tid[:], tab[:, 0:2]).then_inc(g_t, 1)
                dve.wait_ge(g_tr, 1)
                nc.vector.tensor_copy(trow[:], bank[0][0:1, 0:4 * P]).then_inc(g_rw, 1)
                dve.wait_ge(g_ld, 32)
                nc.vector.tensor_copy(idf[:], idr[:]).then_inc(g_t, 1)
                dve.wait_ge(g_tr, 2)
                nc.vector.tensor_copy(ids[:], bank[1][:, 0:2 * P]).then_inc(g_rw, 1)
                dve.wait_ge(g_rw, 2)

            @block.gpsimd
            def _(pool):
                pool.memset(idr[:], 0).then_inc(g_rw2, 1)
                pool.wait_ge(g_rw2, 1)
                pool.wait_ge(g_t, 1)
                for c in range(2):
                    pool.indirect_dma_start(idr[:, c, :], None, IDX, bass.IndirectOffsetOnAxis(tid[:, c:c + 1], 0),
                                            bounds_check=ME * SLOTS + LISTED - 1, oob_is_err=False)\
                        .then_inc(g_ld, 16)

            @block.tensor
            def _(pe):
                pe.wait_ge(g_t, 1)
                for k in range(4):
                    last = nc.tensor.matmul(bank[0][0:1, k * P:(k + 1) * P], tab[:, k:k + 1], ident[:],
                                            start=True, stop=True)
                last.then_inc(g_tr, 1)
                pe.wait_ge(g_t, 2)
                for c in range(2):
                    last = nc.tensor.transpose(bank[1][:, c * P:(c + 1) * P], idf[:, c, :], ident[:])
                last.then_inc(g_tr, 1)

        xg = sb("xg", [P, 4, D], F32, pt)
        gT = sb("gT", [P, 2, DK, P], F32, pt)
        we1 = sb("we1", [P, 4, DK * MF], F32, pt)
        we2 = sb("we2", [MF, 4, D], F32, pt)
        hg = sb("hg", [MF, 2, P], F32, pt)
        yo = sb("yo", [P, 4, D], F32, pt)
        sg = sb("sg", [P, 4, 1], I32, pt)
        p_ld, p_w, p_st = sems("p_ld", 4), sems("p_w", 4), sems("p_st", 4)
        p_0, p_ix, p_hd, p_tr, p_T, p_up, p_h, p_dn, p_y = (
            sem("p_" + n) for n in "0 ix hd tr T up h dn y".split())

        with nc.Block() as block:
            @block.sync
            def _(sp):
                def body(g, s):
                    t = g * 4 + s
                    e = sp.value_load(trow[0:1, bass.ds(t + 2 * P, 1)], min_val=0, max_val=ME - 1)
                    since(sp, p_dn, t, 4)
                    sp.dma_start(we1[:, s, :], M1[bass.ds(e * P, P), :]).then_inc(p_w[s], 16)
                    sp.dma_start(we2[:, s, :], M2[bass.ds(e * MF, MF), :]).then_inc(p_w[s], 16)

                stream(sp, LISTED, 4, body)
                for s in range(4):
                    sp.wait_ge(p_st[s], 16 * ((LISTED + 3 - s) // 4))

            @block.gpsimd
            def _(pool):
                pool.memset(xg[:], 0.0).then_inc(p_0, 1)

                def body(g, s):
                    t = g * 4 + s
                    since(pool, p_tr, t, 4)
                    pool.tensor_copy(sg[:, s, :], ids[:, bass.ds(t, 1)]).then_inc(p_ix, 1)
                    pool.wait_ge(p_ix, t + 1)
                    pool.wait_ge(p_0, 1)
                    hold(pool, 0, s, p_hd, t)
                    pool.indirect_dma_start(xg[:, s, :], None, XN3, bass.IndirectOffsetOnAxis(sg[:, s, 0:1], 0),
                                            bounds_check=NP - 1, oob_is_err=False).then_inc(p_ld[s], 16)

                stream(pool, LISTED, 4, body)

            @block.tensor
            def _(pe):
                def turn(g, s, t):
                    pe.wait_ge(p_ld[s], 16 * (g + 1))
                    tr4(bank[s % 2], xg[:, s, :]).then_inc(p_tr, 1)

                def up(g, s, t):
                    h = s % 2
                    pe.wait_ge(p_T, t + 1)
                    pe.wait_ge(p_w[s], 32 * (g + 1))
                    for k in range(DK):
                        last = nc.tensor.matmul(bank[2 + h][0:MF, 0:P], we1[:, s, k * MF:(k + 1) * MF],
                                                gT[:, h, k, :], start=(k == 0), stop=(k == DK - 1))
                    last.then_inc(p_up, 1)

                def down(g, s, t):
                    h = s % 2
                    pe.wait_ge(p_h, t + 1)
                    since(pe, p_y, t, 2)
                    nc.tensor.matmul(bank[4 + h], hg[:, h, :], we2[:, s, :], start=True, stop=True).then_inc(p_dn, 1)

                steps = ((0, turn), (1, up), (2, down))

                def body(g, s):
                    for lag, step in steps:
                        if warm(g, s, lag, 4):
                            step(*ago(g, s, lag))

                stream(pe, LISTED, 4, body)
                for t in range(LISTED, LISTED + 2):
                    for lag, step in steps:
                        if t - lag < LISTED:
                            step(*ago(0, t, lag))

            @block.scalar
            def _(act):
                def gelu(g, s, t):
                    h = s % 2
                    act.wait_ge(p_up, t + 1)
                    since(act, p_dn, t, 2)
                    act.activation(hg[:, h, :], bank[2 + h][0:MF, 0:P], ACT.Gelu).then_inc(p_h, 1)

                def copy(g, s, t):
                    act.wait_ge(p_tr, t + 1)
                    since(act, p_up, t, 2)
                    act.activation(gT[:, s % 2, :, :].rearrange("p k n -> p (k n)"), bank[s % 2], ACT.Copy)\
                        .then_inc(p_T, 1)

                def store(g, s, t):
                    act.wait_ge(p_y, t + 1)
                    act.dma_start(row(YL, t), yo[:, s, :]).then_inc(p_st[s], 16)

                steps = ((0, copy), (3, store), (1, gelu))

                run(act, LISTED, steps)

            @block.vector
            def _(dve):
                def body(g, s):
                    t = g * 4 + s
                    if warm(g, s, 4, 4):
                        dve.wait_ge(p_st[s], 16 * g)
                    dve.wait_ge(p_dn, t + 1)
                    nc.vector.tensor_copy(yo[:, s, :], bank[4 + s % 2]).then_inc(p_y, 1)

                stream(dve, LISTED, 4, body)
        end_phase(pt)

        pq = ExitStack()
        qx = sb("qx", [P, 4, D], F32, pq)
        q0 = sb("q0", [P, 4, 2, D], F32, pq)
        qs = sb("qs", [P, 4, 2], I32, pq)
        qj = sb("qj", [P, 4, 2, ME], F32, pq)
        qf = sb("qf", [P, 4, 2], F32, pq)
        q_ld, q_x, q_st = sems("q_ld", 4), sems("q_x", 4), sems("q_st", 4)
        q_0, q_ix, q_hd, q_a, q_b, q_f = (sem("q_" + n) for n in "0 ix hd a b f".split())

        with nc.Block() as block:
            @block.sync
            def _(sp):
                def store(g, s, t):
                    sp.wait_ge(q_b, t + 1)
                    n = TAIL if isinstance(t, int) and t == NT - 1 else P
                    sp.dma_start(row(out, t, n), qx[0:n, s, :]).then_inc(q_st[s], 16)

                def body(g, s):
                    t = g * 4 + s
                    if warm(g, s, 4, 4):
                        sp.wait_ge(q_st[s], 16 * g)
                    sp.dma_start(qx[:, s, :], row(X3, t)).then_inc(q_x[s], 16)
                    if warm(g, s, 2, 4):
                        store(*ago(g, s, 2))

                stream(sp, NT, 4, body)
                for t in range(NT - 2, NT):
                    store(*ago(0, t, 0))
                for s in range(4):
                    sp.wait_ge(q_st[s], 16 * ((NT + 3 - s) // 4))

            @block.gpsimd
            def _(pool):
                def body(g, s):
                    t = g * 4 + s
                    since(pool, q_b, t, 4)
                    pool.wait_ge(q_ix, t + 1)
                    pool.wait_ge(q_0, 1)
                    hold(pool, 0, s, q_hd, t)
                    for k in range(2):
                        pool.indirect_dma_start(q0[:, s, k, :], None, YL,
                                                bass.IndirectOffsetOnAxis(qs[:, s, k:k + 1], 0),
                                                bounds_check=LISTED * P - 1, oob_is_err=False)\
                            .then_inc(q_ld[s], 16)

                stream(pool, NT, 4, body)

            @block.vector
            def _(dve):
                nc.vector.memset(q0[:], 0.0).then_inc(q_0, 1)

                def find(g, s, t):
                    if not isinstance(t, int) or t >= 4:
                        dve.wait_ge(q_ld[s], 32 * g)
                    for k in range(2):
                        last = nc.vector.scalar_tensor_tensor(
                            qj[:, s, k, :], iota[:, 0:ME], selk[:, bass.ds(t, 1), k], cbase[:], ALU.is_equal,
                            ALU.mult, accum_out=qf[:, s, k:k + 1])
                    last.then_inc(q_f, 1)
                    dve.wait_ge(q_f, t + 1)
                    nc.vector.tensor_tensor(qs[:, s, :], qf[:, s, :],
                                            plk[:, bass.ds(t, 1), :].rearrange("p t a -> p (t a)"), ALU.add)\
                        .then_inc(q_ix, 1)

                def combine(g, s, t):
                    dve.wait_ge(q_x[s], 16 * (g + 1))
                    dve.wait_ge(q_ld[s], 32 * (g + 1))
                    w = w12[:, bass.ds(t, 1), :].rearrange("p t a -> p (t a)")
                    nc.vector.scalar_tensor_tensor(q0[:, s, 0, :], q0[:, s, 0, :], w[:, 0:1], qx[:, s, :],
                                                   ALU.mult, ALU.add).then_inc(q_a, 1)
                    dve.wait_ge(q_a, t + 1)
                    nc.vector.scalar_tensor_tensor(qx[:, s, :], q0[:, s, 1, :], w[:, 1:2], q0[:, s, 0, :],
                                                   ALU.mult, ALU.add).then_inc(q_b, 1)

                def body(g, s):
                    find(*ago(g, s, 0))
                    if warm(g, s, 3, 4):
                        combine(*ago(g, s, 3))

                stream(dve, NT, 4, body, 2)
                for t in range(NT - 3, NT):
                    combine(*ago(0, t, 0))
        end_phase(pq)


_INS = ["x", "src", "dst", "Wl", "Wr", "att", "gbias", "Wc0", "b1c", "W2e", "b2e", "WT", "bG", "hashp", "M1", "M2"]


def kernel(x, src, dst, L0_gnn_W_l, L0_gnn_W_r, L0_gnn_att, L0_gnn_bias, L0_ffn_Wr, L0_ffn_br, L0_ffn_W1, L0_ffn_b1,
           L0_ffn_W2, L0_ffn_b2, L1_gnn_W, L1_gnn_b, L1_ffn_hash_proj, L1_ffn_W1, L1_ffn_W2):
    import concourse.bacc as _bacc
    from concourse.bass_utils import run_bass_kernel_spmd as _run

    a = {k: np.asarray(v) for k, v in locals().items() if not k.startswith("_")}
    flat = {
        "x": a["x"], "src": a["src"], "dst": a["dst"], "Wl": a["L0_gnn_W_l"], "Wr": a["L0_gnn_W_r"],
        "att": a["L0_gnn_att"].reshape(D), "gbias": a["L0_gnn_bias"],
        "Wc0": np.concatenate([a["L0_ffn_W1"].transpose(1, 0, 2).reshape(D, FC), a["L0_ffn_Wr"]], axis=1),
        "b1c": np.concatenate([a["L0_ffn_b1"].reshape(FC), a["L0_ffn_br"]]),
        "W2e": a["L0_ffn_W2"].reshape(FC, D), "b2e": a["L0_ffn_b2"],
        "WT": a["L1_gnn_W"].T, "bG": a["L1_gnn_b"],
        "hashp": a["L1_ffn_hash_proj"].transpose(1, 0, 2).reshape(D, MH * ME),
        "M1": a["L1_ffn_W1"].reshape(ME, DK, P, MF).transpose(0, 2, 1, 3).reshape(ME * P, DK * MF),
        "M2": a["L1_ffn_W2"].reshape(MC, D),
    }
    nc = _bacc.Bacc("TRN2", target_bir_lowering=False, num_devices=1)
    arrays, aps = {}, []
    for name in _INS:
        v = np.ascontiguousarray(flat[name])
        arrays["in_" + name] = v
        aps.append(nc.dram_tensor("in_" + name, v.shape, mybir.dt.from_np(v.dtype), kind="ExternalInput").ap())
    out = nc.dram_tensor("out_0", (N, D), F32, kind="ExternalOutput").ap()
    gnn_ffn(nc, *aps, out)
    r = _run(nc, [arrays], core_ids=[0])
    return r.results[0]["out_0"]
```
